# Optimizing a Trainium2 kernel written in Bass

```python
import numpy as np
import jax
import jax.numpy as jnp

def _softmax(x, axis=-1):
    return jax.nn.softmax(x, axis=axis)

def _gelu(x):
    return jax.nn.gelu(x, approximate=True)

def _silu(x):
    return jax.nn.silu(x)

def _sigmoid(x):
    return jax.nn.sigmoid(x)

def _layernorm(x, axis=-1, eps=1e-05):
    m = jnp.mean(x, axis=axis, keepdims=True)
    v = jnp.var(x, axis=axis, keepdims=True)
    return (x - m) / jnp.sqrt(v + eps)

def _scatter_add(tgt, idx, src, axis=0):
    return tgt.at[idx].add(src)

def _segment_sum(src, seg, n):
    return jax.ops.segment_sum(src, seg, n)
kernel_name = 'mk_flamingo_gated_d2_seqx_r4_fbbb59'

def setup_inputs(seed: int=0):
    np.random.seed(seed)
    _w = jnp.asarray

    def _rec_inputs():
        import jax
        import jax.numpy as jnp
        _rk = jax.random.key(seed)
        x = 7.22e-05 + 1 * jax.random.normal(jax.random.fold_in(_rk, 1), (16, 100, 256), jnp.float32)
        _lenS = 100 - jax.random.randint(jax.random.fold_in(_rk, 7), (16,), 0, max(1, 100 // 4) + 1, jnp.int32)
        _lenS2 = 361 - jax.random.randint(jax.random.fold_in(_rk, 8), (16,), 0, max(1, 361 // 4) + 1, jnp.int32)
        _ctx_768P = jax.random.normal(jax.random.fold_in(_rk, 11), (16, 16, 192), jnp.float32)
        _ctx_768c = jax.random.dirichlet(jax.random.fold_in(_rk, 511), 0.3 * jnp.ones((16,), jnp.float32), (16, 361))
        _ctx_768t = jnp.einsum('bsk,bkd->bsd', _ctx_768c, _ctx_768P)
        _ctx_768t = _ctx_768t * jax.lax.rsqrt(jnp.mean(jnp.square(_ctx_768t)) + 1e-12) * 0.953939
        ctx_768 = 2.09791e-05 + 1.00001 * (_ctx_768t + 0.3 * jax.random.normal(jax.random.fold_in(_rk, 611), (16, 361, 192), jnp.float32))
        _validS = jnp.arange(100)[None, :] < _lenS[:, None]
        _validS2 = jnp.arange(361)[None, :] < _lenS2[:, None]
        _causal = jnp.tril(jnp.ones((100, 100), dtype=bool))
        mask_BxS_bk0 = jnp.logical_not(jnp.broadcast_to(_validS[:, :], (16, 100)))
        _g = jax.random.normal(jax.random.fold_in(_rk, 9001), (2, 2), jnp.float32)
        _g = jnp.sign(_g) * jnp.maximum(jnp.abs(_g), 1.0) + (_g == 0) * 1.0
        g_xattn = _g[0]
        g_ffn = _g[1]
        return (x, ctx_768, mask_BxS_bk0, g_xattn, g_ffn)
    x, ctx_768, mask_BxS_bk0, g_xattn, g_ffn = _rec_inputs()

    def _L0_xattn_setup():
        import jax, jax.numpy as jnp
        import numpy as np
        NUM_HEADS = 16
        key = jax.random.key(seed)
        k1, k2, k3, k4, k5 = jax.random.split(key, 5)
        B, N, C = (4, 512, 256)
        N2, Cy = (256, 192)
        x = jax.random.normal(k1, (B, N, C), dtype=jnp.float32)
        y = jax.random.normal(k2, (B, N2, Cy), dtype=jnp.float32)
        pad_mask = jax.random.randint(k3, (B, N), 0, 2).astype(jnp.bool_)
        Wq = jax.random.normal(k4, (C, C), dtype=jnp.float32) * C ** (-0.5)
        Wkv = jax.random.normal(k5, (2 * C, Cy), dtype=jnp.float32) * Cy ** (-0.5)
        return {'x': x, 'y': y, 'pad_mask': pad_mask, 'Wq': Wq, 'Wkv': Wkv}
    _L0_xattn_all = _L0_xattn_setup()
    _L0_xattn_in = {k: v for k, v in _L0_xattn_all.items() if k in ('Wq', 'Wkv')}
    del _L0_xattn_all

    def _L0_ffn_setup():
        import jax, jax.numpy as jnp
        import numpy as np
        B, T, H = (8, 512, 256)
        F = 1024
        E = 8
        TOP_K = 2
        key = jax.random.key(seed)
        ks = jax.random.split(key, 6)
        s_h = 1.0 / np.sqrt(H)
        s_f = 1.0 / np.sqrt(F)
        return {'hidden_states': jax.random.normal(ks[0], (B, T, H), dtype=jnp.float32), 'gate_w': jax.random.uniform(ks[1], (H, E), minval=-s_h, maxval=s_h, dtype=jnp.float32), 'w1': jax.random.uniform(ks[2], (E, H, F), minval=-s_h, maxval=s_h, dtype=jnp.float32), 'b1': jax.random.uniform(ks[3], (E, F), minval=-s_h, maxval=s_h, dtype=jnp.float32), 'w2': jax.random.uniform(ks[4], (E, F, H), minval=-s_f, maxval=s_f, dtype=jnp.float32), 'b2': jax.random.uniform(ks[5], (E, H), minval=-s_f, maxval=s_f, dtype=jnp.float32)}
    _L0_ffn_all = _L0_ffn_setup()
    _L0_ffn_in = {k: v for k, v in _L0_ffn_all.items() if k in ('gate_w', 'w1', 'b1', 'w2', 'b2')}
    del _L0_ffn_all

    def _L1_xattn_setup():
        import jax, jax.numpy as jnp
        import numpy as np
        N_HEADS = 16
        DIMS = 256
        D_CTX = 192
        HEAD = DIMS // N_HEADS
        key = jax.random.key(seed)
        ks = jax.random.split(key, 10)
        s_q = 1.0 / np.sqrt(DIMS)
        s_c = 1.0 / np.sqrt(D_CTX)
        return {'x': jax.random.normal(ks[0], (2, 512, DIMS), jnp.float32), 'context': jax.random.normal(ks[1], (2, 512, D_CTX), jnp.float32), 'w_q': jax.random.normal(ks[2], (DIMS, DIMS), jnp.float32) * s_q, 'b_q': jax.random.normal(ks[3], (DIMS,), jnp.float32) * 0.01, 'w_k': jax.random.normal(ks[4], (D_CTX, DIMS), jnp.float32) * s_c, 'b_k': jax.random.normal(ks[5], (DIMS,), jnp.float32) * 0.01, 'w_v': jax.random.normal(ks[6], (D_CTX, DIMS), jnp.float32) * s_c, 'b_v': jax.random.normal(ks[7], (DIMS,), jnp.float32) * 0.01, 'w_o': jax.random.normal(ks[8], (DIMS, DIMS), jnp.float32) * s_q, 'b_o': jax.random.normal(ks[9], (DIMS,), jnp.float32) * 0.01}
    _L1_xattn_all = _L1_xattn_setup()
    _L1_xattn_in = {k: v for k, v in _L1_xattn_all.items() if k in ('w_q', 'b_q', 'w_k', 'b_k', 'w_v', 'b_v', 'w_o', 'b_o')}
    del _L1_xattn_all

    def _L1_ffn_setup():
        import jax, jax.numpy as jnp
        import numpy as np
        MANT_BITS = 8
        _PWL_X = jnp.linspace(-4.0, 4.0, 33, dtype=jnp.float32)
        _PWL_Y = 0.5 * _PWL_X * (1.0 + jax.lax.erf(_PWL_X / jnp.sqrt(jnp.float32(2.0))))

        def float2fix(x, mantissa_bits):
            s = jnp.float32(2.0 ** mantissa_bits)
            q = jnp.round(x * s) / s
            return x + jax.lax.stop_gradient(q - x)

        def pwlin_gelu_basic(x, mantissa_bits_in, mantissa_bits_out):
            xq = float2fix(x, mantissa_bits_in)
            y = jnp.interp(xq, _PWL_X, _PWL_Y)
            y = jnp.where(xq > 4.0, xq, jnp.where(xq < -4.0, jnp.float32(0.0), y))
            return float2fix(y, mantissa_bits_out)
        key = jax.random.key(seed)
        k_x, k_w1, k_b1, k_w2, k_b2 = jax.random.split(key, 5)
        dim, ff_dim = (256, 1024)
        B, S = (32, 128)
        sc1 = 1.0 / np.sqrt(dim)
        sc2 = 1.0 / np.sqrt(ff_dim)
        return {'x': jax.random.normal(k_x, (B, S, dim), dtype=jnp.float32), 'w1': jax.random.uniform(k_w1, (dim, ff_dim), jnp.float32, -sc1, sc1), 'b1': jax.random.uniform(k_b1, (ff_dim,), jnp.float32, -sc1, sc1), 'w2': jax.random.uniform(k_w2, (ff_dim, dim), jnp.float32, -sc2, sc2), 'b2': jax.random.uniform(k_b2, (dim,), jnp.float32, -sc2, sc2)}
    _L1_ffn_all = _L1_ffn_setup()
    _L1_ffn_in = {k: v for k, v in _L1_ffn_all.items() if k in ('w1', 'b1', 'w2', 'b2')}
    del _L1_ffn_all
    return {'x': x, 'ctx_768': ctx_768, 'mask_BxS_bk0': mask_BxS_bk0, 'g_xattn': g_xattn, 'g_ffn': g_ffn, 'L0_xattn_Wq': _L0_xattn_in['Wq'], 'L0_xattn_Wkv': _L0_xattn_in['Wkv'], 'L0_ffn_gate_w': _L0_ffn_in['gate_w'], 'L0_ffn_w1': _L0_ffn_in['w1'], 'L0_ffn_b1': _L0_ffn_in['b1'], 'L0_ffn_w2': _L0_ffn_in['w2'], 'L0_ffn_b2': _L0_ffn_in['b2'], 'L1_xattn_w_q': _L1_xattn_in['w_q'], 'L1_xattn_b_q': _L1_xattn_in['b_q'], 'L1_xattn_w_k': _L1_xattn_in['w_k'], 'L1_xattn_b_k': _L1_xattn_in['b_k'], 'L1_xattn_w_v': _L1_xattn_in['w_v'], 'L1_xattn_b_v': _L1_xattn_in['b_v'], 'L1_xattn_w_o': _L1_xattn_in['w_o'], 'L1_xattn_b_o': _L1_xattn_in['b_o'], 'L1_ffn_w1': _L1_ffn_in['w1'], 'L1_ffn_b1': _L1_ffn_in['b1'], 'L1_ffn_w2': _L1_ffn_in['w2'], 'L1_ffn_b2': _L1_ffn_in['b2']}

def reference(x, ctx_768, mask_BxS_bk0, g_xattn, g_ffn, L0_xattn_Wq, L0_xattn_Wkv, L0_ffn_gate_w, L0_ffn_w1, L0_ffn_b1, L0_ffn_w2, L0_ffn_b2, L1_xattn_w_q, L1_xattn_b_q, L1_xattn_w_k, L1_xattn_b_k, L1_xattn_w_v, L1_xattn_b_v, L1_xattn_w_o, L1_xattn_b_o, L1_ffn_w1, L1_ffn_b1, L1_ffn_w2, L1_ffn_b2):
    import jax
    import jax.numpy as jnp

    def _L0_xattn_ref(x, y, pad_mask, Wq, Wkv):
        import jax, jax.numpy as jnp
        import numpy as np
        NUM_HEADS = 16
        B, N, C = x.shape
        N2 = y.shape[1]
        H = NUM_HEADS
        d = C // H
        scale = d ** (-0.5)
        q = (x @ Wq.T).reshape(B, N, H, d).transpose(0, 2, 1, 3)
        kv = (y @ Wkv.T).reshape(B, N2, 2, H, d).transpose(2, 0, 3, 1, 4)
        k, v = (kv[0], kv[1])
        attn = jnp.einsum('bhnd,bhmd->bhnm', q * scale, k)
        attn = jnp.where(pad_mask[:, None, :, None], attn, jnp.float32(-1000000000.0))
        attn = jax.nn.softmax(attn, axis=-1)
        out = jnp.einsum('bhnm,bhmd->bhnd', attn, v)
        return out.transpose(0, 2, 1, 3).reshape(B, N, C)

    def _L0_ffn_ref(hidden_states, gate_w, w1, b1, w2, b2):
        import jax, jax.numpy as jnp
        import numpy as np
        B, T, H = (8, 512, 256)
        F = 1024
        E = 8
        TOP_K = 2
        b, t, h = hidden_states.shape
        seq_rep = hidden_states.mean(axis=1)
        router_logits = seq_rep @ gate_w
        probs = jax.nn.softmax(router_logits.astype(jnp.float32), axis=-1)
        top_w, top_i = jax.lax.top_k(probs, TOP_K)
        top_w = top_w / top_w.sum(axis=-1, keepdims=True)
        top_w = top_w.astype(hidden_states.dtype)
        combine = jnp.zeros((b, E), dtype=hidden_states.dtype)
        combine = combine.at[jnp.arange(b)[:, None], top_i].set(top_w)
        out = jnp.zeros_like(hidden_states)
        for e in range(E):
            hmid = jax.nn.gelu(jnp.einsum('bth,hf->btf', hidden_states, w1[e]) + b1[e], approximate=False)
            y = jnp.einsum('btf,fh->bth', hmid, w2[e]) + b2[e]
            out = out + combine[:, e][:, None, None] * y
        return out

    def _L1_xattn_ref(x, context, w_q, b_q, w_k, b_k, w_v, b_v, w_o, b_o):
        import jax, jax.numpy as jnp
        import numpy as np
        N_HEADS = 16
        DIMS = 256
        D_CTX = 192
        HEAD = DIMS // N_HEADS
        B, Lq, D = x.shape
        q = x @ w_q + b_q
        k = context @ w_k + b_k
        v = context @ w_v + b_v
        q = q.reshape(B, Lq, N_HEADS, HEAD)
        k = k.reshape(B, -1, N_HEADS, HEAD)
        v = v.reshape(B, -1, N_HEADS, HEAD)
        scale = 1.0 / np.sqrt(HEAD).astype(np.float32)
        scores = jnp.einsum('bqhd,bkhd->bhqk', q, k) * scale
        weights = jax.nn.softmax(scores, axis=-1)
        out = jnp.einsum('bhqk,bkhd->bqhd', weights, v).reshape(B, Lq, D)
        return out @ w_o + b_o

    def _L1_ffn_ref(x, w1, b1, w2, b2):
        import jax, jax.numpy as jnp
        import numpy as np
        MANT_BITS = 8
        _PWL_X = jnp.linspace(-4.0, 4.0, 33, dtype=jnp.float32)
        _PWL_Y = 0.5 * _PWL_X * (1.0 + jax.lax.erf(_PWL_X / jnp.sqrt(jnp.float32(2.0))))

        def float2fix(x, mantissa_bits):
            s = jnp.float32(2.0 ** mantissa_bits)
            q = jnp.round(x * s) / s
            return x + jax.lax.stop_gradient(q - x)

        def pwlin_gelu_basic(x, mantissa_bits_in, mantissa_bits_out):
            xq = float2fix(x, mantissa_bits_in)
            y = jnp.interp(xq, _PWL_X, _PWL_Y)
            y = jnp.where(xq > 4.0, xq, jnp.where(xq < -4.0, jnp.float32(0.0), y))
            return float2fix(y, mantissa_bits_out)
        h = jnp.einsum('bsd,df->bsf', x, w1) + b1
        h = float2fix(h, MANT_BITS)
        h = pwlin_gelu_basic(h, MANT_BITS, MANT_BITS)
        h = float2fix(h, MANT_BITS)
        out = jnp.einsum('bsf,fd->bsd', h, w2) + b2
        return float2fix(out, MANT_BITS)
    x = x + jnp.tanh(g_xattn[0]) * _L0_xattn_ref(_layernorm(x, axis=-1), ctx_768, mask_BxS_bk0, L0_xattn_Wq, L0_xattn_Wkv)
    x = x + jnp.tanh(g_ffn[0]) * _L0_ffn_ref(_layernorm(x, axis=-1), L0_ffn_gate_w, L0_ffn_w1, L0_ffn_b1, L0_ffn_w2, L0_ffn_b2)
    x = x + jnp.tanh(g_xattn[1]) * _L1_xattn_ref(_layernorm(x, axis=-1), ctx_768, L1_xattn_w_q, L1_xattn_b_q, L1_xattn_w_k, L1_xattn_b_k, L1_xattn_w_v, L1_xattn_b_v, L1_xattn_w_o, L1_xattn_b_o)
    x = x + jnp.tanh(g_ffn[1]) * _L1_ffn_ref(_layernorm(x, axis=-1), L1_ffn_w1, L1_ffn_b1, L1_ffn_w2, L1_ffn_b2)
    return x

_drawn_inputs = setup_inputs


def setup_inputs(seed=0):
    import zlib

    import numpy as np

    out = dict(_drawn_inputs(seed))
    spreads = {'g_ffn': (-1.0, 0.6)}
    factors = {'L0_ffn_b1': 8.0,
     'L0_ffn_b2': 6.436,
     'L1_xattn_b_q': 35.478,
     'L1_xattn_b_k': 64.0,
     'L1_xattn_b_v': 7.325,
     'L1_xattn_b_o': 6.873,
     'L1_ffn_b1': 6.529,
     'L1_ffn_b2': 4.609}
    for name, (base, spread) in spreads.items():
        noise = np.random.default_rng([zlib.crc32(name.encode()), seed]).standard_normal(out[name].shape)
        drawn = base * np.exp(spread * noise) if base else spread * noise
        out[name] = jnp.asarray(drawn.astype(out[name].dtype))
    for name, factor in factors.items():
        out[name] = (out[name] * factor).astype(out[name].dtype)
    return out
```

```python
from contextlib import ExitStack

import concourse.bass as bass
from concourse import mybir

F32 = mybir.dt.float32
BF16 = mybir.dt.bfloat16
U8 = mybir.dt.uint8
U32 = mybir.dt.uint32
ALU = mybir.AluOpType
ACT = mybir.ActivationFunctionType
AX = mybir.AxisListType

B, S, C = 16, 100, 256
SC, CC = 361, 192
NH, D = 16, 16
G = C // 128
HG = NH // G
SCALE = D ** -0.5
EPS = 1e-5
KEYS = (120, 120, 121)
KSTEP = 120
HI, LO = 128, CC - 128
Q_PART = (1, 1, 2, 1, 2, 3)
K_PART = (1, 2, 1, 3, 2, 1)
SLOTS = len(Q_PART)
SROWS = SLOTS * D
MROWS = SROWS + 3
SW = S + SC
ROW_BANKS, ST_BANKS, P_BUFS = 2, 3, 2
CHUNK = 4
CHUNKS = NH // CHUNK
VW = 32
E, F, TOP = 8, 1024, 2
FT = F // 128
W2A = 4
FIX = 256.0
ROUND = 1.5 * 2.0 ** 23
SEG = 64.0
LIM = 4.0 * FIX
QUAD = 4


class Shared:
    pass


def setup_phase(nc, t, sh):
    with ExitStack() as ctx:
        def sb(name, shape, dt=F32):
            return ctx.enter_context(nc.sbuf_tensor(name, shape, dt))

        def sem(name):
            return ctx.enter_context(nc.semaphore(name))

        wq_rows = sb("wq_rows", [128, G, C])
        wkv_rows = sb("wkv_rows", [128, 2 * G, CC])
        mask_u8 = sb("mask_u8", [B, S], U8)
        mask_f = sb("mask_f", [B, S])
        gates = sb("gates", [128, 4])
        eb1_rows = sb("eb1_rows", [E * FT, 128])
        fb1_rows = sb("fb1_rows", [FT, 128])
        stats = sb("stats0", [S, B, 6])
        ps = ctx.enter_context(nc.psum_tensor("ps_setup", [128, 4, 512], F32))

        loaded = sem("small_loaded")
        x_loaded = sem("x_loaded")
        ident_made = sem("ident_made")
        mask_cast = sem("mask_cast")
        turned = sem("turned")
        stats_done = sem("stats_done")
        evacuated = sem("setup_evacuated")
        gates_done = sem("gates_done")

        with nc.Block() as block:
            @block.sync
            def _(sp):
                sp.dma_start(wq_rows[:], t["Wq"].rearrange("(g p) c -> p g c", p=128)).then_inc(loaded, 16)
                sp.dma_start(wkv_rows[:], t["Wkv"].rearrange("(g p) c -> p g c", p=128)).then_inc(loaded, 16)
                sp.dma_start(mask_u8[:], t["mask"]).then_inc(loaded, 16)
                sp.dma_start(gates[:, 0:2], t["g_xattn"].partition_broadcast(128)).then_inc(loaded, 16)
                sp.dma_start(gates[:, 2:4], t["g_ffn"].partition_broadcast(128)).then_inc(loaded, 16)
                sp.dma_start(eb1_rows[:], t["e_b1"].rearrange("e (f p) -> (e f) p", p=128)).then_inc(loaded, 16)
                sp.dma_start(fb1_rows[:], t["f_b1"].rearrange("(f p) -> f p", p=128)).then_inc(loaded, 16)
                for tile, w in ((sh.wk1, t["w_k"]), (sh.wv1, t["w_v"])):
                    sp.dma_start(tile[0:HI, 0, :], w[0:HI, :]).then_inc(sh.later, 16)
                    sp.dma_start(tile[0:LO, 1, :], w[HI:CC, :]).then_inc(sh.later, 16)
                sp.dma_start(sh.wk1[LO:LO + 1, 1, :], t["b_k"].unsqueeze(0)).then_inc(sh.later, 16)
                sp.dma_start(sh.wv1[LO:LO + 1, 1, :], t["b_v"].unsqueeze(0)).then_inc(sh.later, 16)
                sp.dma_start(sh.wq1[:], t["w_q"].rearrange("(g p) c -> p g c", p=128)).then_inc(sh.later, 16)
                sp.dma_start(sh.wo1[:], t["w_o"].rearrange("(g p) c -> p g c", p=128)).then_inc(sh.later, 16)
                sp.dma_start(sh.bq1[:], t["b_q"].rearrange("(g p) -> p g", p=128),
                             allow_slow_non_contiguous=True).then_inc(sh.later, 16)
                sp.dma_start(sh.bo1[:], t["b_o"].partition_broadcast(S)).then_inc(sh.later, 16)
                sp.wait_ge(loaded, 7 * 16)
                sp.wait_ge(sh.later, 10 * 16)

            @block.gpsimd
            def _(pool):
                pool.memset(sh.ident[:], 0.0).then_inc(ident_made, 1)
                pool.memset(sh.identb[:], 0.0).then_inc(ident_made, 1)
                pool.wait_ge(ident_made, 2)
                for m in (sh.ident, sh.identb):
                    pool.affine_select(out=m[:], in_=m[:], compare_op=ALU.not_equal, fill=1.0, base=0,
                                       pattern=[[-1, 128]], channel_multiplier=1).then_inc(ident_made, 1)

            @block.scalar
            def _(act):
                act.dma_start(sh.x[:], t["x"].rearrange("b s c -> s b c")).then_inc(x_loaded, 16)
                act.wait_ge(loaded, 7 * 16)
                act.activation(sh.tg[:], gates[:], ACT.Tanh).then_inc(gates_done, 1)
                act.wait_ge(turned, 4)
                act.activation(sh.wq0[:].rearrange("p c (o n) -> p c o n", o=G),
                               ps[:, 0, :].rearrange("p (c o n) -> p c o n", c=G, o=G), ACT.Copy)\
                    .then_inc(evacuated, 1)
                act.wait_ge(turned, 4 + 8)
                for n, w in ((0, sh.wk0), (1, sh.wv0)):
                    act.activation(w[0:HI, 0, :], ps[0:HI, 1, n * C:(n + 1) * C], ACT.Copy).then_inc(evacuated, 1)
                    act.activation(w[0:LO, 1, :], ps[0:LO, 2, n * C:(n + 1) * C], ACT.Copy).then_inc(evacuated, 1)

            @block.tensor
            def _(pe):
                pe.wait_ge(loaded, 7 * 16)
                pe.wait_ge(ident_made, 4)
                for c in range(G):
                    for o in range(G):
                        pe.transpose(ps[:, 0, (c * G + o) * 128:(c * G + o + 1) * 128],
                                     wq_rows[:, o, c * 128:(c + 1) * 128], sh.ident[:]).then_inc(turned, 1)
                for n in range(2 * G):
                    pe.transpose(ps[0:HI, 1, n * 128:(n + 1) * 128], wkv_rows[:, n, 0:HI], sh.ident[:])\
                        .then_inc(turned, 1)
                    pe.transpose(ps[0:LO, 2, n * 128:(n + 1) * 128], wkv_rows[:, n, HI:CC], sh.ident[:])\
                        .then_inc(turned, 1)
                pe.wait_ge(mask_cast, 1)
                pe.transpose(ps[0:S, 3, 0:B], mask_f[:], sh.ident[0:B, 0:B]).then_inc(turned, 1)
                pe.transpose(ps[:, 3, 64:64 + E * FT], eb1_rows[:], sh.ident[0:E * FT, 0:E * FT]).then_inc(turned, 1)
                pe.transpose(ps[:, 3, 192:192 + FT], fb1_rows[:], sh.ident[0:FT, 0:FT]).then_inc(turned, 1)

            @block.vector
            def _(dve):
                dve.wait_ge(loaded, 7 * 16)
                dve.tensor_copy(mask_f[:], mask_u8[:]).then_inc(mask_cast, 1)
                dve.memset(sh.ones[:], 1.0)
                dve.memset(sh.wk0[LO:LO + 1, 1, :], 0.0)
                dve.memset(sh.wv0[LO:LO + 1, 1, :], 0.0)
                dve.memset(sh.gelu_bias[:, 0:1], -ROUND * SEG / FIX)
                dve.memset(sh.gelu_bias[:, 1:2], -ROUND * SEG / FIX + SEG / FIX)
                dve.wait_ge(x_loaded, 16)
                for b in range(B):
                    dve.bn_stats(stats[:, b, :], sh.x[:, b, :]).then_inc(stats_done, 1)
                for b in range(B):
                    dve.wait_ge(stats_done, b + 1)
                    dve.bn_aggr(sh.mv[:, b, :], stats[:, b, :])
                dve.wait_ge(turned, 4 + 8 + 3)
                dve.tensor_copy(sh.keep[:], ps[0:S, 3, 0:B])
                dve.tensor_copy(sh.eb1[:].rearrange("p e f -> p (e f)"), ps[:, 3, 64:64 + E * FT])
                dve.tensor_scalar(sh.fb1[:], ps[:, 3, 192:192 + FT], FIX, None, ALU.mult)


def rstd_steps(nc, sh, ctx, name):
    ready = ctx.enter_context(nc.semaphore(f"{name}_var_eps"))
    rooted = ctx.enter_context(nc.semaphore(f"{name}_rooted"))
    inverted = ctx.enter_context(nc.semaphore(f"{name}_rstd"))

    def on_vector(dve):
        dve.tensor_scalar(sh.rstd[:], sh.mv[:, :, 1], EPS, None, ALU.add).then_inc(ready, 1)
        dve.wait_ge(rooted, 1)
        dve.reciprocal(sh.rstd[:], sh.rstd[:]).then_inc(inverted, 1)
        dve.wait_ge(inverted, 1)

    def on_scalar(act):
        act.wait_ge(ready, 1)
        act.activation(sh.rstd[:], sh.rstd[:], ACT.Sqrt).then_inc(rooted, 1)

    return on_vector, on_scalar


def attention_phase(nc, sh, ctx_dram, layer, extra_loads, extra_start):
    first_layer = layer == 0
    wq, wk, wv = (sh.wq0, sh.wk0, sh.wv0) if first_layer else (sh.wq1, sh.wk1, sh.wv1)
    with ExitStack() as ctx:
        def sb(name, shape, dt=F32):
            return ctx.enter_context(nc.sbuf_tensor(f"{name}_{layer}", shape, dt))

        def psum(name, shape):
            return ctx.enter_context(nc.psum_tensor(f"{name}_{layer}", shape, F32))

        def sem(name):
            return ctx.enter_context(nc.semaphore(f"{name}_{layer}"))

        context = sb("context", [128, 2, 3, CC])
        ctxT = sb("ctxT", [128, 2, SC])
        xn = sb("xn", [S, C])
        xnT = sb("xnT", [128, G, S])
        qf = sb("qf", [128, G, S])
        qrest = sb("qrest", [128, G, S])
        krest = sb("krest", [128, G, SC])
        parts = sb("parts", [128, SLOTS, G, SW], BF16)
        stack = [sb(f"stack{p}", [MROWS, NH, SW], BF16) for p in range(2)]
        v = [sb(f"v{p}", [128, 3, NH, VW]) for p in range(2)]
        probs = [sb(f"probs{p}", [128, 3, CHUNK * S]) for p in range(P_BUFS)]
        rowmax = sb("rowmax", [S, NH])
        mrest = sb("mrest", [S, NH])
        mparts = sb("mparts", [S, 3, NH], BF16)
        mT = sb("mT", [3 * NH, S], BF16)
        oT4 = sb("oT4", [128, CHUNKS * S])
        rden = sb("rden", [S, NH])
        o = sb("o", [S, C])
        stats = sb("stats", [S, 6])
        mv_now = sb("mv_now", [S, 2])
        if not first_layer:
            oT = sb("oT", [128, G, S])
            biased = sb("biased", [S, C])
        scaled = sb("scaled", [S, B])

        rows_ps = psum("rows_ps", [128, ROW_BANKS, 512])
        a_ps = psum("a_ps", [128, 2, 512])
        st_ps = psum("st_ps", [128, ST_BANKS, 512])
        o_ps = psum("o_ps", [128, 512])

        ctx_in = [sem(f"context_loaded{p}") for p in range(2)]
        tick = sem("tick")
        stack_preset = sem("stack_preset")
        presets = sem("presets")
        v_cleared = sem("v_cleared")
        scaled_ready = sem("scaled_ready")
        xn_made = sem("xn_made")
        xnT_ps = sem("xnT_ps")
        xnT_made = sem("xnT_made")
        cT_ps = sem("cT_ps")
        cT_made = sem("cT_made")
        q_ps = sem("q_ps")
        qf_made = sem("qf_made")
        q_cut = sem("q_cut")
        k_ps = sem("k_ps")
        k1_made = sem("k1_made")
        krest_made = sem("krest_made")
        k_cut = sem("k_cut")
        k3_made = sem("k3_made")
        v_ps = sem("v_ps")
        v_made = sem("v_made")
        stacked = [sem(f"stacked{p}") for p in range(2)]
        m_in = [sem(f"max_rows_in{p}") for p in range(2)]
        rows_made = sem("rows_made")
        rows_free = sem("rows_free")
        m_steps = sem("m_steps")
        mT_ps = sem("mT_ps")
        mT_made = sem("mT_made")
        st_made = sem("st_made")
        exp_done = sem("exp_done")
        pv_done = sem("pv_done")
        oT4_made = sem("oT4_made")
        o_turned = sem("o_turned")
        rden_made = sem("rden_made")
        o_made = sem("o_made")
        x_steps = sem("x_steps")
        stats_made = sem("stats_made")
        oT_ps = sem("oT_ps")
        oT_made = sem("oT_made")
        out_ps = sem("out_ps")
        out_read = sem("out_read")

        rstd_vector, rstd_scalar = rstd_steps(nc, sh, ctx, f"att{layer}")
        EXP = 3 * CHUNKS

        def heads(ap):
            return ap.rearrange("p (h d) -> p h d", d=D)

        def run(step, eng):
            for par in range(2):
                step(par, par, 0, par == 0, False)
            with eng.Fori(1, B // 2 - 1) as pair:
                for par in range(2):
                    step(2 * pair + par, par, pair, False, False)
            for par in range(2):
                step(B - 2 + par, par, B // 2 - 1, False, par == 1)

        with nc.Block() as block:
            @block.sync
            def _(sp):
                def load_context(b, par):
                    sp.dma_start(context[0:KSTEP, par, :, :],
                                 ctx_dram[b, 0:3 * KSTEP, :].rearrange("(t p) c -> p t c", p=KSTEP))\
                        .then_inc(ctx_in[par], 16)
                    sp.dma_start(context[KSTEP:KSTEP + 1, par, 2, :], ctx_dram[b, 3 * KSTEP:SC, :])\
                        .then_inc(ctx_in[par], 16)

                def fill_stack(b, par):
                    sp.wait_ge(q_cut, 7 * (b + 1))
                    sp.sem_inc(tick, 1)
                    sp.wait_ge(k_cut, 4 * (b + 1))
                    sp.wait_ge(k3_made, b + 1)
                    for hh in range(HG):
                        sp.dma_start(
                            stack[par][0:SROWS, hh:NH:HG, :],
                            parts[hh * D:(hh + 1) * D, :, :, :]).then_inc(stacked[par], 16)

                load_context(0, 0)
                load_context(1, 1)
                extra_start(sp)
                fill_stack(0, 0)

                def step(b, par, pair, first, last):
                    if not last:
                        sp.wait_ge(exp_done, ST_BANKS + EXP * b)
                        sp.sem_inc(tick, 1)
                        fill_stack(b + 1, 1 - par)
                    if pair is not B // 2 - 1:
                        sp.wait_ge(cT_made, 2 * (b + 1))
                        sp.sem_inc(tick, 1)
                        load_context(b + 2, par)
                    extra_loads(sp, par, pair)

                run(step, sp)

            @block.gpsimd
            def _(pool):
                for p in range(2):
                    pool.memset(stack[p][SROWS:MROWS, :, S:SW], 1.0).then_inc(stack_preset, 1)
                pool.wait_ge(stack_preset, 2)

                def cut(b, par_before):
                    pool.wait_ge(qf_made, b + 1)
                    par_before(pool)
                    pool.sem_inc(tick, 1)
                    qs = [parts[:, s, :, 0:S] for s in range(SLOTS)]
                    ks = [parts[:, s, :, S:SW] for s in range(SLOTS)]
                    n = 7 * b
                    pool.tensor_copy(qs[0], qf[:]).then_inc(q_cut, 1)
                    pool.wait_ge(q_cut, n + 1)
                    pool.tensor_tensor(qrest[:], qf[:], qs[0], ALU.subtract).then_inc(q_cut, 1)
                    pool.wait_ge(q_cut, n + 2)
                    pool.sem_inc(tick, 1)
                    pool.tensor_copy(qs[2], qrest[:]).then_inc(q_cut, 1)
                    pool.wait_ge(q_cut, n + 3)
                    pool.tensor_tensor(qs[5], qrest[:], qs[2], ALU.subtract).then_inc(q_cut, 1)
                    pool.tensor_copy(qs[1], qs[0]).then_inc(q_cut, 1)
                    pool.tensor_copy(qs[3], qs[0]).then_inc(q_cut, 1)
                    pool.tensor_copy(qs[4], qs[2]).then_inc(q_cut, 1)
                    pool.wait_ge(k1_made, b + 1)
                    pool.sem_inc(tick, 1)
                    pool.tensor_copy(ks[2], ks[0]).then_inc(k_cut, 1)
                    pool.tensor_copy(ks[5], ks[0]).then_inc(k_cut, 1)
                    pool.wait_ge(krest_made, b + 1)
                    pool.sem_inc(tick, 1)
                    pool.tensor_copy(ks[1], krest[:]).then_inc(k_cut, 1)
                    pool.wait_ge(k_cut, 4 * b + 3)
                    pool.sem_inc(tick, 1)
                    pool.tensor_copy(ks[4], ks[1]).then_inc(k_cut, 1)

                cut(0, lambda eng: None)

                def step(b, par, pair, first, last):
                    if not last:
                        cut(b + 1, lambda eng: eng.wait_ge(stacked[par], 16 * HG * (pair + 1)))
                run(step, pool)

            @block.scalar
            def _(act):
                rstd_scalar(act)

                def project(b, par, before_parts, before_v):
                    act.wait_ge(xnT_ps, b + 1)
                    act.activation(xnT[:].rearrange("p g s -> p (g s)"), a_ps[:, 0, 0:G * S], ACT.Copy)\
                        .then_inc(xnT_made, 1)
                    act.wait_ge(cT_ps, 2 * b + 1)
                    act.activation(ctxT[:, 0, :], a_ps[:, 1, 0:SC], ACT.Copy).then_inc(cT_made, 1)
                    act.wait_ge(cT_ps, 2 * b + 2)
                    act.activation(ctxT[0:LO, 1, :], a_ps[0:LO, 0, 0:SC], ACT.Copy).then_inc(cT_made, 1)
                    act.wait_ge(k_ps, 2 * (b + 1))
                    before_parts(act)
                    act.activation(parts[:, 0, :, S:SW], a_ps[:, :, 0:SC], ACT.Copy).then_inc(k1_made, 1)
                    before_v(act)
                    for kt, n in enumerate(KEYS):
                        act.wait_ge(v_ps, 3 * b + kt + 1)
                        act.activation(v[par][0:n, kt, :, 0:D], heads(a_ps[0:n, kt % 2, 0:C]), ACT.Copy)\
                            .then_inc(v_made, 1)

                act.wait_ge(presets, 3)
                project(0, 0, lambda eng: None, lambda eng: None)

                def step(b, par, pair, first, last):
                    if not first_layer and not first:
                        act.wait_ge(oT_ps, b)
                        act.activation(oT[:].rearrange("p g s -> p (g s)"), a_ps[:, 1, 0:G * S], ACT.Copy)\
                            .then_inc(oT_made, 1)
                    if not last:
                        project(b + 1, 1 - par, lambda eng: eng.wait_ge(stacked[par], 16 * HG * (pair + 1)),
                                lambda eng: eng.wait_ge(pv_done, P_BUFS + CHUNKS * b))
                    act.wait_ge(mT_ps, b + 1)
                    act.activation(mT[:], a_ps[0:3 * NH, 1, :].bitcast(BF16)[:, 0:S], ACT.Copy).then_inc(mT_made, 1)
                    act.wait_ge(mT_made, b + 1)
                    act.dma_start(stack[par][SROWS:MROWS, :, 0:S], mT[:]).then_inc(m_in[par], 16)
                    for c in range(CHUNKS):
                        act.wait_ge(pv_done, CHUNKS * b + c + 1)
                        for kt, n in enumerate(KEYS):
                            act.wait_ge(st_made, EXP * b + 3 * c + kt + 1)
                            act.activation(probs[c % P_BUFS][0:n, kt, :], st_ps[0:n, kt, 0:CHUNK * S],
                                           ACT.Exp, scale=SCALE).then_inc(exp_done, 1)

                act.sem_inc(exp_done, ST_BANKS)
                run(step, act)
                if not first_layer:
                    act.wait_ge(oT_ps, B)
                    act.activation(oT[:].rearrange("p g s -> p (g s)"), a_ps[:, 1, 0:G * S], ACT.Copy)\
                        .then_inc(oT_made, 1)

            @block.tensor
            def _(pe):
                def turn_xn(b):
                    pe.wait_ge(xn_made, b + 1)
                    for g in range(G):
                        last = pe.transpose(a_ps[:, 0, g * S:(g + 1) * S], xn[:, g * 128:(g + 1) * 128],
                                            sh.ident[0:S, 0:S])
                    last.then_inc(xnT_ps, 1)

                def turn_context_hi(b, par, pair):
                    pe.wait_ge(ctx_in[par], 32 * (pair + 1))
                    for kt, n in enumerate(KEYS):
                        last = pe.transpose(a_ps[:, 1, kt * KSTEP:kt * KSTEP + n], context[0:n, par, kt, 0:HI],
                                            sh.ident[0:n, 0:n])
                    last.then_inc(cT_ps, 1)

                def turn_context_lo(b, par):
                    pe.wait_ge(xnT_made, b + 1)
                    pe.sem_inc(tick, 1)
                    for kt, n in enumerate(KEYS):
                        last = pe.transpose(a_ps[0:LO, 0, kt * KSTEP:kt * KSTEP + n],
                                            context[0:n, par, kt, HI:CC], sh.ident[0:n, 0:n])
                    last.then_inc(cT_ps, 1)

                def project_q(b):
                    pe.wait_ge(xnT_made, b + 1)
                    pe.wait_ge(cT_made, 2 * b + 1)
                    for g in range(G):
                        for c in range(G):
                            last = pe.matmul(a_ps[:, 1, g * S:(g + 1) * S], wq[:, c, g * 128:(g + 1) * 128],
                                             xnT[:, c, :], start=(c == 0), stop=(c == G - 1))
                    last.then_inc(q_ps, 1)

                def project_k(b, g):
                    if g == 0:
                        pe.wait_ge(cT_made, 2 * b + 2)
                    else:
                        pe.wait_ge(qf_made, b + 1)
                    pe.matmul(a_ps[:, g, 0:SC], wk[:, 0, g * 128:(g + 1) * 128], ctxT[:, 0, :],
                              start=True, stop=False)
                    pe.matmul(a_ps[:, g, 0:SC], wk[0:LO + 1, 1, g * 128:(g + 1) * 128], ctxT[0:LO + 1, 1, :],
                              start=False, stop=True).then_inc(k_ps, 1)

                def project_v(b, kt):
                    n = KEYS[kt]
                    pe.wait_ge(krest_made, b + 1)
                    if kt == 2:
                        pe.wait_ge(v_made, 3 * b + 1)
                    keys = slice(kt * KSTEP, kt * KSTEP + n)
                    pe.matmul(a_ps[0:n, kt % 2, 0:C], ctxT[:, 0, keys], wv[:, 0, :], start=True, stop=False)
                    pe.matmul(a_ps[0:n, kt % 2, 0:C], ctxT[0:LO + 1, 1, keys], wv[0:LO + 1, 1, :],
                              start=False, stop=True).then_inc(v_ps, 1)

                def turn_sums(b, v_before):
                    pe.wait_ge(oT4_made, b + 1)
                    pe.wait_ge(v_made, v_before)
                    for c in range(CHUNKS):
                        last = pe.transpose(a_ps[0:S, 0, c * 128:(c + 1) * 128], oT4[:, c * S:(c + 1) * S],
                                            sh.ident[:])
                    last.then_inc(o_turned, 1)

                def turn_o(b):
                    pe.wait_ge(o_made, b + 1)
                    pe.wait_ge(mT_made, b + 1)
                    for g in range(G):
                        last = pe.transpose(a_ps[:, 1, g * S:(g + 1) * S], o[:, g * 128:(g + 1) * 128],
                                            sh.ident[0:S, 0:S])
                    last.then_inc(oT_ps, 1)

                def project_out(b):
                    pe.wait_ge(oT_made, b + 1)
                    for c in range(G):
                        last = pe.matmul(a_ps[0:S, 1, 0:C], oT[:, c, :], sh.wo1[:, c, :],
                                         start=(c == 0), stop=(c == G - 1))
                    last.then_inc(out_ps, 1)

                def row_scores(b, par, h):
                    pe.wait_ge(rows_free, NH * b + h + 1)
                    pe.matmul(rows_ps[0:S, h % ROW_BANKS, 0:SC], stack[par][0:SROWS, h, 0:S],
                              stack[par][0:SROWS, h, S:SW], start=True, stop=True).then_inc(rows_made, 1)

                def projections(b, par, pair):
                    def xn_free():
                        pe.wait_ge(v_made, 3 * b)
                        pe.wait_ge(o_made, b - 1)
                        turn_xn(b)

                    def hi_free():
                        pe.wait_ge(mT_made if first_layer else out_read, b - 1)
                        pe.wait_ge(v_made, 3 * b)
                        turn_context_hi(b, par, pair)

                    return {2: xn_free, 7: hi_free, 8: lambda: turn_context_lo(b, par), 9: lambda: project_q(b),
                            10: lambda: project_k(b, 0), 11: lambda: project_k(b, 1),
                            13: lambda: project_v(b, 0), 14: lambda: project_v(b, 1), 15: lambda: project_v(b, 2)}

                def step(b, par, pair, first, last):
                    before = not first
                    between = {} if last else projections(b + 1, 1 - par, pair + par)
                    pe.wait_ge(stacked[par], 16 * HG * (pair + 1))
                    for h in range(NH):
                        row_scores(b, par, h)
                        if before and h == 0:
                            turn_sums(b - 1, 3 * (b + 1))
                        if before and not first_layer and h == 3:
                            turn_o(b - 1)
                        if before and not first_layer and h == 5:
                            project_out(b - 1)
                        if h in between:
                            between[h]()
                    pe.wait_ge(m_steps, 4 * (b + 1))
                    pe.wait_ge(v_made, 3 * B if last else 3 * (b + 2) - 1)
                    if last:
                        pe.wait_ge(mT_made if first_layer else out_read, b)
                    pe.sem_inc(tick, 1)
                    pe.transpose(a_ps[0:3 * NH, 1, :].bitcast(BF16)[:, 0:S], mparts[:].rearrange("p j h -> p (j h)"),
                                 sh.identb[0:S, 0:S]).then_inc(mT_ps, 1)

                    def scores_T(c):
                        for kt, n in enumerate(KEYS):
                            pe.wait_ge(exp_done, EXP * b + 3 * c + kt + 1)
                            for j in range(CHUNK):
                                h = c * CHUNK + j
                                last_mm = pe.matmul(st_ps[0:n, kt, j * S:(j + 1) * S],
                                                    stack[par][:, h, S + kt * KSTEP:S + kt * KSTEP + n],
                                                    stack[par][:, h, 0:S], start=True, stop=True)
                            last_mm.then_inc(st_made, 1)

                    def weighted_sums(c):
                        if c == 0:
                            pe.wait_ge(oT4_made, b)
                        for kt, n in enumerate(KEYS):
                            pe.wait_ge(exp_done, ST_BANKS + EXP * b + 3 * c + kt + 1)
                            for j in range(CHUNK):
                                last_mm = pe.matmul(o_ps[j * VW:(j + 1) * VW, c * S:(c + 1) * S],
                                                    v[par][0:n, kt, c * CHUNK + j, :],
                                                    probs[c % P_BUFS][0:n, kt, j * S:(j + 1) * S],
                                                    start=(kt == 0), stop=(kt == 2))
                        last_mm.then_inc(pv_done, 1)

                    pe.wait_ge(m_in[par], 16 * (pair + 1))
                    scores_T(0)
                    for c in range(CHUNKS):
                        if c + 1 < CHUNKS:
                            scores_T(c + 1)
                        weighted_sums(c)

                pe.wait_ge(presets, 3)
                pe.wait_ge(stack_preset, 2)
                turn_xn(0)
                turn_context_hi(0, 0, 0)
                turn_context_lo(0, 0)
                project_q(0)
                project_k(0, 0)
                project_k(0, 1)
                for kt in range(3):
                    project_v(0, kt)
                pe.sem_inc(pv_done, P_BUFS)
                run(step, pe)
                turn_sums(B - 1, 3 * B)
                if not first_layer:
                    turn_o(B - 1)
                    project_out(B - 1)

            @block.vector
            def _(dve):
                rstd_vector(dve)
                if first_layer:
                    dve.tensor_tensor(scaled[:], sh.rstd[:], sh.keep[:], ALU.mult).then_inc(scaled_ready, 1)
                else:
                    dve.tensor_copy(scaled[:], sh.rstd[:]).then_inc(scaled_ready, 1)
                dve.wait_ge(scaled_ready, 1)
                dve.memset(ctxT[LO:LO + 1, 1, :], 1.0).then_inc(presets, 1)
                for p in range(2):
                    dve.memset(v[p][:], 0.0).then_inc(v_cleared, 1)
                dve.wait_ge(v_cleared, 2)
                for p in range(2):
                    dve.memset(v[p][:, :, :, D:D + 1], 1.0).then_inc(presets, 1)
                dve.sem_inc(rows_free, ROW_BANKS)

                def normalise(b, turned):
                    turned(dve)
                    dve.tensor_scalar(xn[:], sh.x[:, b, :], sh.mv[:, b, 0:1], scaled[:, bass.ds(b, 1)],
                                      ALU.subtract, ALU.mult).then_inc(xn_made, 1)

                def read_q(b):
                    dve.wait_ge(q_ps, b + 1)
                    dve.wait_ge(q_cut, 7 * b)
                    if first_layer:
                        dve.tensor_copy(qf[:].rearrange("p g s -> p (g s)"), a_ps[:, 1, 0:G * S])\
                            .then_inc(qf_made, 1)
                    else:
                        dve.tensor_tensor(qf[:], a_ps[:, 1, 0:G * S].rearrange("p (g s) -> p g s", g=G),
                                          sh.bq1[:].unsqueeze(2).to_broadcast([128, G, S]), ALU.add)\
                            .then_inc(qf_made, 1)

                def rest_of_k(b):
                    dve.wait_ge(k1_made, b + 1)
                    dve.tensor_tensor(krest[:], a_ps[:, :, 0:SC], parts[:, 0, :, S:SW], ALU.subtract)\
                        .then_inc(krest_made, 1)

                def third_k(b):
                    dve.wait_ge(k_cut, 4 * b + 3)
                    dve.tensor_tensor(parts[:, 3, :, S:SW], krest[:], parts[:, 1, :, S:SW], ALU.subtract)\
                        .then_inc(k3_made, 1)

                def read_sums(b):
                    dve.wait_ge(pv_done, P_BUFS + CHUNKS * (b + 1))
                    dve.tensor_copy(oT4[:], o_ps[:, 0:CHUNKS * S]).then_inc(oT4_made, 1)

                def normalise_sums(b):
                    dve.wait_ge(o_turned, b + 1)
                    per_head = a_ps[0:S, 0, :].rearrange("p (h w) -> p h w", w=VW)
                    dve.reciprocal(rden[:], per_head[:, :, D]).then_inc(rden_made, 1)
                    dve.wait_ge(rden_made, b + 1)
                    dve.tensor_tensor(heads(o[:]), per_head[:, :, 0:D],
                                      rden[:].unsqueeze(2).to_broadcast([S, NH, D]), ALU.mult).then_inc(o_made, 1)
                    dve.wait_ge(o_made, b + 1)

                def add_to_x(b):
                    n = 3 * b
                    if not first_layer:
                        dve.wait_ge(out_ps, b + 1)
                        dve.tensor_tensor(biased[:], a_ps[0:S, 1, 0:C], sh.bo1[:], ALU.add).then_inc(out_read, 1)
                        dve.wait_ge(out_read, b + 1)
                    source = o if first_layer else biased
                    dve.scalar_tensor_tensor(out=sh.x[:, b, :], in0=source[:], scalar=sh.tg[0:S, layer:layer + 1],
                                             in1=sh.x[:, b, :], op0=ALU.mult, op1=ALU.add).then_inc(x_steps, 1)
                    dve.wait_ge(x_steps, n + 1)
                    dve.sem_inc(tick, 1)
                    dve.bn_stats(stats[:], sh.x[:, b, :]).then_inc(x_steps, 1)
                    dve.wait_ge(x_steps, n + 2)
                    dve.sem_inc(tick, 1)
                    dve.bn_aggr(mv_now[:], stats[:]).then_inc(x_steps, 1)
                    dve.wait_ge(x_steps, n + 3)
                    dve.tensor_scalar(sh.mv[:, b, :], mv_now[:], 1.0, None, ALU.mult).then_inc(stats_made, 1)

                def row_max(b, h):
                    dve.wait_ge(rows_made, NH * b + h + 1)
                    if h == 0:
                        dve.wait_ge(m_steps, 4 * b)
                    dve.tensor_reduce(rowmax[:, h:h + 1], rows_ps[0:S, h % ROW_BANKS, 0:SC], AX.X, ALU.max)\
                        .then_inc(rows_free, 1)

                def cut_max(b):
                    n = 4 * b
                    dve.wait_ge(rows_free, ROW_BANKS + NH * (b + 1))
                    dve.wait_ge(mT_ps, b)
                    dve.tensor_scalar(mparts[:, 0, :], rowmax[:], -1.0, None, ALU.mult).then_inc(m_steps, 1)
                    dve.wait_ge(m_steps, n + 1)
                    dve.scalar_tensor_tensor(out=mrest[:], in0=rowmax[:], scalar=-1.0, in1=mparts[:, 0, :],
                                             op0=ALU.mult, op1=ALU.subtract).then_inc(m_steps, 1)
                    dve.wait_ge(m_steps, n + 2)
                    dve.tensor_copy(mparts[:, 1, :], mrest[:]).then_inc(m_steps, 1)
                    dve.wait_ge(m_steps, n + 3)
                    dve.tensor_tensor(mparts[:, 2, :], mrest[:], mparts[:, 1, :], ALU.subtract).then_inc(m_steps, 1)

                normalise(0, lambda eng: None)
                read_q(0)
                rest_of_k(0)
                third_k(0)

                def step(b, par, pair, first, last):
                    before = not first
                    if before:
                        read_sums(b - 1)
                    if not last:
                        normalise(b + 1, lambda eng: eng.wait_ge(xnT_ps, b + 1))
                    for h in range(NH):
                        row_max(b, h)
                        if before and h == 1:
                            normalise_sums(b - 1)
                            if first_layer:
                                add_to_x(b - 1)
                        if before and not first_layer and h == 5:
                            add_to_x(b - 1)
                        if not last:
                            if h == 8:
                                read_q(b + 1)
                            if h == 11:
                                rest_of_k(b + 1)
                            if h == 13:
                                dve.wait_ge(stacked[par], 16 * HG * (pair + 1))
                                third_k(b + 1)
                    cut_max(b)

                run(step, dve)
                read_sums(B - 1)
                normalise_sums(B - 1)
                add_to_x(B - 1)


def normalise_all(nc, sh, ctx, block_name, xnT_all, xn2, tr_ps):
    xn_made = ctx.enter_context(nc.semaphore(f"{block_name}_xn_made"))
    xn_turned = ctx.enter_context(nc.semaphore(f"{block_name}_xn_turned"))
    xnT_made = ctx.enter_context(nc.semaphore(f"{block_name}_xnT_made"))
    rstd_vector, rstd_scalar = rstd_steps(nc, sh, ctx, block_name)

    def on_vector(dve):
        rstd_vector(dve)

        def one(b, par, first):
            if not first:
                dve.wait_ge(xn_turned, b - 1)
            dve.tensor_scalar(xn2[:, par, :], sh.x[:, b, :], sh.mv[:, b, 0:1], sh.rstd[:, bass.ds(b, 1)],
                              ALU.subtract, ALU.mult).then_inc(xn_made, 1)
        for par in range(2):
            one(par, par, True)
        with dve.Fori(1, B // 2) as pair:
            for par in range(2):
                one(2 * pair + par, par, False)

    def on_tensor(pe):
        def one(b, par, first):
            pe.wait_ge(xn_made, b + 1)
            if not first:
                pe.wait_ge(xnT_made, b - 1)
            for g in range(G):
                last = pe.transpose(tr_ps[:, par, g * S:(g + 1) * S], xn2[:, par, g * 128:(g + 1) * 128],
                                    sh.ident[0:S, 0:S])
            last.then_inc(xn_turned, 1)
        for par in range(2):
            one(par, par, True)
        with pe.Fori(1, B // 2) as pair:
            for par in range(2):
                one(2 * pair + par, par, False)

    def on_scalar(act):
        rstd_scalar(act)
        with act.Fori(0, B // 2) as pair:
            for par in range(2):
                b = 2 * pair + par
                act.wait_ge(xn_turned, b + 1)
                act.activation(xnT_all[:, :, b, :], tr_ps[:, par, 0:G * S].rearrange("p (g s) -> p g s", g=G),
                               ACT.Copy).then_inc(xnT_made, 1)

    return on_vector, on_tensor, on_scalar, xnT_made


def experts_phase(nc, t, sh, w1, w2a, w1_in):
    with ExitStack() as ctx:
        def sb(name, shape, dt=F32):
            return ctx.enter_context(nc.sbuf_tensor(name, shape, dt))

        def sem(name):
            return ctx.enter_context(nc.semaphore(name))

        w2b = sb("w2b", [128, FT - W2A, E, C])
        b2 = sb("b2", [S, E, C])
        gate_w = sb("gate_w", [128, G, E])
        xnT_all = sb("xnT_all", [128, G, B, S])
        xn2 = sb("xn2", [S, 2, C])
        mean = sb("mean", [128, G, B])
        logits = sb("logits", [B, E])
        top_logit = sb("top_logit", [B, 1])
        prob = sb("prob", [B, E])
        prob_sum = sb("prob_sum", [B, 1])
        best = sb("best", [B, 8])
        best_at = sb("best_at", [B, 8], U32)
        pair_sum = sb("pair_sum", [B, 1])
        weight = sb("weight", [B, TOP])
        at_row = sb("at_row", [1, B * TOP], U32)
        weight_row = sb("weight_row", [1, B * TOP])
        weight_all = sb("weight_all", [S, B * TOP])
        xnT = sb("xnT_now", [128, G, S])
        hid = [sb(f"hid{j}", [S, F]) for j in range(TOP)]
        biased = sb("hid_biased", [128, FT, S])
        act_hid = [sb(f"act_hid{j}", [128, FT, S]) for j in range(TOP)]
        stats = sb("stats_e", [S, 6])
        mv_now = sb("mv_now_e", [S, 2])

        h_ps = ctx.enter_context(nc.psum_tensor("h_ps", [128, 2 * TOP, 512], F32))
        t_ps = ctx.enter_context(nc.psum_tensor("t_ps", [128, 2, 512], F32))
        y_ps = ctx.enter_context(nc.psum_tensor("y_ps", [128, TOP, 512], F32))

        tick = sem("tick_e")
        gate_in = sem("gate_in")
        w2b_in = sem("w2b_in")
        b2_in = sem("b2_in")
        mean_steps = sem("mean_steps")
        logits_ps = sem("logits_ps")
        route = sem("route_steps")
        prob_made = sem("prob_made")
        row_in = sem("choice_rows_in")
        at_in = sem("chosen_in")
        spread = sem("weights_spread")
        weight_ready = sem("weight_ready")
        xnT_ready = sem("xnT_now_made")
        h_made = sem("h_made")
        hid_made = sem("hid_made")
        hid_turned = sem("hid_turned")
        biased_made = sem("biased_made")
        act_made = sem("act_made")
        y_made = sem("y_made")
        y_read = sem("y_read")
        x_steps = sem("x_steps_e")
        stats_made = sem("stats_made_e")

        on_vector, on_tensor, on_scalar, xnT_made = normalise_all(nc, sh, ctx, "experts", xnT_all, xn2, t_ps)
        on_partitions = "(f p) n -> p f n"

        with nc.Block() as block:
            @block.sync
            def _(sp):
                for e in range(E):
                    sp.dma_start(w2b[:, :, e, :], t["e_w2"][e, W2A * 128:F, :].rearrange(on_partitions, p=128))\
                        .then_inc(w2b_in, 16)
                sp.wait_ge(route, 6)
                sp.dma_start(at_row[:], best_at[:, 0:TOP]).then_inc(at_in, 16)
                sp.dma_start(weight_row[:], weight[:]).then_inc(row_in, 16)

            @block.gpsimd
            def _(pool):
                pool.dma_start(gate_w[:], t["gate_w"].rearrange("(g p) e -> p g e", p=128)).then_inc(gate_in, 16)
                pool.dma_start(b2[:], t["e_b2"].partition_broadcast(S)).then_inc(b2_in, 16)
                pool.wait_ge(xnT_made, B)
                pool.tensor_copy(xnT[:], xnT_all[:, :, 0, :]).then_inc(xnT_ready, 1)
                with pool.Fori(1, B) as b:
                    pool.wait_ge(h_made, TOP * b)
                    pool.sem_inc(tick, 1)
                    pool.tensor_copy(xnT[:], xnT_all[:, :, b, :]).then_inc(xnT_ready, 1)

            @block.scalar
            def _(act):
                on_scalar(act)
                act.wait_ge(route, 2)
                act.activation(prob[:], logits[:], ACT.Exp, bias=top_logit[:]).then_inc(prob_made, 1)

                def copy_hidden(k, j):
                    act.wait_ge(h_made, k + 1)
                    act.activation(hid[j][:].rearrange("p (a n) -> p a n", a=2),
                                   h_ps[0:S, 2 * j:2 * j + 2, :], ACT.Copy).then_inc(hid_made, 1)

                def gelu(k, j):
                    act.wait_ge(biased_made, k + 1)
                    act.activation(act_hid[j][:], biased[:], ACT.Gelu).then_inc(act_made, 1)

                copy_hidden(0, 0)
                copy_hidden(1, 1)
                gelu(0, 0)
                with act.Fori(1, B) as b:
                    copy_hidden(2 * b, 0)
                    gelu(2 * b - 1, 1)
                    copy_hidden(2 * b + 1, 1)
                    gelu(2 * b, 0)
                gelu(TOP * B - 1, 1)

            @block.tensor
            def _(pe):
                on_tensor(pe)
                pe.wait_ge(mean_steps, 2)
                pe.wait_ge(gate_in, 16)
                for g in range(G):
                    last = pe.matmul(y_ps[0:B, 0, 0:E], mean[:, g, :], gate_w[:, g, :], start=(g == 0),
                                     stop=(g == G - 1))
                last.then_inc(logits_ps, 1)
                pe.wait_ge(row_in, 16)
                pe.matmul(y_ps[0:S, 1, 0:TOP * B], sh.ones[0:1, 0:S], weight_row[:], start=True, stop=True)\
                    .then_inc(spread, 1)
                pe.wait_ge(at_in, 16)
                pe.wait_ge(w1_in, 16 * B)

                def first_product(b, j, free):
                    e = pe.value_load(at_row[0:1, bass.ds(TOP * b + j, 1)], min_val=0, max_val=E - 1)
                    if j == 0:
                        pe.wait_ge(xnT_ready, b + 1)
                    if free:
                        pe.wait_ge(hid_made, TOP * b + j - 1)
                    for half in range(2):
                        for g in range(G):
                            last = pe.matmul(h_ps[0:S, 2 * j + half, :], xnT[:, g, :],
                                             w1[:, g, e, half * 512:(half + 1) * 512],
                                             start=(g == 0), stop=(g == G - 1))
                    last.then_inc(h_made, 1)

                def turn_hidden(k, j, free):
                    pe.wait_ge(hid_made, k + 1)
                    if free:
                        pe.wait_ge(biased_made, k)
                    for f in range(FT):
                        last = pe.transpose(t_ps[:, f // 4, (f % 4) * S:(f % 4 + 1) * S],
                                            hid[j][:, f * 128:(f + 1) * 128], sh.ident[0:S, 0:S])
                    last.then_inc(hid_turned, 1)

                def second_product(b, j, free):
                    e = pe.value_load(at_row[0:1, bass.ds(TOP * b + j, 1)], min_val=0, max_val=E - 1)
                    pe.wait_ge(act_made, TOP * b + j + 1)
                    if free:
                        pe.wait_ge(y_read, TOP * b + j - 1)
                    for f in range(FT):
                        w = w2a[:, f, e, :] if f < W2A else w2b[:, f - W2A, e, :]
                        last = pe.matmul(y_ps[0:S, j, 0:C], act_hid[j][:, f, :], w, start=(f == 0),
                                         stop=(f == FT - 1))
                    last.then_inc(y_made, 1)

                first_product(0, 0, False)
                first_product(0, 1, False)
                turn_hidden(0, 0, False)
                pe.wait_ge(weight_ready, 1)
                pe.wait_ge(w2b_in, 16 * E)

                def step(b, free):
                    first_product(b, 0, True)
                    turn_hidden(2 * b - 1, 1, True)
                    second_product(b - 1, 0, free)
                    first_product(b, 1, True)
                    turn_hidden(2 * b, 0, True)
                    second_product(b - 1, 1, free)

                step(1, False)
                with pe.Fori(2, B) as b:
                    step(b, True)
                turn_hidden(TOP * B - 1, 1, True)
                second_product(B - 1, 0, True)
                second_product(B - 1, 1, True)

            @block.vector
            def _(dve):
                on_vector(dve)
                dve.wait_ge(xnT_made, B)
                dve.tensor_reduce(mean[:], xnT_all[:], AX.X, ALU.add).then_inc(mean_steps, 1)
                dve.wait_ge(mean_steps, 1)
                dve.tensor_scalar(mean[:], mean[:], 1.0 / S, None, ALU.mult).then_inc(mean_steps, 1)
                dve.wait_ge(logits_ps, 1)
                dve.tensor_copy(logits[:], y_ps[0:B, 0, 0:E]).then_inc(route, 1)
                dve.wait_ge(route, 1)
                dve.tensor_reduce(top_logit[:], logits[:], AX.X, ALU.max, negate=True).then_inc(route, 1)
                dve.wait_ge(prob_made, 1)
                dve.tensor_reduce(prob_sum[:], prob[:], AX.X, ALU.add).then_inc(prob_made, 1)
                dve.wait_ge(prob_made, 2)
                dve.reciprocal(prob_sum[:], prob_sum[:]).then_inc(prob_made, 1)
                dve.wait_ge(prob_made, 3)
                dve.tensor_scalar(prob[:], prob[:], prob_sum[:], None, ALU.mult).then_inc(prob_made, 1)
                dve.wait_ge(prob_made, 4)
                dve.max(best[:], prob[:]).then_inc(route, 1)
                dve.wait_ge(route, 3)
                dve.max_index(best_at[:], best[:], prob[:]).then_inc(route, 1)
                dve.tensor_tensor(pair_sum[:], best[:, 0:1], best[:, 1:2], ALU.add).then_inc(route, 1)
                dve.wait_ge(route, 5)
                dve.reciprocal(pair_sum[:], pair_sum[:]).then_inc(prob_made, 1)
                dve.wait_ge(prob_made, 5)
                dve.tensor_scalar(weight[:], best[:, 0:TOP], pair_sum[:], sh.tg[0:B, 2:3], ALU.mult, ALU.mult)\
                    .then_inc(route, 1)
                dve.wait_ge(spread, 1)
                dve.tensor_copy(weight_all[:], y_ps[0:S, 1, 0:TOP * B]).then_inc(weight_ready, 1)
                dve.wait_ge(weight_ready, 1)
                dve.wait_ge(at_in, 16)
                dve.wait_ge(b2_in, 16)

                def add_bias(b, j, free):
                    e = dve.value_load(at_row[0:1, bass.ds(TOP * b + j, 1)], min_val=0, max_val=E - 1)
                    dve.wait_ge(hid_turned, TOP * b + j + 1)
                    if free:
                        dve.wait_ge(act_made, TOP * b + j)
                    dve.tensor_tensor(
                        biased[:].rearrange("p (a f) s -> p a f s", a=2),
                        t_ps[:, :, 0:4 * S].rearrange("p a (f s) -> p a f s", s=S),
                        sh.eb1[:, e, :].rearrange("p (a f) -> p a f", a=2).unsqueeze(3).to_broadcast([128, 2, 4, S]),
                        ALU.add).then_inc(biased_made, 1)

                def add_output(b, j):
                    e = dve.value_load(at_row[0:1, bass.ds(TOP * b + j, 1)], min_val=0, max_val=E - 1)
                    n = 7 * b + 2 * j
                    w = weight_all[:, bass.ds(TOP * b + j, 1)]
                    xb = sh.x[:, b, :]
                    dve.wait_ge(x_steps, n)
                    dve.scalar_tensor_tensor(out=xb, in0=b2[:, e, :], scalar=w, in1=xb, op0=ALU.mult, op1=ALU.add)\
                        .then_inc(x_steps, 1)
                    dve.wait_ge(y_made, TOP * b + j + 1)
                    dve.wait_ge(x_steps, n + 1)
                    dve.scalar_tensor_tensor(out=xb, in0=y_ps[0:S, j, 0:C], scalar=w, in1=xb, op0=ALU.mult,
                                             op1=ALU.add).then_inc(x_steps, 1)
                    dve.wait_ge(x_steps, n + 2)
                    dve.sem_inc(y_read, 1)
                    if j == 1:
                        dve.sem_inc(tick, 1)
                        dve.bn_stats(stats[:], xb).then_inc(x_steps, 1)
                        dve.wait_ge(x_steps, n + 3)
                        dve.sem_inc(tick, 1)
                        dve.bn_aggr(mv_now[:], stats[:]).then_inc(x_steps, 1)
                        dve.wait_ge(x_steps, n + 4)
                        dve.tensor_scalar(sh.mv[:, b, :], mv_now[:], 1.0, None, ALU.mult).then_inc(x_steps, 1)

                add_bias(0, 0, False)
                with dve.Fori(1, B) as b:
                    add_bias(b - 1, 1, True)
                    add_output(b - 1, 0)
                    add_bias(b, 0, True)
                    add_output(b - 1, 1)
                add_bias(B - 1, 1, True)
                add_output(B - 1, 0)
                add_output(B - 1, 1)


def fixed_point_phase(nc, sh, w1, w2, b2, weights_in, out_dram):
    with ExitStack() as ctx:
        def sb(name, shape, dt=F32):
            return ctx.enter_context(nc.sbuf_tensor(name, shape, dt))

        def sem(name):
            return ctx.enter_context(nc.semaphore(name))

        N = QUAD * S
        xnT_all = sb("xnT_all_f", [128, G, B, S])
        xn2 = sb("xn2_f", [S, 2, C])
        steps = [sb(f"steps{p}", [128, N]) for p in range(2)]
        n_in = [sb(f"n_in{p}", [128, N]) for p in range(2)]
        clipped = [sb(f"clipped{p}", [128, N]) for p in range(2)]
        seg = [sb(f"seg{p}", [128, N]) for p in range(2)]
        g0 = [sb(f"g0_{p}", [128, N]) for p in range(2)]
        g1 = [sb(f"g1_{p}", [128, N]) for p in range(2)]
        back = [sb(f"back{p}", [128, N]) for p in range(2)]
        over = [sb(f"over{p}", [128, N]) for p in range(2)]
        hidden = [sb(f"hidden{p}", [128, FT, N]) for p in range(2)]
        b2s = sb("b2s", [S, C])
        tgs = sb("tgs", [S, 1])
        y = [sb(f"y{p}", [S, C]) for p in range(2)]

        h_ps = ctx.enter_context(nc.psum_tensor("h_ps_f", [128, 2, 512], F32))
        y_ps = ctx.enter_context(nc.psum_tensor("y_ps_f", [128, 2, 512], F32))
        t_ps = ctx.enter_context(nc.psum_tensor("t_ps_f", [128, 2, 512], F32))

        h_made = sem("h_made_f")
        h_read = sem("h_read_f")
        rounded = sem("rounded")
        gelus = sem("gelus")
        sides = sem("sides")
        hid_steps = sem("hid_steps")
        y_made = sem("y_made_f")
        y_steps = sem("y_steps")
        consts = sem("consts_f")
        stored = sem("stored")

        on_vector, on_tensor, on_scalar, xnT_made = normalise_all(nc, sh, ctx, "fixed", xnT_all, xn2, t_ps)
        QUADS = B // QUAD

        with nc.Block() as block:
            @block.sync
            def _(sp):
                with sp.Fori(0, B) as b:
                    sp.wait_ge(y_steps, 4 * (b + 1))
                    sp.dma_start(out_dram[b, :, :], sh.x[:, b, :]).then_inc(stored, 16)
                sp.wait_ge(stored, 16 * B)

            def tiles(eng, step):
                for p in range(2):
                    step(p, p, p, 0, 0, True)
                for f in range(2, FT):
                    step(f, f, f % 2, 0, 0, False)
                with eng.Fori(1, QUADS) as q:
                    for f in range(FT):
                        step(FT * q + f, f, f % 2, q, None, False)

            @block.tensor
            def _(pe):
                on_tensor(pe)
                pe.wait_ge(weights_in, 16 * 3)
                pe.wait_ge(xnT_made, B)

                def hidden_tile(k, f, q, first):
                    if not first:
                        pe.wait_ge(h_read, k - 1)
                    for g in range(G):
                        last = pe.matmul(h_ps[:, f % 2, 0:N], w1[:, g, f * 128:(f + 1) * 128],
                                         xnT_all[:, g, bass.ds(QUAD * q, QUAD), :],
                                         start=(g == 0), stop=(g == G - 1))
                    last.then_inc(h_made, 1)

                def output_tile(b, i, p, first):
                    if not first:
                        pe.wait_ge(y_steps, 4 * (b - 1) - 3)
                    for f in range(FT):
                        last = pe.matmul(y_ps[0:S, i % 2, 0:C], hidden[p][:, f, i * S:(i + 1) * S], w2[:, f, :],
                                         start=(f == 0), stop=(f == FT - 1))
                    last.then_inc(y_made, 1)

                def quad(q, p, first, more):
                    for i in range(QUAD):
                        if more:
                            for f in (2 * i, 2 * i + 1):
                                hidden_tile(FT * (q + 1) + f, f, q + 1, False)
                        if i == 0:
                            pe.wait_ge(hid_steps, 4 * FT * (q + 1))
                        output_tile(QUAD * q + i, i, p, first and i < 2)

                for f in range(FT):
                    hidden_tile(f, f, 0, f < 2)
                for q in range(QUADS):
                    quad(q, q % 2, q == 0, q + 1 < QUADS)

            @block.scalar
            def _(act):
                on_scalar(act)

                def fill(k, f):
                    p = f % 2
                    act.wait_ge(h_made, k + 1)
                    act.activation(steps[p][:], h_ps[:, p, 0:N], ACT.Identity, bias=sh.fb1[:, f:f + 1], scale=FIX)\
                        .then_inc(h_read, 1)

                def ends(k, f):
                    p = f % 2
                    act.wait_ge(rounded, 4 * k + 3)
                    for n, g in enumerate((g0, g1)):
                        act.activation(g[p][:], seg[p][:], ACT.Gelu, bias=sh.gelu_bias[:, n:n + 1], scale=1 / FIX)\
                            .then_inc(gelus, 1)

                for q in range(QUADS):
                    for f in range(FT):
                        k = FT * q + f
                        if k >= 2:
                            act.wait_ge(rounded, 4 * (k - 2) + 1)
                            act.wait_ge(hid_steps, 4 * (k - 2) + 2)
                        fill(k, f)
                        ends(k, f)

            @block.gpsimd
            def _(pool):
                for q in range(QUADS):
                    for f in range(FT):
                        k, p = FT * q + f, f % 2
                        pool.wait_ge(rounded, 4 * k + 1)
                        if k >= 2:
                            pool.wait_ge(hid_steps, 4 * (k - 2) + 4)
                        pool.tensor_scalar(over[p][:], n_in[p][:], LIM, 0.0, ALU.subtract, ALU.max)\
                            .then_inc(sides, 1)
                        pool.wait_ge(gelus, 2 * (k + 1))
                        pool.tensor_tensor(g1[p][:], g1[p][:], g0[p][:], ALU.subtract).then_inc(sides, 1)

            @block.vector
            def _(dve):
                on_vector(dve)
                dve.wait_ge(weights_in, 16 * 3)
                dve.tensor_scalar(b2s[:], b2[:], FIX, None, ALU.mult).then_inc(consts, 1)
                dve.tensor_scalar(tgs[:], sh.tg[0:S, 3:4], 1 / FIX, None, ALU.mult).then_inc(consts, 1)
                dve.wait_ge(consts, 2)

                def place(k, f):
                    p, n = f % 2, 4 * k
                    dve.wait_ge(h_read, k + 1)
                    if k >= 2:
                        dve.wait_ge(sides, 2 * (k - 1))
                    dve.tensor_scalar(n_in[p][:], steps[p][:], ROUND, ROUND, ALU.add, ALU.subtract)\
                        .then_inc(rounded, 1)
                    dve.wait_ge(rounded, n + 1)
                    dve.tensor_scalar(clipped[p][:], n_in[p][:], LIM, -LIM, ALU.min, ALU.max).then_inc(rounded, 1)
                    dve.wait_ge(rounded, n + 2)
                    if k >= 2:
                        dve.wait_ge(gelus, 2 * (k - 1))
                    dve.tensor_scalar(seg[p][:], clipped[p][:], -(SEG - 1) / 2, ROUND * SEG, ALU.add, ALU.add)\
                        .then_inc(rounded, 1)
                    dve.wait_ge(rounded, n + 3)
                    dve.scalar_tensor_tensor(out=back[p][:], in0=seg[p][:], scalar=ROUND * SEG, in1=clipped[p][:],
                                             op0=ALU.subtract, op1=ALU.subtract).then_inc(rounded, 1)

                def interpolate(k, f, buf):
                    p, n = f % 2, 4 * k
                    dve.wait_ge(rounded, n + 4)
                    dve.wait_ge(sides, 2 * (k + 1))
                    dve.tensor_tensor(back[p][:], back[p][:], g1[p][:], ALU.mult).then_inc(hid_steps, 1)
                    dve.wait_ge(hid_steps, n + 1)
                    dve.scalar_tensor_tensor(out=back[p][:], in0=back[p][:], scalar=-1 / SEG, in1=g0[p][:],
                                             op0=ALU.mult, op1=ALU.add).then_inc(hid_steps, 1)
                    dve.wait_ge(hid_steps, n + 2)
                    dve.tensor_scalar(back[p][:], back[p][:], FIX, ROUND, ALU.mult, ALU.add).then_inc(hid_steps, 1)
                    dve.wait_ge(hid_steps, n + 3)
                    dve.scalar_tensor_tensor(out=hidden[buf][:, f, :], in0=back[p][:], scalar=ROUND, in1=over[p][:],
                                             op0=ALU.subtract, op1=ALU.add).then_inc(hid_steps, 1)

                def add_output(b, i):
                    p, n = i % 2, 4 * b
                    dve.wait_ge(y_made, b + 1)
                    dve.tensor_tensor(y[p][:], y_ps[0:S, p, 0:C], b2s[:], ALU.add).then_inc(y_steps, 1)
                    dve.wait_ge(y_steps, n + 1)
                    dve.tensor_scalar(y[p][:], y[p][:], ROUND, None, ALU.add).then_inc(y_steps, 1)
                    dve.wait_ge(y_steps, n + 2)
                    dve.tensor_scalar(y[p][:], y[p][:], ROUND, tgs[:], ALU.subtract, ALU.mult).then_inc(y_steps, 1)
                    dve.wait_ge(y_steps, n + 3)
                    dve.tensor_tensor(sh.x[:, b, :], y[p][:], sh.x[:, b, :], ALU.add).then_inc(y_steps, 1)

                for q in range(QUADS + 1):
                    for f in range(FT):
                        if q < QUADS:
                            k = FT * q + f
                            if q >= 2 and f == 0:
                                dve.wait_ge(y_made, QUAD * (q - 1))
                            place(k, f)
                            if k >= 1:
                                j = k - 1
                                interpolate(j, j % FT, (j // FT) % 2)
                        elif f == 0:
                            j = FT * QUADS - 1
                            interpolate(j, j % FT, (j // FT) % 2)
                        if q >= 1 and f % 2 == 1:
                            add_output(QUAD * (q - 1) + f // 2, f // 2)


def flamingo_kernel(nc, t, out_dram):
    with ExitStack() as ctx:
        def sb(name, shape, dt=F32, scope=ctx):
            return scope.enter_context(nc.sbuf_tensor(name, shape, dt))

        sh = Shared()
        sh.x = sb("x", [S, B, C])
        sh.mv = sb("mv", [S, B, 2])
        sh.rstd = sb("rstd", [S, B])
        sh.keep = sb("keep", [S, B])
        sh.tg = sb("tg", [128, 4])
        sh.ident = sb("ident", [128, 128])
        sh.identb = sb("identb", [128, 128], BF16)
        sh.ones = sb("ones", [1, 128])
        sh.gelu_bias = sb("gelu_bias", [128, 2])
        sh.eb1 = sb("eb1", [128, E, FT])
        sh.fb1 = sb("fb1", [128, FT])
        sh.bq1 = sb("bq1", [128, G])
        sh.bo1 = sb("bo1", [S, C])
        sh.wq0, sh.wk0, sh.wv0 = sb("wq0", [128, G, C]), sb("wk0", [128, 2, C]), sb("wv0", [128, 2, C])
        sh.wq1, sh.wk1, sh.wv1 = sb("wq1", [128, G, C]), sb("wk1", [128, 2, C]), sb("wv1", [128, 2, C])
        sh.wo1 = sb("wo1", [128, G, C])
        sh.later = ctx.enter_context(nc.semaphore("layer1_loaded"))
        w1_in = ctx.enter_context(nc.semaphore("expert_w_in"))
        ffn_in = ctx.enter_context(nc.semaphore("ffn_w_in"))

        setup_phase(nc, t, sh)
        with ExitStack() as experts:
            w1 = sb("expert_w1", [128, G, E, F], scope=experts)
            w2a = sb("expert_w2a", [128, W2A, E, C], scope=experts)

            def load_experts(sp, par, pair):
                half = W2A // 2
                sp.dma_start(w1[:, par, pair, :], t["e_w1"][pair, par * 128:(par + 1) * 128, :]).then_inc(w1_in, 16)
                sp.dma_start(w2a[:, par * half:(par + 1) * half, pair, :],
                             t["e_w2"][pair, par * half * 128:(par + 1) * half * 128, :]
                             .rearrange("(f p) n -> p f n", p=128)).then_inc(w1_in, 16)

            attention_phase(nc, sh, t["ctx"], 0, load_experts, lambda sp: None)
            experts_phase(nc, t, sh, w1, w2a, w1_in)

        f_w1 = sb("ffn_w1", [128, G, F])
        f_w2 = sb("ffn_w2", [128, FT, C])
        f_b2 = sb("ffn_b2", [S, C])

        def load_ffn(sp):
            sp.dma_start(f_w1[:], t["f_w1"].rearrange("(g p) n -> p g n", p=128)).then_inc(ffn_in, 16)
            sp.dma_start(f_w2[:], t["f_w2"].rearrange("(f p) n -> p f n", p=128)).then_inc(ffn_in, 16)
            sp.dma_start(f_b2[:], t["f_b2"].partition_broadcast(S)).then_inc(ffn_in, 16)

        attention_phase(nc, sh, t["ctx"], 1, lambda sp, par, pair: None, load_ffn)
        fixed_point_phase(nc, sh, f_w1, f_w2, f_b2, ffn_in, out_dram)


_INS = {"x": "x", "ctx_768": "ctx", "mask_BxS_bk0": "mask", "g_xattn": "g_xattn", "g_ffn": "g_ffn",
        "L0_xattn_Wq": "Wq", "L0_xattn_Wkv": "Wkv",
        "L0_ffn_gate_w": "gate_w", "L0_ffn_w1": "e_w1", "L0_ffn_b1": "e_b1", "L0_ffn_w2": "e_w2", "L0_ffn_b2": "e_b2",
        "L1_xattn_w_q": "w_q", "L1_xattn_b_q": "b_q", "L1_xattn_w_k": "w_k", "L1_xattn_b_k": "b_k",
        "L1_xattn_w_v": "w_v", "L1_xattn_b_v": "b_v", "L1_xattn_w_o": "w_o", "L1_xattn_b_o": "b_o",
        "L1_ffn_w1": "f_w1", "L1_ffn_b1": "f_b1", "L1_ffn_w2": "f_w2", "L1_ffn_b2": "f_b2"}


def kernel(**inputs):
    import numpy as _np
    import concourse.bacc as _bacc
    from concourse import mybir as _mybir
    from concourse.bass_utils import run_bass_kernel_spmd as _run

    nc = _bacc.Bacc("TRN2", target_bir_lowering=False, num_devices=1)
    arrays, tensors = {}, {}
    for name, short in _INS.items():
        a = _np.ascontiguousarray(inputs[name])
        arrays[f"in_{short}"] = a
        tensors[short] = nc.dram_tensor(f"in_{short}", a.shape, _mybir.dt.from_np(a.dtype), kind="ExternalInput").ap()
    out = nc.dram_tensor("out_x", (B, S, C), F32, kind="ExternalOutput").ap()
    flamingo_kernel(nc, tensors, out)
    r = _run(nc, [arrays], core_ids=[0])
    return r.results[0]["out_x"]
```

```python
from contextlib import ExitStack

import concourse.bass as bass
from concourse import mybir

F32 = mybir.dt.float32
BF16 = mybir.dt.bfloat16
U8 = mybir.dt.uint8
U32 = mybir.dt.uint32
ALU = mybir.AluOpType
ACT = mybir.ActivationFunctionType
AX = mybir.AxisListType

B, S, C = 16, 100, 256
SC, CC = 361, 192
NH, D = 16, 16
G = C // 128
HG = NH // G
SCALE = D ** -0.5
EPS = 1e-5
KEYS = (120, 120, 121)
KSTEP = 120
HI, LO = 128, CC - 128
Q_PART = (1, 2, 3, 1, 2, 1)
K_PART = (1, 1, 1, 2, 2, 3)
SLOTS = len(Q_PART)
SROWS = SLOTS * D
MROWS = SROWS + 3
SW = S + SC
ROW_BANKS, ST_BANKS, P_BUFS = 2, 3, 2
CHUNK = 4
CHUNKS = NH // CHUNK
VW = 32
E, F, TOP = 8, 1024, 2
FT = F // 128
W2A = 4
FIX = 256.0
ROUND = 1.5 * 2.0 ** 23
SEG = 64.0
LIM = 4.0 * FIX
QUAD = 4


class Shared:
    pass


def setup_phase(nc, t, sh):
    with ExitStack() as ctx:
        def sb(name, shape, dt=F32):
            return ctx.enter_context(nc.sbuf_tensor(name, shape, dt))

        def sem(name):
            return ctx.enter_context(nc.semaphore(name))

        wq_rows = sb("wq_rows", [128, G, C])
        wkv_rows = sb("wkv_rows", [128, 2 * G, CC])
        mask_u8 = sb("mask_u8", [B, S], U8)
        mask_f = sb("mask_f", [B, S])
        gates = sb("gates", [128, 4])
        eb1_rows = sb("eb1_rows", [E * FT, 128])
        fb1_rows = sb("fb1_rows", [FT, 128])
        stats = sb("stats0", [S, B, 6])
        ps = ctx.enter_context(nc.psum_tensor("ps_setup", [128, 4, 512], F32))

        loaded = sem("small_loaded")
        x_loaded = sem("x_loaded")
        ident_made = sem("ident_made")
        mask_cast = sem("mask_cast")
        turned = sem("turned")
        stats_done = sem("stats_done")
        evacuated = sem("setup_evacuated")
        gates_done = sem("gates_done")

        with nc.Block() as block:
            @block.sync
            def _(sp):
                sp.dma_start(wq_rows[:], t["Wq"].rearrange("(g p) c -> p g c", p=128)).then_inc(loaded, 16)
                sp.dma_start(wkv_rows[:], t["Wkv"].rearrange("(g p) c -> p g c", p=128)).then_inc(loaded, 16)
                sp.dma_start(mask_u8[:], t["mask"]).then_inc(loaded, 16)
                sp.dma_start(gates[:, 0:2], t["g_xattn"].partition_broadcast(128)).then_inc(loaded, 16)
                sp.dma_start(gates[:, 2:4], t["g_ffn"].partition_broadcast(128)).then_inc(loaded, 16)
                sp.dma_start(eb1_rows[:], t["e_b1"].rearrange("e (f p) -> (e f) p", p=128)).then_inc(loaded, 16)
                sp.dma_start(fb1_rows[:], t["f_b1"].rearrange("(f p) -> f p", p=128)).then_inc(loaded, 16)
                for tile, w in ((sh.wk1, t["w_k"]), (sh.wv1, t["w_v"])):
                    sp.dma_start(tile[0:HI, 0, :], w[0:HI, :]).then_inc(sh.later, 16)
                    sp.dma_start(tile[0:LO, 1, :], w[HI:CC, :]).then_inc(sh.later, 16)
                sp.dma_start(sh.wk1[LO:LO + 1, 1, :], t["b_k"].unsqueeze(0)).then_inc(sh.later, 16)
                sp.dma_start(sh.wv1[LO:LO + 1, 1, :], t["b_v"].unsqueeze(0)).then_inc(sh.later, 16)
                sp.dma_start(sh.wq1[:], t["w_q"].rearrange("(g p) c -> p g c", p=128)).then_inc(sh.later, 16)
                sp.dma_start(sh.wo1[:], t["w_o"].rearrange("(g p) c -> p g c", p=128)).then_inc(sh.later, 16)
                sp.dma_start(sh.bq1[:], t["b_q"].rearrange("(g p) -> p g", p=128),
                             allow_slow_non_contiguous=True).then_inc(sh.later, 16)
                sp.dma_start(sh.bo1[:], t["b_o"].partition_broadcast(S)).then_inc(sh.later, 16)
                sp.wait_ge(loaded, 7 * 16)
                sp.wait_ge(sh.later, 10 * 16)

            @block.gpsimd
            def _(pool):
                pool.memset(sh.ident[:], 0.0).then_inc(ident_made, 1)
                pool.memset(sh.identb[:], 0.0).then_inc(ident_made, 1)
                pool.wait_ge(ident_made, 2)
                for m in (sh.ident, sh.identb):
                    pool.affine_select(out=m[:], in_=m[:], compare_op=ALU.not_equal, fill=1.0, base=0,
                                       pattern=[[-1, 128]], channel_multiplier=1).then_inc(ident_made, 1)

            @block.scalar
            def _(act):
                act.dma_start(sh.x[:], t["x"].rearrange("b s c -> s b c")).then_inc(x_loaded, 16)
                act.wait_ge(loaded, 7 * 16)
                act.activation(sh.tg[:], gates[:], ACT.Tanh).then_inc(gates_done, 1)
                act.wait_ge(turned, 4)
                act.activation(sh.wq0[:].rearrange("p c (o n) -> p c o n", o=G),
                               ps[:, 0, :].rearrange("p (c o n) -> p c o n", c=G, o=G), ACT.Copy)\
                    .then_inc(evacuated, 1)
                act.wait_ge(turned, 4 + 8)
                for n, w in ((0, sh.wk0), (1, sh.wv0)):
                    act.activation(w[0:HI, 0, :], ps[0:HI, 1, n * C:(n + 1) * C], ACT.Copy).then_inc(evacuated, 1)
                    act.activation(w[0:LO, 1, :], ps[0:LO, 2, n * C:(n + 1) * C], ACT.Copy).then_inc(evacuated, 1)

            @block.tensor
            def _(pe):
                pe.wait_ge(loaded, 7 * 16)
                pe.wait_ge(ident_made, 4)
                for c in range(G):
                    for o in range(G):
                        pe.transpose(ps[:, 0, (c * G + o) * 128:(c * G + o + 1) * 128],
                                     wq_rows[:, o, c * 128:(c + 1) * 128], sh.ident[:]).then_inc(turned, 1)
                for n in range(2 * G):
                    pe.transpose(ps[0:HI, 1, n * 128:(n + 1) * 128], wkv_rows[:, n, 0:HI], sh.ident[:])\
                        .then_inc(turned, 1)
                    pe.transpose(ps[0:LO, 2, n * 128:(n + 1) * 128], wkv_rows[:, n, HI:CC], sh.ident[:])\
                        .then_inc(turned, 1)
                pe.wait_ge(mask_cast, 1)
                pe.transpose(ps[0:S, 3, 0:B], mask_f[:], sh.ident[0:B, 0:B]).then_inc(turned, 1)
                pe.transpose(ps[:, 3, 64:64 + E * FT], eb1_rows[:], sh.ident[0:E * FT, 0:E * FT]).then_inc(turned, 1)
                pe.transpose(ps[:, 3, 192:192 + FT], fb1_rows[:], sh.ident[0:FT, 0:FT]).then_inc(turned, 1)

            @block.vector
            def _(dve):
                dve.wait_ge(loaded, 7 * 16)
                dve.tensor_copy(mask_f[:], mask_u8[:]).then_inc(mask_cast, 1)
                dve.memset(sh.ones[:], 1.0)
                dve.memset(sh.wk0[LO:LO + 1, 1, :], 0.0)
                dve.memset(sh.wv0[LO:LO + 1, 1, :], 0.0)
                dve.memset(sh.gelu_bias[:, 0:1], -ROUND * SEG / FIX)
                dve.memset(sh.gelu_bias[:, 1:2], -ROUND * SEG / FIX + SEG / FIX)
                dve.wait_ge(x_loaded, 16)
                for b in range(B):
                    dve.bn_stats(stats[:, b, :], sh.x[:, b, :]).then_inc(stats_done, 1)
                for b in range(B):
                    dve.wait_ge(stats_done, b + 1)
                    dve.bn_aggr(sh.mv[:, b, :], stats[:, b, :])
                dve.wait_ge(turned, 4 + 8 + 3)
                dve.tensor_copy(sh.keep[:], ps[0:S, 3, 0:B])
                dve.tensor_copy(sh.eb1[:].rearrange("p e f -> p (e f)"), ps[:, 3, 64:64 + E * FT])
                dve.tensor_scalar(sh.fb1[:], ps[:, 3, 192:192 + FT], FIX, None, ALU.mult)


def rstd_steps(nc, sh, ctx, name):
    ready = ctx.enter_context(nc.semaphore(f"{name}_var_eps"))
    rooted = ctx.enter_context(nc.semaphore(f"{name}_rooted"))
    inverted = ctx.enter_context(nc.semaphore(f"{name}_rstd"))

    def on_vector(dve):
        dve.tensor_scalar(sh.rstd[:], sh.mv[:, :, 1], EPS, None, ALU.add).then_inc(ready, 1)
        dve.wait_ge(rooted, 1)
        dve.reciprocal(sh.rstd[:], sh.rstd[:]).then_inc(inverted, 1)
        dve.wait_ge(inverted, 1)

    def on_scalar(act):
        act.wait_ge(ready, 1)
        act.activation(sh.rstd[:], sh.rstd[:], ACT.Sqrt).then_inc(rooted, 1)

    return on_vector, on_scalar


def attention_phase(nc, sh, ctx_dram, layer, extra_loads, extra_start):
    first_layer = layer == 0
    wq, wk, wv = (sh.wq0, sh.wk0, sh.wv0) if first_layer else (sh.wq1, sh.wk1, sh.wv1)
    with ExitStack() as ctx:
        def sb(name, shape, dt=F32):
            return ctx.enter_context(nc.sbuf_tensor(f"{name}_{layer}", shape, dt))

        def psum(name, shape):
            return ctx.enter_context(nc.psum_tensor(f"{name}_{layer}", shape, F32))

        def sem(name):
            return ctx.enter_context(nc.semaphore(f"{name}_{layer}"))

        context = sb("context", [128, 2, 3, CC])
        ctxT = sb("ctxT", [128, 2, SC])
        xn = sb("xn", [S, C])
        xnT = sb("xnT", [128, G, S])
        qf = sb("qf", [128, G, S])
        qrest = sb("qrest", [128, G, S])
        krest = sb("krest", [128, G, SC])
        parts = sb("parts", [128, SLOTS, G, SW], BF16)
        stack = [sb(f"stack{p}", [MROWS, NH, SW], BF16) for p in range(2)]
        v = [sb(f"v{p}", [128, 3, NH, VW]) for p in range(2)]
        probs = [sb(f"probs{p}", [128, 3, CHUNK * S]) for p in range(P_BUFS)]
        rowmax = sb("rowmax", [S, NH])
        mrest = sb("mrest", [S, NH])
        mparts = sb("mparts", [S, 3, NH], BF16)
        mT = sb("mT", [3 * NH, S], BF16)
        oT4 = sb("oT4", [128, CHUNKS * S])
        rden = sb("rden", [S, NH])
        o = sb("o", [S, C])
        stats = sb("stats", [S, 6])
        mv_now = sb("mv_now", [S, 2])
        if not first_layer:
            oT = sb("oT", [128, G, S])
            biased = sb("biased", [S, C])
        scaled = sb("scaled", [S, B])

        rows_ps = psum("rows_ps", [128, ROW_BANKS, 512])
        a_ps = psum("a_ps", [128, 2, 512])
        st_ps = psum("st_ps", [128, ST_BANKS, 512])
        o_ps = psum("o_ps", [128, 512])

        ctx_in = [sem(f"context_loaded{p}") for p in range(2)]
        tick = sem("tick")
        stack_preset = sem("stack_preset")
        presets = sem("presets")
        v_cleared = sem("v_cleared")
        scaled_ready = sem("scaled_ready")
        xn_made = sem("xn_made")
        xnT_ps = sem("xnT_ps")
        xnT_made = sem("xnT_made")
        cT_ps = sem("cT_ps")
        cT_made = sem("cT_made")
        q_ps = sem("q_ps")
        qf_made = sem("qf_made")
        q_cut = sem("q_cut")
        q_repeated = sem("q_repeated")
        k_ps = sem("k_ps")
        k1_made = sem("k1_made")
        krest_made = sem("krest_made")
        k1_repeated = sem("k1_repeated")
        k2_made = sem("k2_made")
        k3_made = sem("k3_made")
        v_ps = sem("v_ps")
        v_made = sem("v_made")
        stacked = [[sem(f"stacked{p}_{half}") for half in range(2)] for p in range(2)]
        m_in = [sem(f"max_rows_in{p}") for p in range(2)]
        rows_made = sem("rows_made")
        rows_free = sem("rows_free")
        m_steps = sem("m_steps")
        mT_ps = sem("mT_ps")
        mT_made = sem("mT_made")
        st_made = sem("st_made")
        exp_done = sem("exp_done")
        pv_done = sem("pv_done")
        oT4_made = sem("oT4_made")
        o_turned = sem("o_turned")
        rden_made = sem("rden_made")
        o_made = sem("o_made")
        x_steps = sem("x_steps")
        stats_made = sem("stats_made")
        oT_ps = sem("oT_ps")
        oT_made = sem("oT_made")
        out_ps = sem("out_ps")
        out_read = sem("out_read")

        rstd_vector, rstd_scalar = rstd_steps(nc, sh, ctx, f"att{layer}")
        EXP = 3 * CHUNKS
        HALF = 16 * HG // 2

        ORDER = [g * HG + hh for hh in range(HG) for g in range(G)]

        def run(step, eng):
            step(0, 0, 0, True, True, False, False)
            step(1, 1, 0, True, True, True, False)
            with eng.Fori(1, B // 2 - 1) as pair:
                for par in range(2):
                    step(2 * pair + par, par, pair, True, True, True, True)
            step(B - 2, 0, B // 2 - 1, True, True, True, True)
            step(B - 1, 1, B // 2 - 1, False, True, True, True)
            step(B, 0, B // 2, False, False, True, True)
            step(B + 1, 1, B // 2, False, False, False, True)

        with nc.Block() as block:
            @block.sync
            def _(sp):
                def load_context(b, par):
                    sp.dma_start(context[0:KSTEP, par, :, :],
                                 ctx_dram[b, 0:3 * KSTEP, :].rearrange("(t p) c -> p t c", p=KSTEP))\
                        .then_inc(ctx_in[par], 16)
                    sp.dma_start(context[KSTEP:KSTEP + 1, par, 2, :], ctx_dram[b, 3 * KSTEP:SC, :])\
                        .then_inc(ctx_in[par], 16)

                def fill_stack(n, par, half, scores_before):
                    sp.wait_ge(st_made, scores_before)
                    sp.sem_inc(tick, 1)
                    for hh in range(half * HG // 2, (half + 1) * HG // 2):
                        sp.dma_start(
                            stack[par][0:SROWS, hh:NH:HG, :],
                            parts[hh * D:(hh + 1) * D, :, :, :]).then_inc(stacked[par][half], 16)

                def parts_ready(n):
                    for part, times in ((q_cut, 4), (q_repeated, 2), (k1_repeated, 1), (k2_made, 1), (k3_made, 1)):
                        sp.wait_ge(part, times * (n + 1))
                        sp.sem_inc(tick, 1)

                load_context(0, 0)
                load_context(1, 1)
                extra_start(sp)
                parts_ready(0)
                for half in range(2):
                    fill_stack(0, 0, half, 0)

                def step(b, par, pair, project, rows, attend, finish):
                    if project and pair is not B // 2 - 1:
                        sp.wait_ge(cT_made, 2 * (b + 1))
                        sp.sem_inc(tick, 1)
                        load_context(b + 2, par)
                    if attend:
                        sp.wait_ge(m_in[1 - par], 16 * (pair + par))
                        sp.sem_inc(tick, 1)
                    if rows:
                        extra_loads(sp, par, pair)
                    if project:
                        parts_ready(b + 1)
                        for half in range(2):
                            before = EXP * (b - 1) + (half + 1) * EXP // 2 if attend else 0
                            fill_stack(b + 1, 1 - par, half, before)

                run(step, sp)

            @block.gpsimd
            def _(pool):
                for p in range(2):
                    pool.memset(stack[p][SROWS:MROWS, :, S:SW], 1.0).then_inc(stack_preset, 1)
                pool.wait_ge(stack_preset, 2)

                def cut(n):
                    pool.wait_ge(q_cut, 4 * n + 3)
                    pool.sem_inc(tick, 1)
                    pool.tensor_copy(parts[:, 3:6:2, :, 0:S], parts[:, 0, :, 0:S].unsqueeze(1)
                                     .to_broadcast([128, 2, G, S])).then_inc(q_repeated, 1)
                    pool.tensor_copy(parts[:, 4, :, 0:S], parts[:, 1, :, 0:S]).then_inc(q_repeated, 1)
                    pool.wait_ge(k1_made, n + 1)
                    pool.sem_inc(tick, 1)
                    pool.tensor_copy(parts[:, 1:3, :, S:SW], parts[:, 0, :, S:SW].unsqueeze(1)
                                     .to_broadcast([128, 2, G, SC])).then_inc(k1_repeated, 1)
                    pool.wait_ge(k2_made, n + 1)
                    pool.sem_inc(tick, 1)
                    pool.tensor_tensor(parts[:, 5, :, S:SW], krest[:], parts[:, 3, :, S:SW], ALU.subtract)\
                        .then_inc(k3_made, 1)

                cut(0)

                def step(b, par, pair, project, rows, attend, finish):
                    if project:
                        cut(b + 1)
                run(step, pool)

            @block.scalar
            def _(act):
                rstd_scalar(act)

                def read_v(n, par):
                    for kt, rows in enumerate(KEYS):
                        act.wait_ge(v_ps, 3 * n + kt + 1)
                        act.activation(v[par][0:rows, kt, :, 0:D],
                                       a_ps[0:rows, kt % 2, 0:C].rearrange("p (h d) -> p h d", d=D), ACT.Copy)\
                            .then_inc(v_made, 1)

                def read_turned(n):
                    act.wait_ge(xnT_ps, n + 1)
                    act.activation(xnT[:].rearrange("p g s -> p (g s)"), a_ps[:, 0, 0:G * S], ACT.Copy)\
                        .then_inc(xnT_made, 1)
                    act.wait_ge(cT_ps, 2 * n + 1)
                    act.activation(ctxT[:, 0, :], a_ps[:, 1, 0:SC], ACT.Copy).then_inc(cT_made, 1)
                    act.wait_ge(cT_ps, 2 * n + 2)
                    act.activation(ctxT[0:LO, 1, :], a_ps[0:LO, 0, 0:SC], ACT.Copy).then_inc(cT_made, 1)

                def first_k(n):
                    act.wait_ge(k_ps, 2 * (n + 1))
                    act.activation(parts[:, 0, :, S:SW], a_ps[:, :, 0:SC], ACT.Copy).then_inc(k1_made, 1)

                def second_k(n):
                    act.wait_ge(krest_made, n + 1)
                    act.activation(parts[:, 3:5, :, S:SW], krest[:].unsqueeze(1).to_broadcast([128, 2, G, SC]),
                                   ACT.Copy).then_inc(k2_made, 1)

                def exponentials(n, c):
                    act.wait_ge(pv_done, CHUNKS * n + c + 1)
                    for kt, rows in enumerate(KEYS):
                        act.wait_ge(st_made, EXP * n + 3 * c + kt + 1)
                        act.activation(probs[c % P_BUFS][0:rows, kt, :], st_ps[0:rows, kt, 0:CHUNK * S],
                                       ACT.Exp, scale=SCALE).then_inc(exp_done, 1)

                act.wait_ge(presets, 3)
                read_turned(0)
                first_k(0)
                second_k(0)
                act.sem_inc(exp_done, ST_BANKS)

                def step(b, par, pair, project, rows, attend, finish):
                    if rows:
                        if finish:
                            act.wait_ge(pv_done, P_BUFS + CHUNKS * (b - 1))
                        read_v(b, par)
                    if attend:
                        act.wait_ge(mT_ps, b)
                        act.activation(mT[:], a_ps[0:3 * NH, 1, :].bitcast(BF16)[:, 0:S], ACT.Copy)\
                            .then_inc(mT_made, 1)
                        act.wait_ge(mT_made, b)
                        act.dma_start(stack[1 - par][SROWS:MROWS, :, 0:S], mT[:]).then_inc(m_in[1 - par], 16)
                    if project:
                        read_turned(b + 1)
                        for half in range(2):
                            act.wait_ge(stacked[par][half], HALF * (pair + 1))
                        act.sem_inc(tick, 1)
                        first_k(b + 1)
                    for c in range(CHUNKS):
                        if attend:
                            exponentials(b - 1, c)
                        if project and c == 0:
                            second_k(b + 1)
                    if finish and not first_layer:
                        act.wait_ge(oT_ps, b - 1)
                        act.activation(oT[:].rearrange("p g s -> p (g s)"), a_ps[:, 1, 0:G * S], ACT.Copy)\
                            .then_inc(oT_made, 1)

                run(step, act)

            @block.tensor
            def _(pe):
                def project_v(n, kt):
                    rows = KEYS[kt]
                    if kt == 2:
                        pe.wait_ge(v_made, 3 * n + 1)
                    keys = slice(kt * KSTEP, kt * KSTEP + rows)
                    pe.matmul(a_ps[0:rows, kt % 2, 0:C], ctxT[:, 0, keys], wv[:, 0, :], start=True, stop=False)
                    pe.matmul(a_ps[0:rows, kt % 2, 0:C], ctxT[0:LO + 1, 1, keys], wv[0:LO + 1, 1, :],
                              start=False, stop=True).then_inc(v_ps, 1)

                def turn_max(n):
                    pe.wait_ge(m_steps, 4 * (n + 1))
                    pe.sem_inc(tick, 1)
                    pe.transpose(a_ps[0:3 * NH, 1, :].bitcast(BF16)[:, 0:S], mparts[:].rearrange("p j h -> p (j h)"),
                                 sh.identb[0:S, 0:S]).then_inc(mT_ps, 1)

                def turn_xn(n):
                    pe.wait_ge(xn_made, n + 1)
                    for g in range(G):
                        last = pe.transpose(a_ps[:, 0, g * S:(g + 1) * S], xn[:, g * 128:(g + 1) * 128],
                                            sh.ident[0:S, 0:S])
                    last.then_inc(xnT_ps, 1)

                def turn_context_hi(n, par, pair):
                    pe.wait_ge(ctx_in[par], 32 * (pair + 1))
                    pe.sem_inc(tick, 1)
                    for kt, rows in enumerate(KEYS):
                        last = pe.transpose(a_ps[:, 1, kt * KSTEP:kt * KSTEP + rows], context[0:rows, par, kt, 0:HI],
                                            sh.ident[0:rows, 0:rows])
                    last.then_inc(cT_ps, 1)

                def turn_context_lo(n, par):
                    pe.wait_ge(xnT_made, n + 1)
                    pe.sem_inc(tick, 1)
                    for kt, rows in enumerate(KEYS):
                        last = pe.transpose(a_ps[0:LO, 0, kt * KSTEP:kt * KSTEP + rows],
                                            context[0:rows, par, kt, HI:CC], sh.ident[0:rows, 0:rows])
                    last.then_inc(cT_ps, 1)

                def project_q(n):
                    pe.wait_ge(cT_made, 2 * n + 1)
                    for g in range(G):
                        for c in range(G):
                            last = pe.matmul(a_ps[:, 1, g * S:(g + 1) * S], wq[:, c, g * 128:(g + 1) * 128],
                                             xnT[:, c, :], start=(c == 0), stop=(c == G - 1))
                    last.then_inc(q_ps, 1)

                def project_k(n, g):
                    if g == 0:
                        pe.wait_ge(cT_made, 2 * n + 2)
                    else:
                        pe.wait_ge(qf_made, n + 1)
                    pe.matmul(a_ps[:, g, 0:SC], wk[:, 0, g * 128:(g + 1) * 128], ctxT[:, 0, :],
                              start=True, stop=False)
                    pe.matmul(a_ps[:, g, 0:SC], wk[0:LO + 1, 1, g * 128:(g + 1) * 128], ctxT[0:LO + 1, 1, :],
                              start=False, stop=True).then_inc(k_ps, 1)

                def turn_sums(n):
                    pe.wait_ge(oT4_made, n + 1)
                    for c in range(CHUNKS):
                        last = pe.transpose(a_ps[0:S, 0, c * 128:(c + 1) * 128], oT4[:, c * S:(c + 1) * S],
                                            sh.ident[:])
                    last.then_inc(o_turned, 1)

                def turn_o(n):
                    pe.wait_ge(o_made, n + 1)
                    for g in range(G):
                        last = pe.transpose(a_ps[:, 1, g * S:(g + 1) * S], o[:, g * 128:(g + 1) * 128],
                                            sh.ident[0:S, 0:S])
                    last.then_inc(oT_ps, 1)

                def project_out(n):
                    pe.wait_ge(oT_made, n + 1)
                    for c in range(G):
                        last = pe.matmul(a_ps[0:S, 1, 0:C], oT[:, c, :], sh.wo1[:, c, :],
                                         start=(c == 0), stop=(c == G - 1))
                    last.then_inc(out_ps, 1)

                def row_scores(n, par, i):
                    pe.wait_ge(rows_free, NH * n + i + 1)
                    pe.matmul(rows_ps[0:S, i % ROW_BANKS, 0:SC], stack[par][0:SROWS, ORDER[i], 0:S],
                              stack[par][0:SROWS, ORDER[i], S:SW], start=True, stop=True).then_inc(rows_made, 1)

                def scores_T(n, par, c):
                    for kt, rows in enumerate(KEYS):
                        pe.wait_ge(exp_done, EXP * n + 3 * c + kt + 1)
                        for j in range(CHUNK):
                            h = ORDER[c * CHUNK + j]
                            last = pe.matmul(st_ps[0:rows, kt, j * S:(j + 1) * S],
                                             stack[par][:, h, S + kt * KSTEP:S + kt * KSTEP + rows],
                                             stack[par][:, h, 0:S], start=True, stop=True)
                        last.then_inc(st_made, 1)

                def weighted_sums(n, par, c):
                    if c == 0:
                        pe.wait_ge(oT4_made, n)
                        pe.wait_ge(v_made, 3 * (n + 1))
                    for kt, rows in enumerate(KEYS):
                        pe.wait_ge(exp_done, ST_BANKS + EXP * n + 3 * c + kt + 1)
                        for j in range(CHUNK):
                            last = pe.matmul(o_ps[j * VW:(j + 1) * VW, c * S:(c + 1) * S],
                                             v[par][0:rows, kt, ORDER[c * CHUNK + j], :],
                                             probs[c % P_BUFS][0:rows, kt, j * S:(j + 1) * S],
                                             start=(kt == 0), stop=(kt == 2))
                    last.then_inc(pv_done, 1)

                pe.wait_ge(presets, 3)
                pe.wait_ge(stack_preset, 2)
                turn_xn(0)
                turn_context_hi(0, 0, 0)
                turn_context_lo(0, 0)
                project_q(0)
                project_k(0, 0)
                project_k(0, 1)
                pe.sem_inc(pv_done, P_BUFS)

                def step(b, par, pair, project, rows, attend, finish):
                    n, n_par, n_pair = b + 1, 1 - par, pair + par
                    m = b - 1
                    f = b - 2

                    def row_group(first, last):
                        if rows:
                            for i in range(first, last):
                                if i % (NH // 2) == 0:
                                    pe.wait_ge(stacked[par][i // (NH // 2)], HALF * (pair + 1))
                                row_scores(b, par, i)

                    if rows:
                        pe.wait_ge(krest_made, b + 1)
                        if b is not 0 and (finish or b is not 1):
                            if finish:
                                pe.wait_ge(o_made, b - 2)
                                if not first_layer:
                                    pe.wait_ge(out_read, b - 2)
                        project_v(b, 0)
                        project_v(b, 1)
                        project_v(b, 2)
                    if attend:
                        if rows:
                            pe.wait_ge(v_made, 3 * b + 2)
                        elif not first_layer:
                            pe.wait_ge(out_read, b - 2)
                        turn_max(m)
                    if project:
                        pe.wait_ge(v_made, 3 * (b + 1))
                        turn_xn(n)
                    row_group(0, 2)
                    if project:
                        if attend:
                            pe.wait_ge(mT_made, b)
                        turn_context_hi(n, n_par, n_pair)
                        turn_context_lo(n, n_par)
                    row_group(2, 3)
                    if project:
                        project_q(n)
                        project_k(n, 0)
                    row_group(3, 4)
                    if project:
                        project_k(n, 1)
                    if attend:
                        pe.wait_ge(m_in[1 - par], 16 * (pair + par))
                        scores_T(m, 1 - par, 0)
                    row_group(4, 6)
                    if attend:
                        scores_T(m, 1 - par, 1)
                        weighted_sums(m, 1 - par, 0)
                    row_group(6, 8)
                    if attend:
                        scores_T(m, 1 - par, 2)
                        weighted_sums(m, 1 - par, 1)
                    row_group(8, 10)
                    if finish:
                        if project:
                            pe.wait_ge(krest_made, b + 2)
                        elif rows:
                            pe.wait_ge(v_made, 3 * B)
                        elif attend:
                            pe.wait_ge(o_made, b - 2)
                        if attend:
                            pe.wait_ge(mT_made, b)
                        turn_sums(f)
                    row_group(10, 11)
                    if attend:
                        scores_T(m, 1 - par, 3)
                        weighted_sums(m, 1 - par, 2)
                    row_group(11, 13)
                    if finish and not first_layer:
                        turn_o(f)
                    row_group(13, 14)
                    if attend:
                        weighted_sums(m, 1 - par, 3)
                    if finish and not first_layer:
                        project_out(f)
                    row_group(14, 16)

                run(step, pe)

            @block.vector
            def _(dve):
                rstd_vector(dve)
                if first_layer:
                    dve.tensor_tensor(scaled[:], sh.rstd[:], sh.keep[:], ALU.mult).then_inc(scaled_ready, 1)
                else:
                    dve.tensor_copy(scaled[:], sh.rstd[:]).then_inc(scaled_ready, 1)
                dve.wait_ge(scaled_ready, 1)

                def normalise(n):
                    dve.wait_ge(xnT_ps, n)
                    dve.tensor_scalar(xn[:], sh.x[:, n, :], sh.mv[:, n, 0:1], scaled[:, bass.ds(n, 1)],
                                      ALU.subtract, ALU.mult).then_inc(xn_made, 1)

                normalise(0)
                dve.memset(ctxT[LO:LO + 1, 1, :], 1.0).then_inc(presets, 1)
                for p in range(2):
                    dve.memset(v[p][:], 0.0).then_inc(v_cleared, 1)
                dve.wait_ge(v_cleared, 2)
                for p in range(2):
                    dve.memset(v[p][:, :, :, D:D + 1], 1.0).then_inc(presets, 1)
                dve.sem_inc(rows_free, ROW_BANKS)

                def cut_q(n):
                    dve.wait_ge(q_ps, n + 1)
                    if first_layer:
                        dve.tensor_copy(qf[:].rearrange("p g s -> p (g s)"), a_ps[:, 1, 0:G * S])\
                            .then_inc(qf_made, 1)
                    else:
                        dve.tensor_tensor(qf[:], a_ps[:, 1, 0:G * S].rearrange("p (g s) -> p g s", g=G),
                                          sh.bq1[:].unsqueeze(2).to_broadcast([128, G, S]), ALU.add)\
                            .then_inc(qf_made, 1)
                    q1, q2, q3 = (parts[:, slot, :, 0:S] for slot in range(3))
                    dve.wait_ge(qf_made, n + 1)
                    dve.sem_inc(tick, 1)
                    dve.tensor_copy(q1, qf[:]).then_inc(q_cut, 1)
                    dve.wait_ge(q_cut, 4 * n + 1)
                    dve.tensor_tensor(qrest[:], qf[:], q1, ALU.subtract).then_inc(q_cut, 1)
                    dve.wait_ge(q_cut, 4 * n + 2)
                    dve.sem_inc(tick, 1)
                    dve.tensor_copy(q2, qrest[:]).then_inc(q_cut, 1)
                    dve.wait_ge(q_cut, 4 * n + 3)
                    dve.tensor_tensor(q3, qrest[:], q2, ALU.subtract).then_inc(q_cut, 1)

                def rest_of_k(n):
                    dve.wait_ge(k1_made, n + 1)
                    dve.wait_ge(k3_made, n)
                    dve.tensor_tensor(krest[:], a_ps[:, :, 0:SC], parts[:, 0, :, S:SW], ALU.subtract)\
                        .then_inc(krest_made, 1)

                def read_sums(n):
                    dve.wait_ge(pv_done, P_BUFS + CHUNKS * (n + 1))
                    dve.wait_ge(o_turned, n)
                    dve.sem_inc(tick, 1)
                    dve.tensor_copy(oT4[:], o_ps[:, 0:CHUNKS * S]).then_inc(oT4_made, 1)

                def normalise_sums(n):
                    dve.wait_ge(o_turned, n + 1)
                    per_head = a_ps[0:S, 0, :].rearrange("p (h w) -> p h w", w=VW)
                    dve.reciprocal(rden[:], per_head[:, :, D]).then_inc(rden_made, 1)
                    dve.wait_ge(rden_made, n + 1)
                    dve.tensor_tensor(o[:].rearrange("p (g hh d) -> p hh g d", g=G, d=D),
                                      per_head[:, :, 0:D].rearrange("p (hh g) d -> p hh g d", g=G),
                                      rden[:].rearrange("p (hh g) -> p hh g", g=G).unsqueeze(3)
                                      .to_broadcast([S, HG, G, D]), ALU.mult).then_inc(o_made, 1)
                    dve.wait_ge(o_made, n + 1)

                def add_to_x(n):
                    steps = 3 * n
                    if not first_layer:
                        dve.wait_ge(out_ps, n + 1)
                        dve.tensor_tensor(biased[:], a_ps[0:S, 1, 0:C], sh.bo1[:], ALU.add).then_inc(out_read, 1)
                        dve.wait_ge(out_read, n + 1)
                    source = o if first_layer else biased
                    dve.scalar_tensor_tensor(out=sh.x[:, n, :], in0=source[:], scalar=sh.tg[0:S, layer:layer + 1],
                                             in1=sh.x[:, n, :], op0=ALU.mult, op1=ALU.add).then_inc(x_steps, 1)
                    dve.wait_ge(x_steps, steps + 1)
                    dve.sem_inc(tick, 1)
                    dve.bn_stats(stats[:], sh.x[:, n, :]).then_inc(x_steps, 1)
                    dve.wait_ge(x_steps, steps + 2)
                    dve.sem_inc(tick, 1)
                    dve.bn_aggr(mv_now[:], stats[:]).then_inc(x_steps, 1)
                    dve.wait_ge(x_steps, steps + 3)
                    dve.tensor_scalar(sh.mv[:, n, :], mv_now[:], 1.0, None, ALU.mult).then_inc(stats_made, 1)

                def row_max(n, i):
                    dve.wait_ge(rows_made, NH * n + i + 1)
                    if i == 0:
                        dve.wait_ge(m_steps, 4 * n)
                    h = ORDER[i]
                    dve.tensor_reduce(rowmax[:, h:h + 1], rows_ps[0:S, i % ROW_BANKS, 0:SC], AX.X, ALU.max)\
                        .then_inc(rows_free, 1)

                def cut_max(n):
                    steps = 4 * n
                    dve.wait_ge(rows_free, ROW_BANKS + NH * (n + 1))
                    dve.wait_ge(mT_ps, n)
                    dve.tensor_scalar(mparts[:, 0, :], rowmax[:], -1.0, None, ALU.mult).then_inc(m_steps, 1)
                    dve.wait_ge(m_steps, steps + 1)
                    dve.scalar_tensor_tensor(out=mrest[:], in0=rowmax[:], scalar=-1.0, in1=mparts[:, 0, :],
                                             op0=ALU.mult, op1=ALU.subtract).then_inc(m_steps, 1)
                    dve.wait_ge(m_steps, steps + 2)
                    dve.tensor_copy(mparts[:, 1, :], mrest[:]).then_inc(m_steps, 1)
                    dve.wait_ge(m_steps, steps + 3)
                    dve.tensor_tensor(mparts[:, 2, :], mrest[:], mparts[:, 1, :], ALU.subtract).then_inc(m_steps, 1)

                cut_q(0)
                rest_of_k(0)
                normalise(1)

                def step(b, par, pair, project, rows, attend, finish):
                    def row_maxima(first, last):
                        if rows:
                            for i in range(first, last):
                                row_max(b, i)

                    if finish:
                        read_sums(b - 2)
                    row_maxima(0, 3)
                    if project:
                        for half in range(2):
                            dve.wait_ge(stacked[par][half], HALF * (pair + 1))
                        cut_q(b + 1)
                    row_maxima(3, 4)
                    if project:
                        rest_of_k(b + 1)
                    row_maxima(4, 10)
                    if finish:
                        normalise_sums(b - 2)
                        if first_layer:
                            add_to_x(b - 2)
                    row_maxima(10, 13)
                    if project and pair is not B // 2 - 1:
                        normalise(b + 2)
                    row_maxima(13, 14)
                    if finish and not first_layer:
                        add_to_x(b - 2)
                    row_maxima(14, 16)
                    if rows:
                        cut_max(b)

                run(step, dve)


def normalise_all(nc, sh, ctx, block_name, xnT_all, xn2, tr_ps):
    xn_made = ctx.enter_context(nc.semaphore(f"{block_name}_xn_made"))
    xn_turned = ctx.enter_context(nc.semaphore(f"{block_name}_xn_turned"))
    xnT_made = ctx.enter_context(nc.semaphore(f"{block_name}_xnT_made"))
    rstd_vector, rstd_scalar = rstd_steps(nc, sh, ctx, block_name)

    def on_vector(dve):
        rstd_vector(dve)

        def one(b, par, first):
            if not first:
                dve.wait_ge(xn_turned, b - 1)
            dve.tensor_scalar(xn2[:, par, :], sh.x[:, b, :], sh.mv[:, b, 0:1], sh.rstd[:, bass.ds(b, 1)],
                              ALU.subtract, ALU.mult).then_inc(xn_made, 1)
        for par in range(2):
            one(par, par, True)
        with dve.Fori(1, B // 2) as pair:
            for par in range(2):
                one(2 * pair + par, par, False)

    def on_tensor(pe):
        def one(b, par, first):
            pe.wait_ge(xn_made, b + 1)
            if not first:
                pe.wait_ge(xnT_made, b - 1)
            for g in range(G):
                last = pe.transpose(tr_ps[:, par, g * S:(g + 1) * S], xn2[:, par, g * 128:(g + 1) * 128],
                                    sh.ident[0:S, 0:S])
            last.then_inc(xn_turned, 1)
        for par in range(2):
            one(par, par, True)
        with pe.Fori(1, B // 2) as pair:
            for par in range(2):
                one(2 * pair + par, par, False)

    def on_scalar(act):
        rstd_scalar(act)
        with act.Fori(0, B // 2) as pair:
            for par in range(2):
                b = 2 * pair + par
                act.wait_ge(xn_turned, b + 1)
                act.activation(xnT_all[:, :, b, :], tr_ps[:, par, 0:G * S].rearrange("p (g s) -> p g s", g=G),
                               ACT.Copy).then_inc(xnT_made, 1)

    return on_vector, on_tensor, on_scalar, xnT_made


def experts_phase(nc, t, sh, w1, w2a, w1_in):
    with ExitStack() as ctx:
        def sb(name, shape, dt=F32):
            return ctx.enter_context(nc.sbuf_tensor(name, shape, dt))

        def sem(name):
            return ctx.enter_context(nc.semaphore(name))

        w2b = sb("w2b", [128, FT - W2A, E, C])
        b2 = sb("b2", [S, E, C])
        gate_w = sb("gate_w", [128, G, E])
        xnT_all = sb("xnT_all", [128, G, B, S])
        xn2 = sb("xn2", [S, 2, C])
        mean = sb("mean", [128, G, B])
        logits = sb("logits", [B, E])
        top_logit = sb("top_logit", [B, 1])
        prob = sb("prob", [B, E])
        prob_sum = sb("prob_sum", [B, 1])
        best = sb("best", [B, 8])
        best_at = sb("best_at", [B, 8], U32)
        pair_sum = sb("pair_sum", [B, 1])
        weight = sb("weight", [B, TOP])
        at_row = sb("at_row", [1, B * TOP], U32)
        weight_row = sb("weight_row", [1, B * TOP])
        weight_all = sb("weight_all", [S, B * TOP])
        xnT = sb("xnT_now", [128, G, S])
        hid = [sb(f"hid{j}", [S, F]) for j in range(TOP)]
        biased = sb("hid_biased", [128, FT, S])
        act_hid = [sb(f"act_hid{j}", [128, FT, S]) for j in range(TOP)]
        stats = sb("stats_e", [S, 6])
        mv_now = sb("mv_now_e", [S, 2])

        h_ps = ctx.enter_context(nc.psum_tensor("h_ps", [128, 2 * TOP, 512], F32))
        t_ps = ctx.enter_context(nc.psum_tensor("t_ps", [128, 2, 512], F32))
        y_ps = ctx.enter_context(nc.psum_tensor("y_ps", [128, TOP, 512], F32))

        tick = sem("tick_e")
        gate_in = sem("gate_in")
        w2b_in = sem("w2b_in")
        b2_in = sem("b2_in")
        mean_steps = sem("mean_steps")
        logits_ps = sem("logits_ps")
        route = sem("route_steps")
        prob_made = sem("prob_made")
        row_in = sem("choice_rows_in")
        at_in = sem("chosen_in")
        spread = sem("weights_spread")
        weight_ready = sem("weight_ready")
        xnT_ready = sem("xnT_now_made")
        h_made = sem("h_made")
        hid_made = sem("hid_made")
        hid_turned = sem("hid_turned")
        biased_made = sem("biased_made")
        act_made = sem("act_made")
        y_made = sem("y_made")
        y_read = sem("y_read")
        x_steps = sem("x_steps_e")
        stats_made = sem("stats_made_e")

        on_vector, on_tensor, on_scalar, xnT_made = normalise_all(nc, sh, ctx, "experts", xnT_all, xn2, t_ps)
        on_partitions = "(f p) n -> p f n"

        with nc.Block() as block:
            @block.sync
            def _(sp):
                for e in range(E):
                    sp.dma_start(w2b[:, :, e, :], t["e_w2"][e, W2A * 128:F, :].rearrange(on_partitions, p=128))\
                        .then_inc(w2b_in, 16)
                sp.wait_ge(route, 6)
                sp.dma_start(at_row[:], best_at[:, 0:TOP]).then_inc(at_in, 16)
                sp.dma_start(weight_row[:], weight[:]).then_inc(row_in, 16)

            @block.gpsimd
            def _(pool):
                pool.dma_start(gate_w[:], t["gate_w"].rearrange("(g p) e -> p g e", p=128)).then_inc(gate_in, 16)
                pool.dma_start(b2[:], t["e_b2"].partition_broadcast(S)).then_inc(b2_in, 16)
                pool.wait_ge(xnT_made, B)
                pool.tensor_copy(xnT[:], xnT_all[:, :, 0, :]).then_inc(xnT_ready, 1)
                with pool.Fori(1, B) as b:
                    pool.wait_ge(h_made, TOP * b)
                    pool.sem_inc(tick, 1)
                    pool.tensor_copy(xnT[:], xnT_all[:, :, b, :]).then_inc(xnT_ready, 1)

            @block.scalar
            def _(act):
                on_scalar(act)
                act.wait_ge(route, 2)
                act.activation(prob[:], logits[:], ACT.Exp, bias=top_logit[:]).then_inc(prob_made, 1)

                def copy_hidden(k, j):
                    act.wait_ge(h_made, k + 1)
                    act.activation(hid[j][:].rearrange("p (a n) -> p a n", a=2),
                                   h_ps[0:S, 2 * j:2 * j + 2, :], ACT.Copy).then_inc(hid_made, 1)

                def gelu(k, j):
                    act.wait_ge(biased_made, k + 1)
                    act.activation(act_hid[j][:], biased[:], ACT.Gelu).then_inc(act_made, 1)

                copy_hidden(0, 0)
                copy_hidden(1, 1)
                gelu(0, 0)
                with act.Fori(1, B) as b:
                    copy_hidden(2 * b, 0)
                    gelu(2 * b - 1, 1)
                    copy_hidden(2 * b + 1, 1)
                    gelu(2 * b, 0)
                gelu(TOP * B - 1, 1)

            @block.tensor
            def _(pe):
                on_tensor(pe)
                pe.wait_ge(mean_steps, 2)
                pe.wait_ge(gate_in, 16)
                for g in range(G):
                    last = pe.matmul(y_ps[0:B, 0, 0:E], mean[:, g, :], gate_w[:, g, :], start=(g == 0),
                                     stop=(g == G - 1))
                last.then_inc(logits_ps, 1)
                pe.wait_ge(row_in, 16)
                pe.matmul(y_ps[0:S, 1, 0:TOP * B], sh.ones[0:1, 0:S], weight_row[:], start=True, stop=True)\
                    .then_inc(spread, 1)
                pe.wait_ge(at_in, 16)
                pe.wait_ge(w1_in, 16 * B)

                def first_product(b, j, free):
                    e = pe.value_load(at_row[0:1, bass.ds(TOP * b + j, 1)], min_val=0, max_val=E - 1)
                    if j == 0:
                        pe.wait_ge(xnT_ready, b + 1)
                    if free:
                        pe.wait_ge(hid_made, TOP * b + j - 1)
                    for half in range(2):
                        for g in range(G):
                            last = pe.matmul(h_ps[0:S, 2 * j + half, :], xnT[:, g, :],
                                             w1[:, g, e, half * 512:(half + 1) * 512],
                                             start=(g == 0), stop=(g == G - 1))
                    last.then_inc(h_made, 1)

                def turn_hidden(k, j, free):
                    pe.wait_ge(hid_made, k + 1)
                    if free:
                        pe.wait_ge(biased_made, k)
                    for f in range(FT):
                        last = pe.transpose(t_ps[:, f // 4, (f % 4) * S:(f % 4 + 1) * S],
                                            hid[j][:, f * 128:(f + 1) * 128], sh.ident[0:S, 0:S])
                    last.then_inc(hid_turned, 1)

                def second_product(b, j, free):
                    e = pe.value_load(at_row[0:1, bass.ds(TOP * b + j, 1)], min_val=0, max_val=E - 1)
                    pe.wait_ge(act_made, TOP * b + j + 1)
                    if free:
                        pe.wait_ge(y_read, TOP * b + j - 1)
                    for f in range(FT):
                        w = w2a[:, f, e, :] if f < W2A else w2b[:, f - W2A, e, :]
                        last = pe.matmul(y_ps[0:S, j, 0:C], act_hid[j][:, f, :], w, start=(f == 0),
                                         stop=(f == FT - 1))
                    last.then_inc(y_made, 1)

                first_product(0, 0, False)
                first_product(0, 1, False)
                turn_hidden(0, 0, False)
                pe.wait_ge(weight_ready, 1)
                pe.wait_ge(w2b_in, 16 * E)

                def step(b, free):
                    first_product(b, 0, True)
                    turn_hidden(2 * b - 1, 1, True)
                    second_product(b - 1, 0, free)
                    first_product(b, 1, True)
                    turn_hidden(2 * b, 0, True)
                    second_product(b - 1, 1, free)

                step(1, False)
                with pe.Fori(2, B) as b:
                    step(b, True)
                turn_hidden(TOP * B - 1, 1, True)
                second_product(B - 1, 0, True)
                second_product(B - 1, 1, True)

            @block.vector
            def _(dve):
                on_vector(dve)
                dve.wait_ge(xnT_made, B)
                dve.tensor_reduce(mean[:], xnT_all[:], AX.X, ALU.add).then_inc(mean_steps, 1)
                dve.wait_ge(mean_steps, 1)
                dve.tensor_scalar(mean[:], mean[:], 1.0 / S, None, ALU.mult).then_inc(mean_steps, 1)
                dve.wait_ge(logits_ps, 1)
                dve.tensor_copy(logits[:], y_ps[0:B, 0, 0:E]).then_inc(route, 1)
                dve.wait_ge(route, 1)
                dve.tensor_reduce(top_logit[:], logits[:], AX.X, ALU.max, negate=True).then_inc(route, 1)
                dve.wait_ge(prob_made, 1)
                dve.tensor_reduce(prob_sum[:], prob[:], AX.X, ALU.add).then_inc(prob_made, 1)
                dve.wait_ge(prob_made, 2)
                dve.reciprocal(prob_sum[:], prob_sum[:]).then_inc(prob_made, 1)
                dve.wait_ge(prob_made, 3)
                dve.tensor_scalar(prob[:], prob[:], prob_sum[:], None, ALU.mult).then_inc(prob_made, 1)
                dve.wait_ge(prob_made, 4)
                dve.max(best[:], prob[:]).then_inc(route, 1)
                dve.wait_ge(route, 3)
                dve.max_index(best_at[:], best[:], prob[:]).then_inc(route, 1)
                dve.tensor_tensor(pair_sum[:], best[:, 0:1], best[:, 1:2], ALU.add).then_inc(route, 1)
                dve.wait_ge(route, 5)
                dve.reciprocal(pair_sum[:], pair_sum[:]).then_inc(prob_made, 1)
                dve.wait_ge(prob_made, 5)
                dve.tensor_scalar(weight[:], best[:, 0:TOP], pair_sum[:], sh.tg[0:B, 2:3], ALU.mult, ALU.mult)\
                    .then_inc(route, 1)
                dve.wait_ge(spread, 1)
                dve.tensor_copy(weight_all[:], y_ps[0:S, 1, 0:TOP * B]).then_inc(weight_ready, 1)
                dve.wait_ge(weight_ready, 1)
                dve.wait_ge(at_in, 16)
                dve.wait_ge(b2_in, 16)

                def add_bias(b, j, free):
                    e = dve.value_load(at_row[0:1, bass.ds(TOP * b + j, 1)], min_val=0, max_val=E - 1)
                    dve.wait_ge(hid_turned, TOP * b + j + 1)
                    if free:
                        dve.wait_ge(act_made, TOP * b + j)
                    dve.tensor_tensor(
                        biased[:].rearrange("p (a f) s -> p a f s", a=2),
                        t_ps[:, :, 0:4 * S].rearrange("p a (f s) -> p a f s", s=S),
                        sh.eb1[:, e, :].rearrange("p (a f) -> p a f", a=2).unsqueeze(3).to_broadcast([128, 2, 4, S]),
                        ALU.add).then_inc(biased_made, 1)

                def add_output(b, j):
                    e = dve.value_load(at_row[0:1, bass.ds(TOP * b + j, 1)], min_val=0, max_val=E - 1)
                    n = 7 * b + 2 * j
                    w = weight_all[:, bass.ds(TOP * b + j, 1)]
                    xb = sh.x[:, b, :]
                    dve.wait_ge(x_steps, n)
                    dve.scalar_tensor_tensor(out=xb, in0=b2[:, e, :], scalar=w, in1=xb, op0=ALU.mult, op1=ALU.add)\
                        .then_inc(x_steps, 1)
                    dve.wait_ge(y_made, TOP * b + j + 1)
                    dve.wait_ge(x_steps, n + 1)
                    dve.scalar_tensor_tensor(out=xb, in0=y_ps[0:S, j, 0:C], scalar=w, in1=xb, op0=ALU.mult,
                                             op1=ALU.add).then_inc(x_steps, 1)
                    dve.wait_ge(x_steps, n + 2)
                    dve.sem_inc(y_read, 1)
                    if j == 1:
                        dve.sem_inc(tick, 1)
                        dve.bn_stats(stats[:], xb).then_inc(x_steps, 1)
                        dve.wait_ge(x_steps, n + 3)
                        dve.sem_inc(tick, 1)
                        dve.bn_aggr(mv_now[:], stats[:]).then_inc(x_steps, 1)
                        dve.wait_ge(x_steps, n + 4)
                        dve.tensor_scalar(sh.mv[:, b, :], mv_now[:], 1.0, None, ALU.mult).then_inc(x_steps, 1)

                add_bias(0, 0, False)
                with dve.Fori(1, B) as b:
                    add_bias(b - 1, 1, True)
                    add_output(b - 1, 0)
                    add_bias(b, 0, True)
                    add_output(b - 1, 1)
                add_bias(B - 1, 1, True)
                add_output(B - 1, 0)
                add_output(B - 1, 1)


def fixed_point_phase(nc, sh, w1, w2, b2, weights_in, out_dram):
    with ExitStack() as ctx:
        def sb(name, shape, dt=F32):
            return ctx.enter_context(nc.sbuf_tensor(name, shape, dt))

        def sem(name):
            return ctx.enter_context(nc.semaphore(name))

        N = QUAD * S
        xnT_all = sb("xnT_all_f", [128, G, B, S])
        xn2 = sb("xn2_f", [S, 2, C])
        steps = [sb(f"steps{p}", [128, N]) for p in range(2)]
        n_in = [sb(f"n_in{p}", [128, N]) for p in range(2)]
        clipped = [sb(f"clipped{p}", [128, N]) for p in range(2)]
        seg = [sb(f"seg{p}", [128, N]) for p in range(2)]
        g0 = [sb(f"g0_{p}", [128, N]) for p in range(2)]
        g1 = [sb(f"g1_{p}", [128, N]) for p in range(2)]
        back = [sb(f"back{p}", [128, N]) for p in range(2)]
        over = [sb(f"over{p}", [128, N]) for p in range(2)]
        hidden = [sb(f"hidden{p}", [128, FT, N]) for p in range(2)]
        b2s = sb("b2s", [S, C])
        tgs = sb("tgs", [S, 1])
        y = [sb(f"y{p}", [S, C]) for p in range(2)]

        h_ps = ctx.enter_context(nc.psum_tensor("h_ps_f", [128, 2, 512], F32))
        y_ps = ctx.enter_context(nc.psum_tensor("y_ps_f", [128, 2, 512], F32))
        t_ps = ctx.enter_context(nc.psum_tensor("t_ps_f", [128, 2, 512], F32))

        h_made = sem("h_made_f")
        h_read = sem("h_read_f")
        rounded = sem("rounded")
        gelus = sem("gelus")
        sides = sem("sides")
        hid_steps = sem("hid_steps")
        y_made = sem("y_made_f")
        y_steps = sem("y_steps")
        consts = sem("consts_f")
        stored = sem("stored")

        on_vector, on_tensor, on_scalar, xnT_made = normalise_all(nc, sh, ctx, "fixed", xnT_all, xn2, t_ps)
        QUADS = B // QUAD

        with nc.Block() as block:
            @block.sync
            def _(sp):
                with sp.Fori(0, B) as b:
                    sp.wait_ge(y_steps, 4 * (b + 1))
                    sp.dma_start(out_dram[b, :, :], sh.x[:, b, :]).then_inc(stored, 16)
                sp.wait_ge(stored, 16 * B)

            def tiles(eng, step):
                for p in range(2):
                    step(p, p, p, 0, 0, True)
                for f in range(2, FT):
                    step(f, f, f % 2, 0, 0, False)
                with eng.Fori(1, QUADS) as q:
                    for f in range(FT):
                        step(FT * q + f, f, f % 2, q, None, False)

            @block.tensor
            def _(pe):
                on_tensor(pe)
                pe.wait_ge(weights_in, 16 * 3)
                pe.wait_ge(xnT_made, B)

                def hidden_tile(k, f, q, first):
                    if not first:
                        pe.wait_ge(h_read, k - 1)
                    for g in range(G):
                        last = pe.matmul(h_ps[:, f % 2, 0:N], w1[:, g, f * 128:(f + 1) * 128],
                                         xnT_all[:, g, bass.ds(QUAD * q, QUAD), :],
                                         start=(g == 0), stop=(g == G - 1))
                    last.then_inc(h_made, 1)

                def output_tile(b, i, p, first):
                    if not first:
                        pe.wait_ge(y_steps, 4 * (b - 1) - 3)
                    for f in range(FT):
                        last = pe.matmul(y_ps[0:S, i % 2, 0:C], hidden[p][:, f, i * S:(i + 1) * S], w2[:, f, :],
                                         start=(f == 0), stop=(f == FT - 1))
                    last.then_inc(y_made, 1)

                def quad(q, p, first, more):
                    for i in range(QUAD):
                        if more:
                            for f in (2 * i, 2 * i + 1):
                                hidden_tile(FT * (q + 1) + f, f, q + 1, False)
                        if i == 0:
                            pe.wait_ge(hid_steps, 4 * FT * (q + 1))
                        output_tile(QUAD * q + i, i, p, first and i < 2)

                for f in range(FT):
                    hidden_tile(f, f, 0, f < 2)
                for q in range(QUADS):
                    quad(q, q % 2, q == 0, q + 1 < QUADS)

            @block.scalar
            def _(act):
                on_scalar(act)

                def fill(k, f):
                    p = f % 2
                    act.wait_ge(h_made, k + 1)
                    act.activation(steps[p][:], h_ps[:, p, 0:N], ACT.Identity, bias=sh.fb1[:, f:f + 1], scale=FIX)\
                        .then_inc(h_read, 1)

                def ends(k, f):
                    p = f % 2
                    act.wait_ge(rounded, 4 * k + 3)
                    for n, g in enumerate((g0, g1)):
                        act.activation(g[p][:], seg[p][:], ACT.Gelu, bias=sh.gelu_bias[:, n:n + 1], scale=1 / FIX)\
                            .then_inc(gelus, 1)

                for q in range(QUADS):
                    for f in range(FT):
                        k = FT * q + f
                        if k >= 2:
                            act.wait_ge(rounded, 4 * (k - 2) + 1)
                            act.wait_ge(hid_steps, 4 * (k - 2) + 2)
                        fill(k, f)
                        ends(k, f)

            @block.gpsimd
            def _(pool):
                for q in range(QUADS):
                    for f in range(FT):
                        k, p = FT * q + f, f % 2
                        pool.wait_ge(rounded, 4 * k + 1)
                        if k >= 2:
                            pool.wait_ge(hid_steps, 4 * (k - 2) + 4)
                        pool.tensor_scalar(over[p][:], n_in[p][:], LIM, 0.0, ALU.subtract, ALU.max)\
                            .then_inc(sides, 1)
                        pool.wait_ge(gelus, 2 * (k + 1))
                        pool.tensor_tensor(g1[p][:], g1[p][:], g0[p][:], ALU.subtract).then_inc(sides, 1)

            @block.vector
            def _(dve):
                on_vector(dve)
                dve.wait_ge(weights_in, 16 * 3)
                dve.tensor_scalar(b2s[:], b2[:], FIX, None, ALU.mult).then_inc(consts, 1)
                dve.tensor_scalar(tgs[:], sh.tg[0:S, 3:4], 1 / FIX, None, ALU.mult).then_inc(consts, 1)
                dve.wait_ge(consts, 2)

                def place(k, f):
                    p, n = f % 2, 4 * k
                    dve.wait_ge(h_read, k + 1)
                    if k >= 2:
                        dve.wait_ge(sides, 2 * (k - 1))
                    dve.tensor_scalar(n_in[p][:], steps[p][:], ROUND, ROUND, ALU.add, ALU.subtract)\
                        .then_inc(rounded, 1)
                    dve.wait_ge(rounded, n + 1)
                    dve.tensor_scalar(clipped[p][:], n_in[p][:], LIM, -LIM, ALU.min, ALU.max).then_inc(rounded, 1)
                    dve.wait_ge(rounded, n + 2)
                    if k >= 2:
                        dve.wait_ge(gelus, 2 * (k - 1))
                    dve.tensor_scalar(seg[p][:], clipped[p][:], -(SEG - 1) / 2, ROUND * SEG, ALU.add, ALU.add)\
                        .then_inc(rounded, 1)
                    dve.wait_ge(rounded, n + 3)
                    dve.scalar_tensor_tensor(out=back[p][:], in0=seg[p][:], scalar=ROUND * SEG, in1=clipped[p][:],
                                             op0=ALU.subtract, op1=ALU.subtract).then_inc(rounded, 1)

                def interpolate(k, f, buf):
                    p, n = f % 2, 4 * k
                    dve.wait_ge(rounded, n + 4)
                    dve.wait_ge(sides, 2 * (k + 1))
                    dve.tensor_tensor(back[p][:], back[p][:], g1[p][:], ALU.mult).then_inc(hid_steps, 1)
                    dve.wait_ge(hid_steps, n + 1)
                    dve.scalar_tensor_tensor(out=back[p][:], in0=back[p][:], scalar=-1 / SEG, in1=g0[p][:],
                                             op0=ALU.mult, op1=ALU.add).then_inc(hid_steps, 1)
                    dve.wait_ge(hid_steps, n + 2)
                    dve.tensor_scalar(back[p][:], back[p][:], FIX, ROUND, ALU.mult, ALU.add).then_inc(hid_steps, 1)
                    dve.wait_ge(hid_steps, n + 3)
                    dve.scalar_tensor_tensor(out=hidden[buf][:, f, :], in0=back[p][:], scalar=ROUND, in1=over[p][:],
                                             op0=ALU.subtract, op1=ALU.add).then_inc(hid_steps, 1)

                def add_output(b, i):
                    p, n = i % 2, 4 * b
                    dve.wait_ge(y_made, b + 1)
                    dve.tensor_tensor(y[p][:], y_ps[0:S, p, 0:C], b2s[:], ALU.add).then_inc(y_steps, 1)
                    dve.wait_ge(y_steps, n + 1)
                    dve.tensor_scalar(y[p][:], y[p][:], ROUND, None, ALU.add).then_inc(y_steps, 1)
                    dve.wait_ge(y_steps, n + 2)
                    dve.tensor_scalar(y[p][:], y[p][:], ROUND, tgs[:], ALU.subtract, ALU.mult).then_inc(y_steps, 1)
                    dve.wait_ge(y_steps, n + 3)
                    dve.tensor_tensor(sh.x[:, b, :], y[p][:], sh.x[:, b, :], ALU.add).then_inc(y_steps, 1)

                for q in range(QUADS + 1):
                    for f in range(FT):
                        if q < QUADS:
                            k = FT * q + f
                            if q >= 2 and f == 0:
                                dve.wait_ge(y_made, QUAD * (q - 1))
                            place(k, f)
                            if k >= 1:
                                j = k - 1
                                interpolate(j, j % FT, (j // FT) % 2)
                        elif f == 0:
                            j = FT * QUADS - 1
                            interpolate(j, j % FT, (j // FT) % 2)
                        if q >= 1 and f % 2 == 1:
                            add_output(QUAD * (q - 1) + f // 2, f // 2)


def flamingo_kernel(nc, t, out_dram):
    with ExitStack() as ctx:
        def sb(name, shape, dt=F32, scope=ctx):
            return scope.enter_context(nc.sbuf_tensor(name, shape, dt))

        sh = Shared()
        sh.x = sb("x", [S, B, C])
        sh.mv = sb("mv", [S, B, 2])
        sh.rstd = sb("rstd", [S, B])
        sh.keep = sb("keep", [S, B])
        sh.tg = sb("tg", [128, 4])
        sh.ident = sb("ident", [128, 128])
        sh.identb = sb("identb", [128, 128], BF16)
        sh.ones = sb("ones", [1, 128])
        sh.gelu_bias = sb("gelu_bias", [128, 2])
        sh.eb1 = sb("eb1", [128, E, FT])
        sh.fb1 = sb("fb1", [128, FT])
        sh.bq1 = sb("bq1", [128, G])
        sh.bo1 = sb("bo1", [S, C])
        sh.wq0, sh.wk0, sh.wv0 = sb("wq0", [128, G, C]), sb("wk0", [128, 2, C]), sb("wv0", [128, 2, C])
        sh.wq1, sh.wk1, sh.wv1 = sb("wq1", [128, G, C]), sb("wk1", [128, 2, C]), sb("wv1", [128, 2, C])
        sh.wo1 = sb("wo1", [128, G, C])
        sh.later = ctx.enter_context(nc.semaphore("layer1_loaded"))
        w1_in = ctx.enter_context(nc.semaphore("expert_w_in"))
        ffn_in = ctx.enter_context(nc.semaphore("ffn_w_in"))

        setup_phase(nc, t, sh)
        with ExitStack() as experts:
            w1 = sb("expert_w1", [128, G, E, F], scope=experts)
            w2a = sb("expert_w2a", [128, W2A, E, C], scope=experts)

            def load_experts(sp, par, pair):
                half = W2A // 2
                sp.dma_start(w1[:, par, pair, :], t["e_w1"][pair, par * 128:(par + 1) * 128, :]).then_inc(w1_in, 16)
                sp.dma_start(w2a[:, par * half:(par + 1) * half, pair, :],
                             t["e_w2"][pair, par * half * 128:(par + 1) * half * 128, :]
                             .rearrange("(f p) n -> p f n", p=128)).then_inc(w1_in, 16)

            attention_phase(nc, sh, t["ctx"], 0, load_experts, lambda sp: None)
            experts_phase(nc, t, sh, w1, w2a, w1_in)

        f_w1 = sb("ffn_w1", [128, G, F])
        f_w2 = sb("ffn_w2", [128, FT, C])
        f_b2 = sb("ffn_b2", [S, C])

        def load_ffn(sp):
            sp.dma_start(f_w1[:], t["f_w1"].rearrange("(g p) n -> p g n", p=128)).then_inc(ffn_in, 16)
            sp.dma_start(f_w2[:], t["f_w2"].rearrange("(f p) n -> p f n", p=128)).then_inc(ffn_in, 16)
            sp.dma_start(f_b2[:], t["f_b2"].partition_broadcast(S)).then_inc(ffn_in, 16)

        attention_phase(nc, sh, t["ctx"], 1, lambda sp, par, pair: None, load_ffn)
        fixed_point_phase(nc, sh, f_w1, f_w2, f_b2, ffn_in, out_dram)


_INS = {"x": "x", "ctx_768": "ctx", "mask_BxS_bk0": "mask", "g_xattn": "g_xattn", "g_ffn": "g_ffn",
        "L0_xattn_Wq": "Wq", "L0_xattn_Wkv": "Wkv",
        "L0_ffn_gate_w": "gate_w", "L0_ffn_w1": "e_w1", "L0_ffn_b1": "e_b1", "L0_ffn_w2": "e_w2", "L0_ffn_b2": "e_b2",
        "L1_xattn_w_q": "w_q", "L1_xattn_b_q": "b_q", "L1_xattn_w_k": "w_k", "L1_xattn_b_k": "b_k",
        "L1_xattn_w_v": "w_v", "L1_xattn_b_v": "b_v", "L1_xattn_w_o": "w_o", "L1_xattn_b_o": "b_o",
        "L1_ffn_w1": "f_w1", "L1_ffn_b1": "f_b1", "L1_ffn_w2": "f_w2", "L1_ffn_b2": "f_b2"}


def kernel(**inputs):
    import numpy as _np
    import concourse.bacc as _bacc
    from concourse import mybir as _mybir
    from concourse.bass_utils import run_bass_kernel_spmd as _run

    nc = _bacc.Bacc("TRN2", target_bir_lowering=False, num_devices=1)
    arrays, tensors = {}, {}
    for name, short in _INS.items():
        a = _np.ascontiguousarray(inputs[name])
        arrays[f"in_{short}"] = a
        tensors[short] = nc.dram_tensor(f"in_{short}", a.shape, _mybir.dt.from_np(a.dtype), kind="ExternalInput").ap()
    out = nc.dram_tensor("out_x", (B, S, C), F32, kind="ExternalOutput").ap()
    flamingo_kernel(nc, tensors, out)
    r = _run(nc, [arrays], core_ids=[0])
    return r.results[0]["out_x"]
```

```python
from contextlib import ExitStack

import concourse.bass as bass
from concourse import mybir

F32 = mybir.dt.float32
BF16 = mybir.dt.bfloat16
U8 = mybir.dt.uint8
U32 = mybir.dt.uint32
ALU = mybir.AluOpType
ACT = mybir.ActivationFunctionType
AX = mybir.AxisListType

B, S, C = 16, 100, 256
SC, CC = 361, 192
NH, D = 16, 16
G = C // 128
HG = NH // G
SCALE = D ** -0.5
EPS = 1e-5
KEYS = (120, 120, 121)
KSTEP = 120
HI, LO = 128, CC - 128
Q_PART = (1, 2, 3, 1, 2, 1)
K_PART = (1, 1, 1, 2, 2, 3)
SLOTS = len(Q_PART)
SROWS = SLOTS * D
MROWS = SROWS + 3
SW = S + SC
ROW_BANKS, ST_BANKS, P_BUFS = 2, 3, 2
CHUNK = 4
CHUNKS = NH // CHUNK
VW = 32
E, F, TOP = 8, 1024, 2
FT = F // 128
W2A = 4
FIX = 256.0
ROUND = 1.5 * 2.0 ** 23
SEG = 64.0
LIM = 4.0 * FIX
QUAD = 4


class Shared:
    pass


def setup_phase(nc, t, sh):
    with ExitStack() as ctx:
        def sb(name, shape, dt=F32):
            return ctx.enter_context(nc.sbuf_tensor(name, shape, dt))

        def sem(name):
            return ctx.enter_context(nc.semaphore(name))

        wq_rows = sb("wq_rows", [128, G, C])
        wkv_rows = sb("wkv_rows", [128, 2 * G, CC])
        mask_u8 = sb("mask_u8", [B, S], U8)
        mask_f = sb("mask_f", [B, S])
        gates = sb("gates", [128, 4])
        eb1_rows = sb("eb1_rows", [E * FT, 128])
        fb1_rows = sb("fb1_rows", [FT, 128])
        stats = sb("stats0", [S, B, 6])
        ps = ctx.enter_context(nc.psum_tensor("ps_setup", [128, 4, 512], F32))

        weights_loaded = sem("weights_loaded")
        loaded = sem("small_loaded")
        x_loaded = [sem(f"x_loaded{part}") for part in range(2)]
        ident_made = sem("ident_made")
        mask_cast = sem("mask_cast")
        turned = sem("turned")
        stats_done = sem("stats_done")

        with nc.Block() as block:
            @block.sync
            def _(sp):
                sp.dma_start(wq_rows[:], t["Wq"].rearrange("(g p) c -> p g c", p=128)).then_inc(weights_loaded, 16)
                sp.dma_start(wkv_rows[:], t["Wkv"].rearrange("(g p) c -> p g c", p=128))\
                    .then_inc(weights_loaded, 16)
                sp.dma_start(mask_u8[:], t["mask"]).then_inc(loaded, 16)
                sp.dma_start(gates[:, 0:2], t["g_xattn"].partition_broadcast(128)).then_inc(loaded, 16)
                sp.dma_start(gates[:, 2:4], t["g_ffn"].partition_broadcast(128)).then_inc(loaded, 16)
                sp.dma_start(eb1_rows[:], t["e_b1"].rearrange("e (f p) -> (e f) p", p=128)).then_inc(loaded, 16)
                sp.dma_start(fb1_rows[:], t["f_b1"].rearrange("(f p) -> f p", p=128)).then_inc(loaded, 16)

            @block.gpsimd
            def _(pool):
                pool.memset(sh.ident[:], 0.0).then_inc(ident_made, 1)
                pool.memset(sh.identb[:], 0.0).then_inc(ident_made, 1)
                pool.wait_ge(ident_made, 2)
                for m in (sh.ident, sh.identb):
                    pool.affine_select(out=m[:], in_=m[:], compare_op=ALU.not_equal, fill=1.0, base=0,
                                       pattern=[[-1, 128]], channel_multiplier=1).then_inc(ident_made, 1)

            @block.scalar
            def _(act):
                for part in range(2):
                    half = slice(part * B // 2, (part + 1) * B // 2)
                    act.dma_start(sh.x[:, half, :], t["x"][half, :, :].rearrange("b s c -> s b c"))\
                        .then_inc(x_loaded[part], 16)
                act.wait_ge(loaded, 5 * 16)
                act.activation(sh.tg[:], gates[:], ACT.Tanh)
                act.wait_ge(turned, 4)
                act.activation(sh.wq0[:].rearrange("p c (o n) -> p c o n", o=G),
                               ps[:, 0, :].rearrange("p (c o n) -> p c o n", c=G, o=G), ACT.Copy)
                act.wait_ge(turned, 4 + 8)
                for n, w in ((0, sh.wk0), (1, sh.wv0)):
                    act.activation(w[0:HI, 0, :], ps[0:HI, 1, n * C:(n + 1) * C], ACT.Copy)
                    act.activation(w[0:LO, 1, :], ps[0:LO, 2, n * C:(n + 1) * C], ACT.Copy)

            @block.tensor
            def _(pe):
                pe.wait_ge(weights_loaded, 2 * 16)
                pe.wait_ge(ident_made, 4)
                for c in range(G):
                    for o in range(G):
                        pe.transpose(ps[:, 0, (c * G + o) * 128:(c * G + o + 1) * 128],
                                     wq_rows[:, o, c * 128:(c + 1) * 128], sh.ident[:]).then_inc(turned, 1)
                for n in range(2 * G):
                    pe.transpose(ps[0:HI, 1, n * 128:(n + 1) * 128], wkv_rows[:, n, 0:HI], sh.ident[:])\
                        .then_inc(turned, 1)
                    pe.transpose(ps[0:LO, 2, n * 128:(n + 1) * 128], wkv_rows[:, n, HI:CC], sh.ident[:])\
                        .then_inc(turned, 1)
                pe.wait_ge(mask_cast, 1)
                pe.transpose(ps[0:S, 3, 0:B], mask_f[:], sh.ident[0:B, 0:B]).then_inc(turned, 1)
                pe.transpose(ps[:, 3, 64:64 + E * FT], eb1_rows[:], sh.ident[0:E * FT, 0:E * FT]).then_inc(turned, 1)
                pe.transpose(ps[:, 3, 192:192 + FT], fb1_rows[:], sh.ident[0:FT, 0:FT]).then_inc(turned, 1)

            @block.vector
            def _(dve):
                dve.memset(sh.ones[:], 1.0)
                dve.memset(sh.wk0[LO:LO + 1, 1, :], 0.0)
                dve.memset(sh.wv0[LO:LO + 1, 1, :], 0.0)
                dve.memset(sh.gelu_bias[:, 0:1], -ROUND * SEG / FIX)
                dve.memset(sh.gelu_bias[:, 1:2], -ROUND * SEG / FIX + SEG / FIX)
                for b in range(B):
                    if b % (B // 2) == 0:
                        dve.wait_ge(x_loaded[b // (B // 2)], 16)
                    dve.bn_stats(stats[:, b, :], sh.x[:, b, :]).then_inc(stats_done, 1)
                dve.wait_ge(loaded, 5 * 16)
                dve.tensor_copy(mask_f[:], mask_u8[:]).then_inc(mask_cast, 1)
                for b in range(B):
                    dve.wait_ge(stats_done, b + 1)
                    dve.bn_aggr(sh.mv[:, b, :], stats[:, b, :])
                dve.wait_ge(turned, 4 + 8 + 3)
                dve.tensor_copy(sh.keep[:], ps[0:S, 3, 0:B])
                dve.tensor_copy(sh.eb1[:].rearrange("p e f -> p (e f)"), ps[:, 3, 64:64 + E * FT])
                dve.tensor_scalar(sh.fb1[:], ps[:, 3, 192:192 + FT], FIX, None, ALU.mult)


def rstd_steps(nc, sh, ctx, name):
    rstd_steps_done = ctx.enter_context(nc.semaphore(f"{name}_rstd_steps"))
    rooted = ctx.enter_context(nc.semaphore(f"{name}_rooted"))

    def on_vector(dve):
        dve.tensor_scalar(sh.rstd[:], sh.mv[:, :, 1], EPS, None, ALU.add).then_inc(rstd_steps_done, 1)
        dve.wait_ge(rooted, 1)
        dve.reciprocal(sh.rstd[:], sh.rstd[:]).then_inc(rstd_steps_done, 1)
        dve.wait_ge(rstd_steps_done, 2)

    def on_scalar(act):
        act.wait_ge(rstd_steps_done, 1)
        act.activation(sh.rstd[:], sh.rstd[:], ACT.Sqrt).then_inc(rooted, 1)

    return on_vector, on_scalar


def attention_phase(nc, sh, ctx_dram, layer, extra_loads, extra_start):
    first_layer = layer == 0
    wq, wk, wv = (sh.wq0, sh.wk0, sh.wv0) if first_layer else (sh.wq1, sh.wk1, sh.wv1)
    with ExitStack() as ctx:
        def sb(name, shape, dt=F32):
            return ctx.enter_context(nc.sbuf_tensor(f"{name}_{layer}", shape, dt))

        def psum(name, shape):
            return ctx.enter_context(nc.psum_tensor(f"{name}_{layer}", shape, F32))

        def sem(name):
            return ctx.enter_context(nc.semaphore(f"{name}_{layer}"))

        context = sb("context", [128, 2, 3, CC])
        ctxT = sb("ctxT", [128, 2, SC])
        xn = sb("xn", [S, C])
        xnT = sb("xnT", [128, G, S])
        qf = sb("qf", [128, G, S])
        qrest = sb("qrest", [128, G, S])
        krest = sb("krest", [128, G, SC])
        parts = sb("parts", [128, SLOTS, G, SW], BF16)
        stack = [sb(f"stack{p}", [MROWS, NH, SW], BF16) for p in range(2)]
        v = [sb(f"v{p}", [128, 3, NH, VW]) for p in range(2)]
        probs = [sb(f"probs{p}", [128, 3, CHUNK * S]) for p in range(P_BUFS)]
        rowmax = sb("rowmax", [S, NH])
        mrest = sb("mrest", [S, NH])
        mparts = sb("mparts", [S, 3, NH], BF16)
        mT = sb("mT", [3 * NH, S], BF16)
        oT4 = sb("oT4", [128, CHUNKS * S])
        rden = sb("rden", [S, NH])
        o = sb("o", [S, C])
        stats = sb("stats", [S, 6])
        mv_now = sb("mv_now", [S, 2])
        if not first_layer:
            oT = sb("oT", [128, G, S])
            biased = sb("biased", [S, C])
        scaled = sb("scaled", [S, B])

        rows_ps = psum("rows_ps", [128, ROW_BANKS, 512])
        a_ps = psum("a_ps", [128, 2, 512])
        st_ps = psum("st_ps", [128, ST_BANKS, 512])
        o_ps = psum("o_ps", [128, 512])

        ctx_in = [sem(f"context_loaded{p}") for p in range(2)]
        tick = sh.tick
        stack_preset = sem("stack_preset")
        presets = sem("presets")
        v_cleared = sem("v_cleared")
        scaled_ready = sem("scaled_ready")
        xn_made = sem("xn_made")
        xnT_ps = sem("xnT_ps")
        xnT_made = sem("xnT_made")
        cT_ps = sem("cT_ps")
        cT_made = sem("cT_made")
        q_ps = sem("q_ps")
        qf_made = sem("qf_made")
        q_cut = sem("q_cut")
        repeated = sem("repeated")
        k_ps = sem("k_ps")
        k1_made = sem("k1_made")
        krest_made = sem("krest_made")
        k2_made = sem("k2_made")
        k3_made = sem("k3_made")
        v_ps = sem("v_ps")
        v_made = sem("v_made")
        stacked = [[sem(f"stacked{p}_{half}") for half in range(2)] for p in range(2)]
        m_in = [sem(f"max_rows_in{p}") for p in range(2)]
        rows_made = sem("rows_made")
        rows_free = sem("rows_free")
        m_steps = sem("m_steps")
        mT_ps = sem("mT_ps")
        mT_made = sem("mT_made")
        st_made = sem("st_made")
        exp_done = sem("exp_done")
        pv_done = sem("pv_done")
        oT4_made = sem("oT4_made")
        o_turned = sem("o_turned")
        rden_made = sem("rden_made")
        o_made = sem("o_made")
        x_steps = sem("x_steps")
        if not first_layer:
            oT_ps = sem("oT_ps")
            oT_made = sem("oT_made")
            out_ps = sem("out_ps")
            out_read = sem("out_read")

        rstd_vector, rstd_scalar = rstd_steps(nc, sh, ctx, f"att{layer}")
        EXP = 3 * CHUNKS
        HALF = 16 * HG // 2

        ORDER = [g * HG + hh for hh in range(HG) for g in range(G)]

        def final(pair):
            return isinstance(pair, int) and pair == B // 2 - 1

        def run(step, eng):
            step(0, 0, 0, True, True, False, False)
            step(1, 1, 0, True, True, True, False)
            with eng.Fori(1, B // 2 - 1) as pair:
                for par in range(2):
                    step(2 * pair + par, par, pair, True, True, True, True)
            step(B - 2, 0, B // 2 - 1, True, True, True, True)
            step(B - 1, 1, B // 2 - 1, False, True, True, True)
            step(B, 0, B // 2, False, False, True, True)
            step(B + 1, 1, B // 2, False, False, False, True)

        with nc.Block() as block:
            @block.sync
            def _(sp):
                def load_context(b, par):
                    sp.dma_start(context[0:KSTEP, par, :, :],
                                 ctx_dram[b, 0:3 * KSTEP, :].rearrange("(t p) c -> p t c", p=KSTEP))\
                        .then_inc(ctx_in[par], 16)
                    sp.dma_start(context[KSTEP:KSTEP + 1, par, 2, :], ctx_dram[b, 3 * KSTEP:SC, :])\
                        .then_inc(ctx_in[par], 16)

                def fill_stack(n, par, half, scores_before):
                    sp.wait_ge(st_made, scores_before)
                    sp.sem_inc(tick, 1)
                    for hh in range(half * HG // 2, (half + 1) * HG // 2):
                        sp.dma_start(
                            stack[par][0:SROWS, hh:NH:HG, :],
                            parts[hh * D:(hh + 1) * D, :, :, :]).then_inc(stacked[par][half], 16)

                def parts_ready(n):
                    for part, times in ((q_cut, 4), (repeated, 3), (k2_made, 1), (k3_made, 1)):
                        sp.wait_ge(part, times * (n + 1))
                        sp.sem_inc(tick, 1)

                load_context(0, 0)
                load_context(1, 1)
                extra_start(sp)
                parts_ready(0)
                for half in range(2):
                    fill_stack(0, 0, half, 0)

                def step(b, par, pair, project, rows, attend, finish):
                    if project and not final(pair):
                        sp.wait_ge(cT_made, 2 * (b + 1))
                        sp.sem_inc(tick, 1)
                        load_context(b + 2, par)
                    if attend:
                        sp.wait_ge(m_in[1 - par], 16 * (pair + par))
                        sp.sem_inc(tick, 1)
                    if rows:
                        extra_loads(sp, par, pair)
                    if project:
                        parts_ready(b + 1)
                        for half in range(2):
                            before = EXP * (b - 1) + (half + 1) * EXP // 2 if attend else 0
                            fill_stack(b + 1, 1 - par, half, before)

                run(step, sp)

            @block.gpsimd
            def _(pool):
                for p in range(2):
                    pool.memset(stack[p][SROWS:MROWS, :, S:SW], 1.0).then_inc(stack_preset, 1)
                pool.wait_ge(stack_preset, 2)

                def third_k(n):
                    pool.wait_ge(k2_made, n + 1)
                    pool.sem_inc(tick, 1)
                    pool.tensor_tensor(parts[:, 5, :, S:SW], krest[:], parts[:, 3, :, S:SW], ALU.subtract)\
                        .then_inc(k3_made, 1)

                third_k(0)

                def step(b, par, pair, project, rows, attend, finish):
                    if project:
                        third_k(b + 1)
                run(step, pool)

            @block.scalar
            def _(act):
                rstd_scalar(act)

                def read_v(n, par, kt):
                    rows = KEYS[kt]
                    act.wait_ge(v_ps, 3 * n + kt + 1)
                    act.activation(v[par][0:rows, kt, :, 0:D],
                                   st_ps[0:rows, kt, 0:C].rearrange("p (h d) -> p h d", d=D), ACT.Copy)\
                        .then_inc(v_made, 1)

                def read_turned(n):
                    act.wait_ge(xnT_ps, n + 1)
                    act.activation(xnT[:].rearrange("p g s -> p (g s)"), o_ps[:, 0:G * S], ACT.Copy)\
                        .then_inc(xnT_made, 1)
                    act.wait_ge(cT_ps, 2 * n + 1)
                    act.activation(ctxT[0:LO, 1, :], a_ps[0:LO, 0, 0:SC], ACT.Copy).then_inc(cT_made, 1)
                    act.wait_ge(cT_ps, 2 * n + 2)
                    act.activation(ctxT[:, 0, :], a_ps[:, 1, 0:SC], ACT.Copy).then_inc(cT_made, 1)

                def first_k(n):
                    act.wait_ge(k_ps, 2 * (n + 1))
                    act.activation(parts[:, 0, :, S:SW], a_ps[:, :, 0:SC], ACT.Copy).then_inc(k1_made, 1)

                def second_k(n):
                    act.wait_ge(krest_made, n + 1)
                    act.activation(parts[:, 3:5, :, S:SW], krest[:].unsqueeze(1).to_broadcast([128, 2, G, SC]),
                                   ACT.Copy).then_inc(k2_made, 1)

                def read_sums(n):
                    act.wait_ge(pv_done, P_BUFS + CHUNKS * (n + 1))
                    act.wait_ge(o_turned, n + 1)
                    act.activation(oT4[:], o_ps[:, 0:CHUNKS * S], ACT.Copy).then_inc(oT4_made, 1)

                def exponentials(n, c):
                    act.wait_ge(pv_done, CHUNKS * n + c + 1)
                    for kt, rows in enumerate(KEYS):
                        act.wait_ge(st_made, EXP * n + 3 * c + kt + 1)
                        act.activation(probs[c % P_BUFS][0:rows, kt, :], st_ps[0:rows, kt, 0:CHUNK * S],
                                       ACT.Exp, scale=SCALE).then_inc(exp_done, 1)

                read_turned(0)
                first_k(0)
                second_k(0)
                act.wait_ge(presets, 3)
                act.sem_inc(exp_done, ST_BANKS)

                def step(b, par, pair, project, rows, attend, finish):
                    if finish:
                        read_sums(b - 2)
                    if rows:
                        if finish:
                            act.wait_ge(pv_done, P_BUFS + CHUNKS * (b - 1))
                        read_v(b, par, 0)
                        read_v(b, par, 1)
                    if attend:
                        act.wait_ge(mT_ps, b)
                        act.activation(mT[:], a_ps[0:3 * NH, 1, :].bitcast(BF16)[:, 0:S], ACT.Copy)\
                            .then_inc(mT_made, 1)
                        act.wait_ge(mT_made, b)
                        act.dma_start(stack[1 - par][SROWS:MROWS, :, 0:S], mT[:]).then_inc(m_in[1 - par], 16)
                    if rows:
                        read_v(b, par, 2)
                    if project:
                        read_turned(b + 1)
                    for c in range(CHUNKS):
                        if attend:
                            exponentials(b - 1, c)
                        if project and c == 0:
                            for half in range(2):
                                act.wait_ge(stacked[par][half], HALF * (pair + 1))
                            act.sem_inc(tick, 1)
                            first_k(b + 1)
                        if project and c == 1:
                            second_k(b + 1)
                    if finish and not first_layer:
                        act.wait_ge(oT_ps, b - 1)
                        act.activation(oT[:].rearrange("p g s -> p (g s)"), a_ps[:, 1, 0:G * S], ACT.Copy)\
                            .then_inc(oT_made, 1)

                run(step, act)

            @block.tensor
            def _(pe):
                def project_v(n, kt):
                    rows = KEYS[kt]
                    keys = slice(kt * KSTEP, kt * KSTEP + rows)
                    pe.matmul(st_ps[0:rows, kt, 0:C], ctxT[:, 0, keys], wv[:, 0, :], start=True, stop=False)
                    pe.matmul(st_ps[0:rows, kt, 0:C], ctxT[0:LO + 1, 1, keys], wv[0:LO + 1, 1, :],
                              start=False, stop=True).then_inc(v_ps, 1)

                def turn_max(n):
                    pe.wait_ge(m_steps, 4 * (n + 1))
                    pe.sem_inc(tick, 1)
                    pe.transpose(a_ps[0:3 * NH, 1, :].bitcast(BF16)[:, 0:S], mparts[:].rearrange("p j h -> p (j h)"),
                                 sh.identb[0:S, 0:S]).then_inc(mT_ps, 1)

                def turn_xn(n):
                    pe.wait_ge(xn_made, n + 1)
                    for g in range(G):
                        last = pe.transpose(o_ps[:, g * S:(g + 1) * S], xn[:, g * 128:(g + 1) * 128],
                                            sh.ident[0:S, 0:S])
                    last.then_inc(xnT_ps, 1)

                def turn_context_lo(n, par, pair):
                    pe.wait_ge(ctx_in[par], 32 * (pair + 1))
                    pe.sem_inc(tick, 1)
                    for kt, rows in enumerate(KEYS):
                        last = pe.transpose(a_ps[0:LO, 0, kt * KSTEP:kt * KSTEP + rows],
                                            context[0:rows, par, kt, HI:CC], sh.ident[0:rows, 0:rows])
                    last.then_inc(cT_ps, 1)

                def turn_context_hi(n, par):
                    for kt, rows in enumerate(KEYS):
                        last = pe.transpose(a_ps[:, 1, kt * KSTEP:kt * KSTEP + rows], context[0:rows, par, kt, 0:HI],
                                            sh.ident[0:rows, 0:rows])
                    last.then_inc(cT_ps, 1)

                def project_q(n):
                    pe.wait_ge(xnT_made, n + 1)
                    for g in range(G):
                        for c in range(G):
                            last = pe.matmul(o_ps[:, g * S:(g + 1) * S], wq[:, c, g * 128:(g + 1) * 128],
                                             xnT[:, c, :], start=(c == 0), stop=(c == G - 1))
                    last.then_inc(q_ps, 1)

                def project_k(n, g):
                    pe.wait_ge(cT_made, 2 * n + 2)
                    pe.matmul(a_ps[:, g, 0:SC], wk[:, 0, g * 128:(g + 1) * 128], ctxT[:, 0, :],
                              start=True, stop=False)
                    pe.matmul(a_ps[:, g, 0:SC], wk[0:LO + 1, 1, g * 128:(g + 1) * 128], ctxT[0:LO + 1, 1, :],
                              start=False, stop=True).then_inc(k_ps, 1)

                def turn_sums(n):
                    pe.wait_ge(oT4_made, n + 1)
                    for c in range(CHUNKS):
                        last = pe.transpose(a_ps[0:S, 0, c * 128:(c + 1) * 128], oT4[:, c * S:(c + 1) * S],
                                            sh.ident[:])
                    last.then_inc(o_turned, 1)

                def turn_o(n):
                    pe.wait_ge(o_made, n + 2)
                    for g in range(G):
                        last = pe.transpose(a_ps[:, 1, g * S:(g + 1) * S], o[:, g * 128:(g + 1) * 128],
                                            sh.ident[0:S, 0:S])
                    last.then_inc(oT_ps, 1)

                def project_out(n):
                    pe.wait_ge(oT_made, n + 1)
                    for c in range(G):
                        last = pe.matmul(a_ps[0:S, 1, 0:C], oT[:, c, :], sh.wo1[:, c, :],
                                         start=(c == 0), stop=(c == G - 1))
                    last.then_inc(out_ps, 1)

                def row_scores(n, par, i):
                    pe.wait_ge(rows_free, NH * n + i + 1)
                    pe.matmul(rows_ps[0:S, i % ROW_BANKS, 0:SC], stack[par][0:SROWS, ORDER[i], 0:S],
                              stack[par][0:SROWS, ORDER[i], S:SW], start=True, stop=True).then_inc(rows_made, 1)

                def scores_T(n, par, c, v_behind):
                    for kt, rows in enumerate(KEYS):
                        if c == 0 and v_behind:
                            pe.wait_ge(v_made, 3 * (n + 1) + kt + 1)
                        pe.wait_ge(exp_done, EXP * n + 3 * c + kt + 1)
                        for j in range(CHUNK):
                            h = ORDER[c * CHUNK + j]
                            last = pe.matmul(st_ps[0:rows, kt, j * S:(j + 1) * S],
                                             stack[par][:, h, S + kt * KSTEP:S + kt * KSTEP + rows],
                                             stack[par][:, h, 0:S], start=True, stop=True)
                        last.then_inc(st_made, 1)

                def weighted_sums(n, par, c, q_behind):
                    if c == 0:
                        pe.wait_ge(oT4_made, n)
                        if q_behind:
                            pe.wait_ge(qf_made, n + 3)
                        pe.wait_ge(v_made, 3 * (n + 1))
                    for kt, rows in enumerate(KEYS):
                        pe.wait_ge(exp_done, ST_BANKS + EXP * n + 3 * c + kt + 1)
                        for j in range(CHUNK):
                            last = pe.matmul(o_ps[j * VW:(j + 1) * VW, c * S:(c + 1) * S],
                                             v[par][0:rows, kt, ORDER[c * CHUNK + j], :],
                                             probs[c % P_BUFS][0:rows, kt, j * S:(j + 1) * S],
                                             start=(kt == 0), stop=(kt == 2))
                    last.then_inc(pv_done, 1)

                turn_xn(0)
                turn_context_lo(0, 0, 0)
                turn_context_hi(0, 0)
                pe.wait_ge(presets, 1)
                project_q(0)
                project_k(0, 0)
                project_k(0, 1)
                pe.sem_inc(pv_done, P_BUFS)
                pe.sem_inc(o_turned, 1)

                def step(b, par, pair, project, rows, attend, finish):
                    n, n_par, n_pair = b + 1, 1 - par, pair + par
                    m = b - 1
                    f = b - 2

                    def row_group(first, last):
                        if rows:
                            for i in range(first, last):
                                if i % (NH // 2) == 0:
                                    pe.wait_ge(stacked[par][i // (NH // 2)], HALF * (pair + 1))
                                row_scores(b, par, i)

                    if rows:
                        pe.wait_ge(v_made, 3 * b)
                        if finish:
                            pe.wait_ge(exp_done, ST_BANKS + EXP * (b - 1))
                        project_v(b, 0)
                        project_v(b, 1)
                    if attend:
                        if rows:
                            pe.wait_ge(krest_made, b + 1)
                        if finish and not first_layer:
                            pe.wait_ge(out_read, b - 1)
                        turn_max(m)
                    row_group(0, 2)
                    if rows:
                        project_v(b, 2)
                    if project:
                        pe.wait_ge(qf_made, b + 1)
                        if finish:
                            pe.wait_ge(oT4_made, b - 1)
                        turn_xn(n)
                        pe.wait_ge(krest_made, b + 1)
                        if finish:
                            pe.wait_ge(o_made, b - 1)
                        turn_context_lo(n, n_par, n_pair)
                        if attend:
                            pe.wait_ge(mT_made, b)
                            pe.sem_inc(tick, 1)
                        turn_context_hi(n, n_par)
                    row_group(2, 3)
                    if project:
                        project_q(n)
                    row_group(3, 5)
                    if project:
                        project_k(n, 0)
                    row_group(5, 6)
                    if attend:
                        if not finish:
                            pe.wait_ge(stack_preset, 2)
                            pe.wait_ge(presets, 3)
                        pe.wait_ge(m_in[1 - par], 16 * (pair + par))
                        scores_T(m, 1 - par, 0, rows)
                    if project:
                        project_k(n, 1)
                    row_group(6, 7)
                    if attend:
                        scores_T(m, 1 - par, 1, rows)
                        weighted_sums(m, 1 - par, 0, project)
                    row_group(7, 9)
                    if finish:
                        if project:
                            pe.wait_ge(krest_made, b + 2)
                        elif attend:
                            pe.wait_ge(mT_made, b)
                            pe.wait_ge(krest_made, B)
                        pe.wait_ge(o_made, b - 1)
                        turn_sums(f)
                    if attend:
                        scores_T(m, 1 - par, 2, rows)
                        weighted_sums(m, 1 - par, 1, project)
                    row_group(9, 11)
                    if attend:
                        scores_T(m, 1 - par, 3, rows)
                    if finish and not first_layer:
                        turn_o(f)
                    if attend:
                        weighted_sums(m, 1 - par, 2, project)
                    row_group(11, 13)
                    if finish and not first_layer:
                        project_out(f)
                    if attend:
                        weighted_sums(m, 1 - par, 3, project)
                    row_group(13, 16)

                run(step, pe)

            @block.vector
            def _(dve):
                rstd_vector(dve)
                if first_layer:
                    dve.tensor_tensor(scaled[:], sh.rstd[:], sh.keep[:], ALU.mult).then_inc(scaled_ready, 1)
                else:
                    dve.tensor_copy(scaled[:], sh.rstd[:]).then_inc(scaled_ready, 1)
                dve.wait_ge(scaled_ready, 1)

                def normalise(n):
                    dve.wait_ge(xnT_ps, n)
                    dve.tensor_scalar(xn[:], sh.x[:, n, :], sh.mv[:, n, 0:1], scaled[:, bass.ds(n, 1)],
                                      ALU.subtract, ALU.mult).then_inc(xn_made, 1)

                normalise(0)
                dve.memset(ctxT[LO:LO + 1, 1, :], 1.0).then_inc(presets, 1)
                for p in range(2):
                    dve.memset(v[p][:], 0.0).then_inc(v_cleared, 1)
                dve.wait_ge(v_cleared, 2)
                for p in range(2):
                    dve.memset(v[p][:, :, :, D:D + 1], 1.0).then_inc(presets, 1)
                dve.sem_inc(rows_free, ROW_BANKS)
                dve.sem_inc(o_made, 1)
                if not first_layer:
                    dve.sem_inc(out_read, 1)

                q_slot = [parts[:, slot, :, 0:S] for slot in range(SLOTS)]
                k_slot = [parts[:, slot, :, S:SW] for slot in range(SLOTS)]

                def read_q(n):
                    dve.wait_ge(q_ps, n + 1)
                    if first_layer:
                        dve.tensor_copy(qf[:].rearrange("p g s -> p (g s)"), o_ps[:, 0:G * S])\
                            .then_inc(qf_made, 1)
                    else:
                        dve.tensor_tensor(qf[:], o_ps[:, 0:G * S].rearrange("p (g s) -> p g s", g=G),
                                          sh.bq1[:].unsqueeze(2).to_broadcast([128, G, S]), ALU.add)\
                            .then_inc(qf_made, 1)

                def cut_q(n, piece):
                    if piece == 0:
                        dve.wait_ge(qf_made, n + 1)
                        dve.sem_inc(tick, 1)
                        dve.tensor_copy(q_slot[0], qf[:]).then_inc(q_cut, 1)
                        return
                    dve.wait_ge(q_cut, 4 * n + piece)
                    if piece == 1:
                        dve.tensor_tensor(qrest[:], qf[:], q_slot[0], ALU.subtract).then_inc(q_cut, 1)
                    elif piece == 2:
                        dve.sem_inc(tick, 1)
                        dve.tensor_copy(q_slot[1], qrest[:]).then_inc(q_cut, 1)
                    else:
                        dve.tensor_tensor(q_slot[2], qrest[:], q_slot[1], ALU.subtract).then_inc(q_cut, 1)

                def repeat_parts(n):
                    dve.tensor_copy(parts[:, 3:6:2, :, 0:S], q_slot[0].unsqueeze(1).to_broadcast([128, 2, G, S]))\
                        .then_inc(repeated, 1)
                    dve.tensor_copy(parts[:, 1:3, :, S:SW], k_slot[0].unsqueeze(1).to_broadcast([128, 2, G, SC]))\
                        .then_inc(repeated, 1)
                    dve.wait_ge(q_cut, 4 * n + 3)
                    dve.sem_inc(tick, 1)
                    dve.tensor_copy(q_slot[4], q_slot[1]).then_inc(repeated, 1)

                def rest_of_k(n):
                    dve.wait_ge(k1_made, n + 1)
                    dve.wait_ge(k3_made, n)
                    dve.tensor_tensor(krest[:], a_ps[:, :, 0:SC], parts[:, 0, :, S:SW], ALU.subtract)\
                        .then_inc(krest_made, 1)

                def normalise_sums(n):
                    dve.wait_ge(o_turned, n + 2)
                    per_head = a_ps[0:S, 0, :].rearrange("p (h w) -> p h w", w=VW)
                    dve.reciprocal(rden[:], per_head[:, :, D]).then_inc(rden_made, 1)
                    dve.wait_ge(rden_made, n + 1)
                    dve.tensor_tensor(o[:].rearrange("p (g hh d) -> p hh g d", g=G, d=D),
                                      per_head[:, :, 0:D].rearrange("p (hh g) d -> p hh g d", g=G),
                                      rden[:].rearrange("p (hh g) -> p hh g", g=G).unsqueeze(3)
                                      .to_broadcast([S, HG, G, D]), ALU.mult).then_inc(o_made, 1)
                    dve.wait_ge(o_made, n + 2)

                def add_to_x(n, piece):
                    steps = 3 * n
                    if piece == 0 and not first_layer:
                        dve.wait_ge(out_ps, n + 1)
                        dve.tensor_tensor(biased[:], a_ps[0:S, 1, 0:C], sh.bo1[:], ALU.add).then_inc(out_read, 1)
                    elif piece == 1:
                        source = o if first_layer else biased
                        dve.wait_ge(o_made if first_layer else out_read, n + 2)
                        dve.scalar_tensor_tensor(out=sh.x[:, n, :], in0=source[:],
                                                 scalar=sh.tg[0:S, layer:layer + 1],
                                                 in1=sh.x[:, n, :], op0=ALU.mult, op1=ALU.add).then_inc(x_steps, 1)
                    elif piece == 2:
                        dve.wait_ge(x_steps, steps + 1)
                        dve.sem_inc(tick, 1)
                        dve.bn_stats(stats[:], sh.x[:, n, :]).then_inc(x_steps, 1)
                    elif piece == 3:
                        dve.wait_ge(x_steps, steps + 2)
                        dve.sem_inc(tick, 1)
                        dve.bn_aggr(mv_now[:], stats[:]).then_inc(x_steps, 1)
                    elif piece == 4:
                        dve.wait_ge(x_steps, steps + 3)
                        dve.tensor_scalar(sh.mv[:, n, :], mv_now[:], 1.0, None, ALU.mult)

                def row_max(n, i):
                    dve.wait_ge(rows_made, NH * n + i + 1)
                    if i == 0:
                        dve.wait_ge(m_steps, 4 * n)
                    h = ORDER[i]
                    dve.tensor_reduce(rowmax[:, h:h + 1], rows_ps[0:S, i % ROW_BANKS, 0:SC], AX.X, ALU.max)\
                        .then_inc(rows_free, 1)

                def cut_max(n, piece):
                    steps = 4 * n
                    if piece == 0:
                        dve.wait_ge(rows_free, ROW_BANKS + NH * (n + 1))
                        dve.wait_ge(mT_ps, n)
                        dve.tensor_scalar(mparts[:, 0, :], rowmax[:], -1.0, None, ALU.mult).then_inc(m_steps, 1)
                        return
                    dve.wait_ge(m_steps, steps + piece)
                    if piece == 1:
                        dve.scalar_tensor_tensor(out=mrest[:], in0=rowmax[:], scalar=-1.0, in1=mparts[:, 0, :],
                                                 op0=ALU.mult, op1=ALU.subtract).then_inc(m_steps, 1)
                    elif piece == 2:
                        dve.tensor_copy(mparts[:, 1, :], mrest[:]).then_inc(m_steps, 1)
                    else:
                        dve.tensor_tensor(mparts[:, 2, :], mrest[:], mparts[:, 1, :], ALU.subtract)\
                            .then_inc(m_steps, 1)

                read_q(0)
                for piece in range(4):
                    cut_q(0, piece)
                rest_of_k(0)
                repeat_parts(0)
                normalise(1)

                def step(b, par, pair, project, rows, attend, finish):
                    n, f = b + 1, b - 2

                    def row_maxima(first, last):
                        if rows:
                            for i in range(first, last):
                                row_max(b, i)

                    row_maxima(0, 5)
                    if project:
                        read_q(n)
                        for half in range(2):
                            dve.wait_ge(stacked[par][half], HALF * (pair + 1))
                        cut_q(n, 0)
                        cut_q(n, 1)
                    if project and not final(pair):
                        normalise(b + 2)
                    row_maxima(5, 7)
                    if project:
                        cut_q(n, 2)
                        rest_of_k(n)
                        cut_q(n, 3)
                    row_maxima(7, 8)
                    if project:
                        repeat_parts(n)
                    row_maxima(8, 9)
                    if finish:
                        normalise_sums(f)
                    row_maxima(9, 11)
                    if finish and first_layer:
                        add_to_x(f, 1)
                    row_maxima(11, 13)
                    if finish and not first_layer:
                        add_to_x(f, 0)
                        add_to_x(f, 1)
                    row_maxima(13, 16)
                    for piece in range(4):
                        if rows:
                            cut_max(b, piece)
                        if finish and piece + 2 < 5:
                            add_to_x(f, piece + 2)

                run(step, dve)


def normalise_all(nc, sh, ctx, block_name, xnT_all, xn4, tr_ps, mean_to=None):
    xn_made = ctx.enter_context(nc.semaphore(f"{block_name}_xn_made"))
    xn_turned = ctx.enter_context(nc.semaphore(f"{block_name}_xn_turned"))
    xnT_made = ctx.enter_context(nc.semaphore(f"{block_name}_xnT_made"))
    mean_made = None
    if mean_to is not None:
        mean_made = ctx.enter_context(nc.semaphore(f"{block_name}_mean_made"))
        turn_ready = ctx.enter_context(nc.semaphore(f"{block_name}_turn_ready"))
        turn = ctx.enter_context(nc.sbuf_tensor(f"{block_name}_turn", [S, S + 1], F32))
    rstd_vector, rstd_scalar = rstd_steps(nc, sh, ctx, block_name)
    W = S if mean_to is None else S + 1

    def run(one, eng):
        for bank in range(2):
            one(bank, bank, True)
        with eng.Fori(1, B // 4) as quad:
            for bank in range(2):
                one(2 * quad + bank, bank, False)

    def on_vector(dve):
        if mean_to is not None:
            dve.memset(turn[:, S:S + 1], 1.0 / S).then_inc(turn_ready, 1)
            dve.tensor_copy(turn[:, 0:S], sh.ident[0:S, 0:S]).then_inc(turn_ready, 1)
        rstd_vector(dve)

        def one(pair, bank, first):
            if not first:
                dve.wait_ge(xn_turned, pair - 1)
            for j in range(2):
                b = 2 * pair + j
                dve.tensor_scalar(xn4[:, 2 * bank + j, :], sh.x[:, b, :], sh.mv[:, b, 0:1],
                                  sh.rstd[:, bass.ds(b, 1)], ALU.subtract, ALU.mult).then_inc(xn_made, 1)
        run(one, dve)

    def on_tensor(pe):
        if mean_to is not None:
            pe.wait_ge(turn_ready, 2)

        def one(pair, bank, first):
            if not first:
                pe.wait_ge(xnT_made, pair - 1)
                if mean_to is not None:
                    pe.wait_ge(mean_made, pair - 1)
            for j in range(2):
                pe.wait_ge(xn_made, 2 * pair + j + 1)
                pe.sem_inc(sh.tick, 1)
                for g in range(G):
                    rows = xn4[:, 2 * bank + j, g * 128:(g + 1) * 128]
                    at = (g * 2 + j) * W
                    if mean_to is None:
                        last = pe.transpose(tr_ps[:, bank, at:at + S], rows, sh.ident[0:S, 0:S])
                    else:
                        last = pe.matmul(tr_ps[:, bank, at:at + W], rows, turn[:], start=True, stop=True)
            last.then_inc(xn_turned, 1)
        run(one, pe)

    def on_scalar(act):
        rstd_scalar(act)

        def blocks(bank):
            return tr_ps[:, bank, 0:2 * G * W].rearrange("p (g j w) -> p g j w", g=G, j=2)

        def one(pair, bank, first):
            act.wait_ge(xn_turned, pair + 1)
            act.activation(xnT_all[:, :, bass.ds(2 * pair, 2), :],
                           blocks(bank)[:, :, :, 0:S],
                           ACT.Copy).then_inc(xnT_made, 1)
            if mean_to is not None:
                act.activation(mean_to[:, :, bass.ds(2 * pair, 2)],
                               blocks(bank)[:, :, :, S],
                               ACT.Copy).then_inc(mean_made, 1)
        run(one, act)

    return on_vector, on_tensor, on_scalar, xnT_made, mean_made


def experts_phase(nc, t, sh, w1, w2a, w1_in):
    with ExitStack() as ctx:
        def sb(name, shape, dt=F32):
            return ctx.enter_context(nc.sbuf_tensor(name, shape, dt))

        def sem(name):
            return ctx.enter_context(nc.semaphore(name))

        w2b = sb("w2b", [128, FT - W2A, E, C])
        b2 = sb("b2", [S, E, C])
        gate_w = sb("gate_w", [128, G, E])
        xnT_all = sb("xnT_all", [128, G, B, S])
        xn4 = sb("xn4", [S, 4, C])
        mean = sb("mean", [128, G, B])
        logits = sb("logits", [B, E])
        top_logit = sb("top_logit", [B, 1])
        prob = sb("prob", [B, E])
        prob_sum = sb("prob_sum", [B, 1])
        best = sb("best", [B, 8])
        best_at = sb("best_at", [B, 8], U32)
        pair_sum = sb("pair_sum", [B, 1])
        weight = sb("weight", [B, TOP])
        at_row = sb("at_row", [1, B * TOP], U32)
        weight_row = sb("weight_row", [1, B * TOP])
        weight_all = sb("weight_all", [S, B * TOP])
        xnT = sb("xnT_now", [128, G, S])
        hid = [sb(f"hid{j}", [S, F]) for j in range(TOP)]
        biased = sb("hid_biased", [128, FT, S])
        act_hid = [sb(f"act_hid{j}", [128, FT, S]) for j in range(TOP)]
        stats = sb("stats_e", [S, 6])
        mv_now = sb("mv_now_e", [S, 2])

        h_ps = ctx.enter_context(nc.psum_tensor("h_ps", [128, 2 * TOP, 512], F32))
        t_ps = ctx.enter_context(nc.psum_tensor("t_ps", [128, 2, 512], F32))
        y_ps = ctx.enter_context(nc.psum_tensor("y_ps", [128, TOP, 512], F32))

        tick = sh.tick
        gate_in = sem("gate_in")
        w2b_in = sem("w2b_in")
        b2_in = sem("b2_in")
        logits_ps = sem("logits_ps")
        route = sem("route_steps")
        prob_made = sem("prob_made")
        row_in = sem("choice_rows_in")
        at_in = sem("chosen_in")
        spread = sem("weights_spread")
        weight_ready = sem("weight_ready")
        xnT_ready = sem("xnT_now_made")
        h_made = sem("h_made")
        hid_made = sem("hid_made")
        hid_turned = sem("hid_turned")
        biased_made = sem("biased_made")
        act_made = sem("act_made")
        y_made = sem("y_made")
        y_read = sem("y_read")
        x_steps = sem("x_steps_e")

        on_vector, on_tensor, on_scalar, xnT_made, mean_made = normalise_all(nc, sh, ctx, "experts", xnT_all,
                                                                             xn4, t_ps, mean)
        on_partitions = "(f p) n -> p f n"

        with nc.Block() as block:
            @block.sync
            def _(sp):
                for e in range(E):
                    sp.dma_start(w2b[:, :, e, :], t["e_w2"][e, W2A * 128:F, :].rearrange(on_partitions, p=128))\
                        .then_inc(w2b_in, 16)
                sp.wait_ge(route, 6)
                sp.dma_start(at_row[:], best_at[:, 0:TOP]).then_inc(at_in, 16)
                sp.dma_start(weight_row[:], weight[:]).then_inc(row_in, 16)

            @block.gpsimd
            def _(pool):
                pool.dma_start(gate_w[:], t["gate_w"].rearrange("(g p) e -> p g e", p=128)).then_inc(gate_in, 16)
                pool.dma_start(b2[:], t["e_b2"].partition_broadcast(S)).then_inc(b2_in, 16)
                pool.wait_ge(xnT_made, B // 2)
                pool.tensor_copy(xnT[:], xnT_all[:, :, 0, :]).then_inc(xnT_ready, 1)
                with pool.Fori(1, B) as b:
                    pool.wait_ge(h_made, TOP * b)
                    pool.sem_inc(tick, 1)
                    pool.tensor_copy(xnT[:], xnT_all[:, :, b, :]).then_inc(xnT_ready, 1)

            @block.scalar
            def _(act):
                on_scalar(act)
                act.wait_ge(route, 2)
                act.activation(prob[:], logits[:], ACT.Exp, bias=top_logit[:]).then_inc(prob_made, 1)

                def copy_hidden(k, j):
                    act.wait_ge(h_made, k + 1)
                    act.activation(hid[j][:].rearrange("p (a n) -> p a n", a=2),
                                   h_ps[0:S, 2 * j:2 * j + 2, :], ACT.Copy).then_inc(hid_made, 1)

                def gelu(k, j):
                    act.wait_ge(biased_made, k + 1)
                    act.activation(act_hid[j][:], biased[:], ACT.Gelu).then_inc(act_made, 1)

                copy_hidden(0, 0)
                copy_hidden(1, 1)
                gelu(0, 0)
                with act.Fori(1, B) as b:
                    copy_hidden(2 * b, 0)
                    gelu(2 * b - 1, 1)
                    copy_hidden(2 * b + 1, 1)
                    gelu(2 * b, 0)
                gelu(TOP * B - 1, 1)

            @block.tensor
            def _(pe):
                on_tensor(pe)
                pe.wait_ge(mean_made, B // 2)
                pe.wait_ge(gate_in, 16)
                for g in range(G):
                    last = pe.matmul(y_ps[0:B, 0, 0:E], mean[:, g, :], gate_w[:, g, :], start=(g == 0),
                                     stop=(g == G - 1))
                last.then_inc(logits_ps, 1)
                pe.wait_ge(row_in, 16)
                pe.matmul(y_ps[0:S, 1, 0:TOP * B], sh.ones[0:1, 0:S], weight_row[:], start=True, stop=True)\
                    .then_inc(spread, 1)
                pe.wait_ge(at_in, 16)
                pe.wait_ge(w1_in, 16 * B)

                def first_product(b, j, free):
                    e = pe.value_load(at_row[0:1, bass.ds(TOP * b + j, 1)], min_val=0, max_val=E - 1)
                    if j == 0:
                        pe.wait_ge(xnT_ready, b + 1)
                    if free:
                        pe.wait_ge(hid_made, TOP * b + j - 1)
                    for half in range(2):
                        for g in range(G):
                            last = pe.matmul(h_ps[0:S, 2 * j + half, :], xnT[:, g, :],
                                             w1[:, g, e, half * 512:(half + 1) * 512],
                                             start=(g == 0), stop=(g == G - 1))
                    last.then_inc(h_made, 1)

                def turn_hidden(k, j, free):
                    pe.wait_ge(hid_made, k + 1)
                    if free:
                        pe.wait_ge(biased_made, k)
                    for f in range(FT):
                        last = pe.transpose(t_ps[:, f // 4, (f % 4) * S:(f % 4 + 1) * S],
                                            hid[j][:, f * 128:(f + 1) * 128], sh.ident[0:S, 0:S])
                    last.then_inc(hid_turned, 1)

                def second_product(b, j, free):
                    e = pe.value_load(at_row[0:1, bass.ds(TOP * b + j, 1)], min_val=0, max_val=E - 1)
                    pe.wait_ge(act_made, TOP * b + j + 1)
                    if free:
                        pe.wait_ge(y_read, TOP * b + j - 1)
                    for f in range(FT):
                        w = w2a[:, f, e, :] if f < W2A else w2b[:, f - W2A, e, :]
                        last = pe.matmul(y_ps[0:S, j, 0:C], act_hid[j][:, f, :], w, start=(f == 0),
                                         stop=(f == FT - 1))
                    last.then_inc(y_made, 1)

                first_product(0, 0, False)
                first_product(0, 1, False)
                turn_hidden(0, 0, False)
                pe.wait_ge(weight_ready, 1)
                pe.wait_ge(w2b_in, 16 * E)

                def step(b, free):
                    first_product(b, 0, True)
                    turn_hidden(2 * b - 1, 1, True)
                    second_product(b - 1, 0, free)
                    first_product(b, 1, True)
                    turn_hidden(2 * b, 0, True)
                    second_product(b - 1, 1, free)

                step(1, False)
                with pe.Fori(2, B) as b:
                    step(b, True)
                turn_hidden(TOP * B - 1, 1, True)
                second_product(B - 1, 0, True)
                second_product(B - 1, 1, True)

            @block.vector
            def _(dve):
                on_vector(dve)
                dve.wait_ge(logits_ps, 1)
                dve.tensor_copy(logits[:], y_ps[0:B, 0, 0:E]).then_inc(route, 1)
                dve.wait_ge(route, 1)
                dve.tensor_reduce(top_logit[:], logits[:], AX.X, ALU.max, negate=True).then_inc(route, 1)
                dve.wait_ge(prob_made, 1)
                dve.tensor_reduce(prob_sum[:], prob[:], AX.X, ALU.add).then_inc(prob_made, 1)
                dve.wait_ge(prob_made, 2)
                dve.reciprocal(prob_sum[:], prob_sum[:]).then_inc(prob_made, 1)
                dve.wait_ge(prob_made, 3)
                dve.tensor_scalar(prob[:], prob[:], prob_sum[:], None, ALU.mult).then_inc(prob_made, 1)
                dve.wait_ge(prob_made, 4)
                dve.max(best[:], prob[:]).then_inc(route, 1)
                dve.wait_ge(route, 3)
                dve.max_index(best_at[:], best[:], prob[:]).then_inc(route, 1)
                dve.tensor_tensor(pair_sum[:], best[:, 0:1], best[:, 1:2], ALU.add).then_inc(route, 1)
                dve.wait_ge(route, 5)
                dve.reciprocal(pair_sum[:], pair_sum[:]).then_inc(prob_made, 1)
                dve.wait_ge(prob_made, 5)
                dve.tensor_scalar(weight[:], best[:, 0:TOP], pair_sum[:], sh.tg[0:B, 2:3], ALU.mult, ALU.mult)\
                    .then_inc(route, 1)
                dve.wait_ge(spread, 1)
                dve.tensor_copy(weight_all[:], y_ps[0:S, 1, 0:TOP * B]).then_inc(weight_ready, 1)
                dve.wait_ge(weight_ready, 1)
                dve.wait_ge(at_in, 16)
                dve.wait_ge(b2_in, 16)

                def add_bias(b, j, free):
                    e = dve.value_load(at_row[0:1, bass.ds(TOP * b + j, 1)], min_val=0, max_val=E - 1)
                    dve.wait_ge(hid_turned, TOP * b + j + 1)
                    if free:
                        dve.wait_ge(act_made, TOP * b + j)
                    dve.tensor_tensor(
                        biased[:].rearrange("p (a f) s -> p a f s", a=2),
                        t_ps[:, :, 0:4 * S].rearrange("p a (f s) -> p a f s", s=S),
                        sh.eb1[:, e, :].rearrange("p (a f) -> p a f", a=2).unsqueeze(3).to_broadcast([128, 2, 4, S]),
                        ALU.add).then_inc(biased_made, 1)

                def add_output(b, j):
                    e = dve.value_load(at_row[0:1, bass.ds(TOP * b + j, 1)], min_val=0, max_val=E - 1)
                    n = 7 * b + 2 * j
                    w = weight_all[:, bass.ds(TOP * b + j, 1)]
                    xb = sh.x[:, b, :]
                    if j == 1:
                        dve.wait_ge(x_steps, n)
                    dve.scalar_tensor_tensor(out=xb, in0=b2[:, e, :], scalar=w, in1=xb, op0=ALU.mult, op1=ALU.add)\
                        .then_inc(x_steps, 1)
                    dve.wait_ge(y_made, TOP * b + j + 1)
                    dve.wait_ge(x_steps, n + 1)
                    dve.scalar_tensor_tensor(out=xb, in0=y_ps[0:S, j, 0:C], scalar=w, in1=xb, op0=ALU.mult,
                                             op1=ALU.add).then_inc(x_steps, 1)
                    dve.wait_ge(x_steps, n + 2)
                    dve.sem_inc(y_read, 1)
                    if j == 1:
                        dve.sem_inc(tick, 1)
                        dve.bn_stats(stats[:], xb).then_inc(x_steps, 1)
                        dve.wait_ge(x_steps, n + 3)
                        dve.sem_inc(tick, 1)
                        dve.bn_aggr(mv_now[:], stats[:]).then_inc(x_steps, 1)
                        dve.wait_ge(x_steps, n + 4)
                        dve.tensor_scalar(sh.mv[:, b, :], mv_now[:], 1.0, None, ALU.mult).then_inc(x_steps, 1)

                add_bias(0, 0, False)
                with dve.Fori(1, B) as b:
                    add_bias(b - 1, 1, True)
                    add_output(b - 1, 0)
                    add_bias(b, 0, True)
                    add_output(b - 1, 1)
                add_bias(B - 1, 1, True)
                add_output(B - 1, 0)
                add_output(B - 1, 1)


def fixed_point_phase(nc, sh, w1, w2, b2, weights_in, out_dram):
    with ExitStack() as ctx:
        def sb(name, shape, dt=F32):
            return ctx.enter_context(nc.sbuf_tensor(name, shape, dt))

        def sem(name):
            return ctx.enter_context(nc.semaphore(name))

        N = QUAD * S
        QUADS = B // QUAD
        H_BANKS = 2
        RING = 4
        LAG = 4
        tick = sh.tick
        xnT_all = sb("xnT_all_f", [128, G, B, S])
        xn4 = sb("xn4_f", [S, 4, C])
        steps = sb("steps", [128, N])
        shifted = [sb(f"shifted{p}", [128, N]) for p in range(2)]
        clipped = [sb(f"clipped{p}", [128, N]) for p in range(2)]
        seg = [sb(f"seg{p}", [128, N]) for p in range(2)]
        g0 = [sb(f"g0_{p}", [128, N]) for p in range(2)]
        g1 = [sb(f"g1_{p}", [128, N]) for p in range(2)]
        back = [sb(f"back{p}", [128, N]) for p in range(2)]
        lifted = [sb(f"lifted{p}", [128, N]) for p in range(2)]
        over = [sb(f"over{p}", [128, N]) for p in range(2)]
        hidden = [sb(f"hidden{r}", [128, N]) for r in range(RING)]
        b2s = sb("b2s", [S, C])
        tgs = sb("tgs", [S, 1])
        round_bias = sb("round_bias", [128, 1])
        y = [sb(f"y{i}", [S, C]) for i in range(QUAD)]

        t_ps = ctx.enter_context(nc.psum_tensor("t_ps_f", [128, 2, 512], F32))
        h_ps = ctx.enter_context(nc.psum_tensor("h_ps_f", [128, H_BANKS, 512], F32))
        y_ps = ctx.enter_context(nc.psum_tensor("y_ps_f", [128, QUAD, 512], F32))

        h_made = sem("h_made_f")
        steps_made = sem("steps_made")
        shifted_made = sem("shifted_made")
        placed = sem("placed")
        gelus = sem("gelus")
        over_made = sem("over_made")
        rise_made = sem("rise_made")
        chord = sem("chord")
        lifted_made = sem("lifted_made")
        hid_made = sem("hid_made_f")
        out_made = sem("out_made_f")
        y_read = sem("y_read_f")
        y_rounded = sem("y_rounded")
        x_final = sem("x_final")
        consts = sem("consts_f")
        stored = sem("stored")

        on_vector, on_tensor, on_scalar, xnT_made, _ = normalise_all(nc, sh, ctx, "fixed", xnT_all, xn4, t_ps)

        with nc.Block() as block:
            @block.sync
            def _(sp):
                with sp.Fori(0, B) as b:
                    sp.wait_ge(x_final, b + 1)
                    sp.dma_start(out_dram[b, :, :], sh.x[:, b, :]).then_inc(stored, 16)
                sp.wait_ge(stored, 16 * B)

            @block.tensor
            def _(pe):
                on_tensor(pe)
                pe.wait_ge(weights_in, 16 * 3)
                pe.wait_ge(xnT_made, B // 2)

                def hidden_tile(q, f, free):
                    if free:
                        pe.wait_ge(steps_made, FT * q + f - H_BANKS + 1)
                    for g in range(G):
                        last = pe.matmul(h_ps[:, f % H_BANKS, 0:N], w1[:, g, f * 128:(f + 1) * 128],
                                         xnT_all[:, g, bass.ds(QUAD * q, QUAD), :],
                                         start=(g == 0), stop=(g == G - 1))
                    last.then_inc(h_made, 1)

                def output_tiles(q, f, first=False):
                    pe.wait_ge(hid_made, FT * q + f + 1)
                    for i in range(QUAD):
                        if f == 0 and not first:
                            pe.wait_ge(y_read, QUAD * (q - 1) + i + 1)
                        last = pe.matmul(y_ps[0:S, i, 0:C], hidden[f % RING][:, i * S:(i + 1) * S], w2[:, f, :],
                                         start=(f == 0), stop=(f == FT - 1))
                    last.then_inc(out_made, 1)

                for f in range(FT):
                    hidden_tile(0, f, f >= H_BANKS)
                    if f >= LAG:
                        output_tiles(0, f - LAG, first=True)

                def step(q, before):
                    for f in range(FT):
                        hidden_tile(q, f, True)
                        output_tiles(q if f >= LAG else before, (f - LAG) % FT)

                step(1, 0)
                with pe.Fori(2, QUADS) as q:
                    step(q, q - 1)
                for f in range(FT - LAG, FT):
                    output_tiles(QUADS - 1, f)

            @block.scalar
            def _(act):
                on_scalar(act)
                act.wait_ge(consts, 3)

                def fill(q, f, free):
                    k = FT * q + f
                    if free or f >= 1:
                        act.wait_ge(shifted_made, k)
                    act.wait_ge(h_made, k + 1)
                    act.activation(steps[:], h_ps[:, f % H_BANKS, 0:N], ACT.Identity, bias=sh.fb1[:, f:f + 1],
                                   scale=FIX).then_inc(steps_made, 1)
                    act.wait_ge(steps_made, k + 1)
                    if free:
                        act.wait_ge(placed, 3 * (k - 2) + 1)
                        act.wait_ge(over_made, k - 1)
                    act.activation(shifted[f % 2][:], steps[:], ACT.Identity, bias=round_bias[:])\
                        .then_inc(shifted_made, 1)

                def ends(q, f, free):
                    k = FT * q + f
                    act.wait_ge(placed, 3 * k + 2)
                    if free:
                        act.wait_ge(chord, 2 * (k - 1))
                    for n, g in enumerate((g0, g1)):
                        act.activation(g[f % 2][:], seg[f % 2][:], ACT.Gelu, bias=sh.gelu_bias[:, n:n + 1],
                                       scale=1 / FIX).then_inc(gelus, 1)

                def lift(k, p, free):
                    act.wait_ge(chord, 2 * (k + 1))
                    if free:
                        act.wait_ge(hid_made, k - 1)
                    act.activation(lifted[p][:], back[p][:], ACT.Identity, bias=round_bias[:], scale=FIX)\
                        .then_inc(lifted_made, 1)

                def step(q, first, last):
                    for f in range(FT):
                        if f + 1 < FT:
                            fill(q, f + 1, not first or f >= 1)
                        elif not last:
                            fill(q + 1, 0, True)
                        ends(q, f, not first or f >= 2)
                        if not first or f >= 1:
                            lift(FT * q + f - 1, (f + 1) % 2, not first or f >= 3)

                fill(0, 0, False)
                step(0, True, False)
                with act.Fori(1, QUADS - 1) as q:
                    step(q, False, False)
                step(QUADS - 1, False, True)
                lift(FT * QUADS - 1, 1, True)

            @block.gpsimd
            def _(pool):
                def sides(q, f, free):
                    k, p = FT * q + f, f % 2
                    pool.wait_ge(shifted_made, k + 1)
                    if free:
                        pool.wait_ge(hid_made, k - 1)
                    pool.sem_inc(tick, 1)
                    pool.tensor_scalar(over[p][:], shifted[p][:], ROUND + LIM, 0.0, ALU.subtract, ALU.max)\
                        .then_inc(over_made, 1)
                    pool.wait_ge(gelus, 2 * (k + 1))
                    pool.sem_inc(tick, 1)
                    pool.tensor_tensor(g1[p][:], g1[p][:], g0[p][:], ALU.subtract).then_inc(rise_made, 1)

                for f in range(FT):
                    sides(0, f, f >= 2)
                with pool.Fori(1, QUADS) as q:
                    for f in range(FT):
                        sides(q, f, True)

            @block.vector
            def _(dve):
                on_vector(dve)
                dve.memset(round_bias[:], ROUND).then_inc(consts, 1)
                dve.wait_ge(weights_in, 16 * 3)
                dve.tensor_scalar(b2s[:], b2[:], FIX, None, ALU.mult).then_inc(consts, 1)
                dve.tensor_scalar(tgs[:], sh.tg[0:S, 3:4], 1 / FIX, None, ALU.mult).then_inc(consts, 1)
                dve.wait_ge(consts, 3)

                def clip(k, p):
                    dve.wait_ge(shifted_made, k + 1)
                    dve.tensor_scalar(clipped[p][:], shifted[p][:], ROUND + LIM, ROUND - LIM, ALU.min, ALU.max)\
                        .then_inc(placed, 1)

                def segment(k, p, free):
                    dve.wait_ge(placed, 3 * k + 1)
                    if free:
                        dve.wait_ge(gelus, 2 * (k - 1))
                    dve.tensor_scalar(seg[p][:], clipped[p][:], ROUND + SEG / 2, ROUND * SEG, ALU.subtract, ALU.add)\
                        .then_inc(placed, 1)

                def place(k, p):
                    dve.wait_ge(placed, 3 * k + 2)
                    dve.scalar_tensor_tensor(out=back[p][:], in0=seg[p][:], scalar=ROUND * SEG, in1=clipped[p][:],
                                             op0=ALU.subtract, op1=ALU.subtract).then_inc(placed, 1)

                def multiply(k, p):
                    dve.wait_ge(placed, 3 * k + 3)
                    dve.wait_ge(rise_made, k + 1)
                    dve.scalar_tensor_tensor(out=back[p][:], in0=back[p][:], scalar=ROUND, in1=g1[p][:],
                                             op0=ALU.add, op1=ALU.mult).then_inc(chord, 1)

                def make_chord(k, p):
                    dve.wait_ge(chord, 2 * k + 1)
                    dve.scalar_tensor_tensor(out=back[p][:], in0=back[p][:], scalar=-1 / SEG, in1=g0[p][:],
                                             op0=ALU.mult, op1=ALU.add).then_inc(chord, 1)

                def finish(k, f, free):
                    dve.wait_ge(lifted_made, k + 1)
                    dve.wait_ge(over_made, k + 1)
                    if free:
                        dve.wait_ge(out_made, k - RING + 1)
                    dve.scalar_tensor_tensor(out=hidden[f % RING][:], in0=lifted[f % 2][:], scalar=ROUND,
                                             in1=over[f % 2][:], op0=ALU.subtract, op1=ALU.add)\
                        .then_inc(hid_made, 1)

                def read_output(q, i):
                    if i == 0:
                        dve.wait_ge(out_made, FT * (q + 1))
                    dve.tensor_tensor(y[i][:], y_ps[0:S, i, 0:C], b2s[:], ALU.add).then_inc(y_read, 1)

                def round_output(q, i):
                    b = QUAD * q + i
                    dve.wait_ge(y_read, b + 1)
                    dve.tensor_scalar(y[i][:], y[i][:], ROUND, ROUND, ALU.add, ALU.subtract)\
                        .then_inc(y_rounded, 1)

                def add_output(q, i):
                    b = QUAD * q + i
                    dve.wait_ge(y_rounded, b + 1)
                    dve.scalar_tensor_tensor(out=sh.x[:, b, :], in0=y[i][:], scalar=tgs[:],
                                             in1=sh.x[:, b, :], op0=ALU.mult, op1=ALU.add).then_inc(x_final, 1)

                def slot(q, f, first, placing=True, chording=True):
                    k, p = FT * q + f, f % 2
                    outputs = placing and not first
                    reading = {2: (0, 1), 3: (2, 3)}.get(f, ()) if outputs else ()
                    adding = f - 4 if outputs and f >= 4 else None
                    if placing:
                        clip(k, p)
                    for i in reading:
                        read_output(q - 1, i)
                    if placing:
                        segment(k, p, not first or f >= 2)
                    if not first or f >= 2:
                        finish(k - 2, (f - 2) % FT, not first or f >= 2 + RING)
                    if chording and (not first or f >= 1):
                        multiply(k - 1, 1 - p)
                    if adding is not None:
                        round_output(q - 1, adding)
                    if placing:
                        place(k, p)
                    if chording and (not first or f >= 1):
                        make_chord(k - 1, 1 - p)
                    if adding is not None:
                        add_output(q - 1, adding)

                for f in range(FT):
                    slot(0, f, True)
                with dve.Fori(1, QUADS) as q:
                    for f in range(FT):
                        slot(q, f, False)
                slot(QUADS, 0, False, placing=False)
                slot(QUADS, 1, False, placing=False, chording=False)
                for i in range(QUAD):
                    read_output(QUADS - 1, i)
                for i in range(QUAD):
                    round_output(QUADS - 1, i)
                for i in range(QUAD):
                    add_output(QUADS - 1, i)


def flamingo_kernel(nc, t, out_dram):
    with ExitStack() as ctx:
        def sb(name, shape, dt=F32, scope=ctx):
            return scope.enter_context(nc.sbuf_tensor(name, shape, dt))

        sh = Shared()
        sh.x = sb("x", [S, B, C])
        sh.mv = sb("mv", [S, B, 2])
        sh.rstd = sb("rstd", [S, B])
        sh.keep = sb("keep", [S, B])
        sh.tg = sb("tg", [128, 4])
        sh.ident = sb("ident", [128, 128])
        sh.identb = sb("identb", [128, 128], BF16)
        sh.ones = sb("ones", [1, 128])
        sh.gelu_bias = sb("gelu_bias", [128, 2])
        sh.eb1 = sb("eb1", [128, E, FT])
        sh.fb1 = sb("fb1", [128, FT])
        sh.bq1 = sb("bq1", [128, G])
        sh.bo1 = sb("bo1", [S, C])
        sh.wq0, sh.wk0, sh.wv0 = sb("wq0", [128, G, C]), sb("wk0", [128, 2, C]), sb("wv0", [128, 2, C])
        sh.wq1, sh.wk1, sh.wv1 = sb("wq1", [128, G, C]), sb("wk1", [128, 2, C]), sb("wv1", [128, 2, C])
        sh.wo1 = sb("wo1", [128, G, C])
        sh.tick = ctx.enter_context(nc.semaphore("tick"))
        sh.later = ctx.enter_context(nc.semaphore("layer1_loaded"))
        w1_in = ctx.enter_context(nc.semaphore("expert_w_in"))
        ffn_in = ctx.enter_context(nc.semaphore("ffn_w_in"))

        setup_phase(nc, t, sh)
        with ExitStack() as experts:
            w1 = sb("expert_w1", [128, G, E, F], scope=experts)
            w2a = sb("expert_w2a", [128, W2A, E, C], scope=experts)

            def load_experts(sp, par, pair):
                half = W2A // 2
                sp.dma_start(w1[:, par, pair, :], t["e_w1"][pair, par * 128:(par + 1) * 128, :]).then_inc(w1_in, 16)
                sp.dma_start(w2a[:, par * half:(par + 1) * half, pair, :],
                             t["e_w2"][pair, par * half * 128:(par + 1) * half * 128, :]
                             .rearrange("(f p) n -> p f n", p=128)).then_inc(w1_in, 16)

            def load_later(sp):
                for tile, w in ((sh.wk1, t["w_k"]), (sh.wv1, t["w_v"])):
                    sp.dma_start(tile[0:HI, 0, :], w[0:HI, :]).then_inc(sh.later, 16)
                    sp.dma_start(tile[0:LO, 1, :], w[HI:CC, :]).then_inc(sh.later, 16)
                sp.dma_start(sh.wk1[LO:LO + 1, 1, :], t["b_k"].unsqueeze(0)).then_inc(sh.later, 16)
                sp.dma_start(sh.wv1[LO:LO + 1, 1, :], t["b_v"].unsqueeze(0)).then_inc(sh.later, 16)
                sp.dma_start(sh.wq1[:], t["w_q"].rearrange("(g p) c -> p g c", p=128)).then_inc(sh.later, 16)
                sp.dma_start(sh.wo1[:], t["w_o"].rearrange("(g p) c -> p g c", p=128)).then_inc(sh.later, 16)
                sp.dma_start(sh.bq1[:], t["b_q"].rearrange("(g p) -> p g", p=128),
                             allow_slow_non_contiguous=True).then_inc(sh.later, 16)
                sp.dma_start(sh.bo1[:], t["b_o"].partition_broadcast(S)).then_inc(sh.later, 16)
                sp.wait_ge(sh.later, 10 * 16)

            attention_phase(nc, sh, t["ctx"], 0, load_experts, load_later)
            experts_phase(nc, t, sh, w1, w2a, w1_in)

        f_w1 = sb("ffn_w1", [128, G, F])
        f_w2 = sb("ffn_w2", [128, FT, C])
        f_b2 = sb("ffn_b2", [S, C])

        def load_ffn(sp):
            sp.dma_start(f_w1[:], t["f_w1"].rearrange("(g p) n -> p g n", p=128)).then_inc(ffn_in, 16)
            sp.dma_start(f_w2[:], t["f_w2"].rearrange("(f p) n -> p f n", p=128)).then_inc(ffn_in, 16)
            sp.dma_start(f_b2[:], t["f_b2"].partition_broadcast(S)).then_inc(ffn_in, 16)

        attention_phase(nc, sh, t["ctx"], 1, lambda sp, par, pair: None, load_ffn)
        fixed_point_phase(nc, sh, f_w1, f_w2, f_b2, ffn_in, out_dram)


_INS = {"x": "x", "ctx_768": "ctx", "mask_BxS_bk0": "mask", "g_xattn": "g_xattn", "g_ffn": "g_ffn",
        "L0_xattn_Wq": "Wq", "L0_xattn_Wkv": "Wkv",
        "L0_ffn_gate_w": "gate_w", "L0_ffn_w1": "e_w1", "L0_ffn_b1": "e_b1", "L0_ffn_w2": "e_w2", "L0_ffn_b2": "e_b2",
        "L1_xattn_w_q": "w_q", "L1_xattn_b_q": "b_q", "L1_xattn_w_k": "w_k", "L1_xattn_b_k": "b_k",
        "L1_xattn_w_v": "w_v", "L1_xattn_b_v": "b_v", "L1_xattn_w_o": "w_o", "L1_xattn_b_o": "b_o",
        "L1_ffn_w1": "f_w1", "L1_ffn_b1": "f_b1", "L1_ffn_w2": "f_w2", "L1_ffn_b2": "f_b2"}


def kernel(**inputs):
    import numpy as _np
    import concourse.bacc as _bacc
    from concourse import mybir as _mybir
    from concourse.bass_utils import run_bass_kernel_spmd as _run

    nc = _bacc.Bacc("TRN2", target_bir_lowering=False, num_devices=1)
    arrays, tensors = {}, {}
    for name, short in _INS.items():
        a = _np.ascontiguousarray(inputs[name])
        arrays[f"in_{short}"] = a
        tensors[short] = nc.dram_tensor(f"in_{short}", a.shape, _mybir.dt.from_np(a.dtype), kind="ExternalInput").ap()
    out = nc.dram_tensor("out_x", (B, S, C), F32, kind="ExternalOutput").ap()
    flamingo_kernel(nc, tensors, out)
    r = _run(nc, [arrays], core_ids=[0])
    return r.results[0]["out_x"]
```
